# Optimizing a Trainium2 kernel written in Bass

```python
import numpy as np
import jax
import jax.numpy as jnp

def _softmax(x, axis=-1):
    return jax.nn.softmax(x, axis=axis)

def _gelu(x):
    return jax.nn.gelu(x, approximate=True)

def _silu(x):
    return jax.nn.silu(x)

def _sigmoid(x):
    return jax.nn.sigmoid(x)

def _layernorm(x, axis=-1, eps=1e-05):
    m = jnp.mean(x, axis=axis, keepdims=True)
    v = jnp.var(x, axis=axis, keepdims=True)
    return (x - m) / jnp.sqrt(v + eps)

def _scatter_add(tgt, idx, src, axis=0):
    return tgt.at[idx].add(src)

def _segment_sum(src, seg, n):
    return jax.ops.segment_sum(src, seg, n)
kernel_name = 'mk_decoder_postln_d1_seqx_r4_730def'

def setup_inputs(seed: int=0):
    np.random.seed(seed)
    _w = jnp.asarray

    def _rec_inputs():
        import jax
        import jax.numpy as jnp
        _rk = jax.random.key(seed)
        x = -0.000125 + 0.9999 * jax.random.normal(jax.random.fold_in(_rk, 1), (4, 512, 256), jnp.float32)
        _lenS = 512 - jax.random.randint(jax.random.fold_in(_rk, 7), (4,), 0, max(1, 512 // 4) + 1, jnp.int32)
        _lenS2 = 1601 - jax.random.randint(jax.random.fold_in(_rk, 8), (4,), 0, max(1, 1601 // 4) + 1, jnp.int32)
        _ctx_768P = jax.random.normal(jax.random.fold_in(_rk, 11), (4, 16, 192), jnp.float32)
        _ctx_768c = jax.random.dirichlet(jax.random.fold_in(_rk, 511), 0.3 * jnp.ones((16,), jnp.float32), (4, 1601))
        _ctx_768t = jnp.einsum('bsk,bkd->bsd', _ctx_768c, _ctx_768P)
        _ctx_768t = _ctx_768t * jax.lax.rsqrt(jnp.mean(jnp.square(_ctx_768t)) + 1e-12) * 0.953939
        ctx_768 = 0.00272024 + 0.999456 * (_ctx_768t + 0.3 * jax.random.normal(jax.random.fold_in(_rk, 611), (4, 1601, 192), jnp.float32))
        return (x, ctx_768)
    x, ctx_768 = _rec_inputs()

    def _L0_attn_setup():
        import jax, jax.numpy as jnp
        import numpy as np
        HID = 256
        HEADS = 16
        FEAT = 16
        HD = HID // HEADS
        EPS = 1e-05
        LN_EPS = 1e-05
        B, T = (1, 256)
        IU, JU = np.triu_indices(FEAT, 1)

        def _feature_map(x, gamma, beta):
            mu = x.mean(axis=-1, keepdims=True)
            var = ((x - mu) ** 2).mean(axis=-1, keepdims=True)
            xn = (x - mu) / jnp.sqrt(var + LN_EPS) * gamma + beta
            diag = xn * xn
            off = xn[..., IU] * xn[..., JU]
            return jnp.concatenate([diag * FEAT ** (-0.5), off * (2.0 / FEAT) ** 0.5], axis=-1)
        key = jax.random.key(seed)
        ks = jax.random.split(key, 5)
        s = 0.02
        return {'hidden_states': jax.random.normal(ks[0], (B, T, HID), dtype=jnp.float32), 'Wq': jax.random.normal(ks[1], (FEAT * HEADS, HID), dtype=jnp.float32) * s, 'Wk': jax.random.normal(ks[2], (FEAT * HEADS, HID), dtype=jnp.float32) * s, 'Wv': jax.random.normal(ks[3], (HEADS * HD, HID), dtype=jnp.float32) * s, 'Wo': jax.random.normal(ks[4], (HID, HEADS * HD), dtype=jnp.float32) * s, 'gamma': jnp.ones((FEAT,), dtype=jnp.float32), 'beta': jnp.zeros((FEAT,), dtype=jnp.float32)}
    _L0_attn_all = _L0_attn_setup()
    _L0_attn_in = {k: v for k, v in _L0_attn_all.items() if k in ('Wq', 'Wk', 'Wv', 'Wo', 'gamma', 'beta')}
    del _L0_attn_all

    def _L0_xattn_setup():
        import jax, jax.numpy as jnp
        import numpy as np
        QUERY_DIM = 256
        CONTEXT_DIM = 192
        HEADS = 8
        DIM_HEAD = 64
        INNER = HEADS * DIM_HEAD
        key = jax.random.key(seed)
        ks = jax.random.split(key, 7)
        B, S, L = (8, 1024, 77)
        x = jax.random.normal(ks[0], (B, S, QUERY_DIM), dtype=jnp.float32)
        context = jax.random.normal(ks[1], (B, L, CONTEXT_DIM), dtype=jnp.float32)
        Wq = jax.random.normal(ks[2], (QUERY_DIM, INNER), dtype=jnp.float32) * QUERY_DIM ** (-0.5)
        Wk = jax.random.normal(ks[3], (CONTEXT_DIM, INNER), dtype=jnp.float32) * CONTEXT_DIM ** (-0.5)
        Wv = jax.random.normal(ks[4], (CONTEXT_DIM, INNER), dtype=jnp.float32) * CONTEXT_DIM ** (-0.5)
        Wo = jax.random.normal(ks[5], (INNER, QUERY_DIM), dtype=jnp.float32) * INNER ** (-0.5)
        bo = jax.random.normal(ks[6], (QUERY_DIM,), dtype=jnp.float32) * 0.01
        return {'x': x, 'context': context, 'Wq': Wq, 'Wk': Wk, 'Wv': Wv, 'Wo': Wo, 'bo': bo}
    _L0_xattn_all = _L0_xattn_setup()
    _L0_xattn_in = {k: v for k, v in _L0_xattn_all.items() if k in ('Wq', 'Wk', 'Wv', 'Wo', 'bo')}
    del _L0_xattn_all

    def _L0_ffn_setup():
        import jax, jax.numpy as jnp
        import numpy as np
        DIM = 256
        N_EXPERTS = 8
        D_FF = 512
        TOP_K = 2
        key = jax.random.key(seed)
        ks = jax.random.split(key, 5)
        s = 0.02
        return {'x': jax.random.normal(ks[0], (2, 512, DIM), dtype=jnp.float32), 'gate_w': jax.random.normal(ks[1], (N_EXPERTS, DIM), dtype=jnp.float32) * s, 'w1': jax.random.normal(ks[2], (N_EXPERTS, D_FF, DIM), dtype=jnp.float32) * s, 'w2': jax.random.normal(ks[3], (N_EXPERTS, DIM, D_FF), dtype=jnp.float32) * s, 'w3': jax.random.normal(ks[4], (N_EXPERTS, D_FF, DIM), dtype=jnp.float32) * s}
    _L0_ffn_all = _L0_ffn_setup()
    _L0_ffn_in = {k: v for k, v in _L0_ffn_all.items() if k in ('gate_w', 'w1', 'w2', 'w3')}
    del _L0_ffn_all
    return {'x': x, 'ctx_768': ctx_768, 'L0_attn_Wq': _L0_attn_in['Wq'], 'L0_attn_Wk': _L0_attn_in['Wk'], 'L0_attn_Wv': _L0_attn_in['Wv'], 'L0_attn_Wo': _L0_attn_in['Wo'], 'L0_attn_gamma': _L0_attn_in['gamma'], 'L0_attn_beta': _L0_attn_in['beta'], 'L0_xattn_Wq': _L0_xattn_in['Wq'], 'L0_xattn_Wk': _L0_xattn_in['Wk'], 'L0_xattn_Wv': _L0_xattn_in['Wv'], 'L0_xattn_Wo': _L0_xattn_in['Wo'], 'L0_xattn_bo': _L0_xattn_in['bo'], 'L0_ffn_gate_w': _L0_ffn_in['gate_w'], 'L0_ffn_w1': _L0_ffn_in['w1'], 'L0_ffn_w2': _L0_ffn_in['w2'], 'L0_ffn_w3': _L0_ffn_in['w3']}

def reference(x, ctx_768, L0_attn_Wq, L0_attn_Wk, L0_attn_Wv, L0_attn_Wo, L0_attn_gamma, L0_attn_beta, L0_xattn_Wq, L0_xattn_Wk, L0_xattn_Wv, L0_xattn_Wo, L0_xattn_bo, L0_ffn_gate_w, L0_ffn_w1, L0_ffn_w2, L0_ffn_w3):
    import jax
    import jax.numpy as jnp

    def _L0_attn_ref(hidden_states, Wq, Wk, Wv, Wo, gamma, beta):
        import jax, jax.numpy as jnp
        import numpy as np
        HID = 256
        HEADS = 16
        FEAT = 16
        HD = HID // HEADS
        EPS = 1e-05
        LN_EPS = 1e-05
        B, T = (1, 256)
        IU, JU = np.triu_indices(FEAT, 1)

        def _feature_map(x, gamma, beta):
            mu = x.mean(axis=-1, keepdims=True)
            var = ((x - mu) ** 2).mean(axis=-1, keepdims=True)
            xn = (x - mu) / jnp.sqrt(var + LN_EPS) * gamma + beta
            diag = xn * xn
            off = xn[..., IU] * xn[..., JU]
            return jnp.concatenate([diag * FEAT ** (-0.5), off * (2.0 / FEAT) ** 0.5], axis=-1)
        b, t, _ = hidden_states.shape
        q = (hidden_states @ Wq.T).reshape(b, t, HEADS, FEAT).transpose(0, 2, 1, 3)
        k = (hidden_states @ Wk.T).reshape(b, t, HEADS, FEAT).transpose(0, 2, 1, 3)
        v = (hidden_states @ Wv.T).reshape(b, t, HEADS, HD).transpose(0, 2, 1, 3)
        phi_q = _feature_map(q, gamma, beta)
        phi_k = _feature_map(k, gamma, beta)
        kv_cum = jnp.cumsum(phi_k[..., :, None] * v[..., None, :], axis=2)
        num = jnp.einsum('bhtf,bhtfd->bhtd', phi_q, kv_cum)
        den = jnp.einsum('bhtf,bhtf->bht', phi_q, jnp.cumsum(phi_k, axis=2))[..., None] + EPS
        y = (num / den).transpose(0, 2, 1, 3).reshape(b, t, HEADS * HD)
        return y @ Wo.T

    def _L0_xattn_ref(x, context, Wq, Wk, Wv, Wo, bo):
        import jax, jax.numpy as jnp
        import numpy as np
        QUERY_DIM = 256
        CONTEXT_DIM = 192
        HEADS = 8
        DIM_HEAD = 64
        INNER = HEADS * DIM_HEAD
        B, S, _ = x.shape
        L = context.shape[1]
        scale = DIM_HEAD ** (-0.5)
        q = (x @ Wq).reshape(B, S, HEADS, DIM_HEAD).transpose(0, 2, 1, 3)
        k = (context @ Wk).reshape(B, L, HEADS, DIM_HEAD).transpose(0, 2, 1, 3)
        v = (context @ Wv).reshape(B, L, HEADS, DIM_HEAD).transpose(0, 2, 1, 3)
        attn = jnp.einsum('bhsd,bhld->bhsl', q, k) * scale
        attn = jax.nn.softmax(attn, axis=-1)
        out = jnp.einsum('bhsl,bhld->bhsd', attn, v)
        out = out.transpose(0, 2, 1, 3).reshape(B, S, INNER)
        return out @ Wo + bo

    def _L0_ffn_ref(x, gate_w, w1, w2, w3):
        import jax, jax.numpy as jnp
        import numpy as np
        DIM = 256
        N_EXPERTS = 8
        D_FF = 512
        TOP_K = 2
        orig_shape = x.shape
        xf = x.reshape(-1, orig_shape[-1])
        scores = jnp.einsum('td,ed->te', xf, gate_w)
        probs = jax.nn.softmax(scores.astype(jnp.float32), axis=-1)
        weights, idx = jax.lax.top_k(probs, TOP_K)
        weights = weights / jnp.sum(weights, axis=-1, keepdims=True)
        weights = weights.astype(x.dtype)
        x1 = jax.nn.silu(jnp.einsum('td,efd->tef', xf, w1))
        x3 = jnp.einsum('td,efd->tef', xf, w3)
        out_all = jnp.einsum('tef,edf->ted', x1 * x3, w2)
        expert_outs = jnp.take_along_axis(out_all, idx[:, :, None], axis=1)
        result = jnp.einsum('tkd,tk->td', expert_outs, weights)
        return result.reshape(orig_shape)
    x = _layernorm(x + _L0_attn_ref(x, L0_attn_Wq, L0_attn_Wk, L0_attn_Wv, L0_attn_Wo, L0_attn_gamma, L0_attn_beta), axis=-1)
    x = _layernorm(x + _L0_xattn_ref(x, ctx_768, L0_xattn_Wq, L0_xattn_Wk, L0_xattn_Wv, L0_xattn_Wo, L0_xattn_bo), axis=-1)
    x = _layernorm(x + _L0_ffn_ref(x, L0_ffn_gate_w, L0_ffn_w1, L0_ffn_w2, L0_ffn_w3), axis=-1)
    return x

_drawn_inputs = setup_inputs


def setup_inputs(seed=0):
    import zlib

    import numpy as np

    out = dict(_drawn_inputs(seed))
    spreads = {'L0_attn_gamma': (1.0, 0.6), 'L0_attn_beta': (0.0, 0.8)}
    factors = {'L0_attn_Wq': 4.825,
     'L0_attn_Wk': 4.757,
     'L0_attn_Wv': 3.512,
     'L0_attn_Wo': 3.547,
     'L0_xattn_bo': 6.018,
     'L0_ffn_gate_w': 3.831,
     'L0_ffn_w1': 3.364,
     'L0_ffn_w2': 3.326,
     'L0_ffn_w3': 3.325}
    for name, (base, spread) in spreads.items():
        noise = np.random.default_rng([zlib.crc32(name.encode()), seed]).standard_normal(out[name].shape)
        drawn = base * np.exp(spread * noise) if base else spread * noise
        out[name] = jnp.asarray(drawn.astype(out[name].dtype))
    for name, factor in factors.items():
        out[name] = (out[name] * factor).astype(out[name].dtype)
    return out
```

```python
import concourse.bass as bass
from concourse import mybir
from contextlib import ExitStack

B, T, D = 4, 512, 256
P = 128
NT = T // P
KC = D // P
SH, SF = 16, 16
L, C = 1601, 192
XH, XD = 8, 64
INNER = XH * XD
E, FF = 8, 512
FC = FF // P
LN_EPS = 1e-5
DEN_EPS = 1e-5
QUADS = SH // 4
PAIRS = XH // 2
NL = (L + P - 1) // P
LROWS = [min(P, L - P * j) for j in range(NL)]
BW = 402
BSTART = [0, 400, 800, L - BW]
BEDGE = [0, 402, 802, 1202, L]
NB = len(BSTART)


def decoder_layer(nc, x, xt, ctxt, wqkv, wo_s, gamma, beta, wq, wk, wv, wo_x, bo, gate, w1, w3, w2, out):
    f32 = mybir.dt.float32
    f32r = mybir.dt.float32r
    ALU = mybir.AluOpType
    ACT = mybir.ActivationFunctionType
    AX = mybir.AxisListType.X

    ctx = ExitStack()
    with ctx:
        def sem(name):
            return ctx.enter_context(nc.semaphore(name))

        def keep(name, shape, dt=f32):
            return ctx.enter_context(nc.sbuf_tensor(name, shape, dt))

        def stage_buffers(stack):
            return lambda name, shape, dt=f32: stack.enter_context(nc.sbuf_tensor(name, shape, dt))

        X = keep("X", [P, B * NT, D])
        ident = keep("ident", [P, P])
        gam = keep("gam", [P, SF])
        bet = keep("bet", [P, SF])
        neg_half = keep("neg_half", [P, 128])
        ln_st = keep("ln_st", [P, NT, 6])
        ln_mv = keep("ln_mv", [P, NT, 2])
        ln_ve = keep("ln_ve", [P, NT])
        ln_rs = keep("ln_rs", [P, NT])

        PS = ctx.enter_context(nc.psum_tensor("PS", [P, 8, 512], f32))

        both = ExitStack()
        sx = stage_buffers(both)
        WQh, WQl = sx("WQh", [P, KC, INNER], f32r), sx("WQl", [P, KC, INNER], f32r)
        WKh, WKl = sx("WKh", [P, 2, INNER], f32r), sx("WKl", [P, 2, INNER], f32r)
        WVh, WVl = sx("WVh", [P, 2, INNER], f32r), sx("WVl", [P, 2, INNER], f32r)
        WOh, WOl = sx("WOh", [P, PAIRS, D], f32r), sx("WOl", [P, PAIRS, D], f32r)

        st = ExitStack()
        ss = stage_buffers(st)
        raw = ss("raw", [P, 4, 1024])
        WSh, WSl = ss("WSh", [P, KC, 4 * D], f32r), ss("WSl", [P, KC, 4 * D], f32r)
        xt_raw = ss("xt_raw", [P, KC, T])
        xt_h, xt_l = ss("xt_h", [P, KC, T], f32r), ss("xt_l", [P, KC, T], f32r)
        cen = ss("cen", [P, NT, 2 * D])
        sq = ss("sq", [P, NT, 2 * D])
        g_sum = ss("g_sum", [P, NT * 32])
        g_var = ss("g_var", [P, NT * 32])
        g_rs = ss("g_rs", [P, NT * 32])
        QX = ss("QX", [P, NT, SH, 4, SF], f32r)
        KX = ss("KX", [P, NT, SH, 4, SF], f32r)
        qT = ss("qT", [P, 2, 2, T], f32r)
        kT = ss("kT", [P, 2, 4, T], f32r)
        A = ss("A", [P, 8, T])
        VS = ss("VS", [P, NT, SH, 2 * SF])
        osb = ss("osb", [P, 2, T])
        den = ss("den", [P, NT * 4])
        rden = ss("rden", [P, NT * 4])
        y = ss("y", [P, NT, D])
        y_h, y_l = ss("y_h", [P, KC, T], f32r), ss("y_l", [P, KC, T], f32r)
        st.close()

        xs_ = ExitStack()
        sxx = stage_buffers(xs_)
        work = sxx("work", [P, 6 * T])
        c_raw = work[:, 0:4 * BW].rearrange("p (k r n) -> p k r n", k=2, r=2)
        xs = work[:, 4 * BW:4 * BW + NT * D].rearrange("p (i d) -> p i d", i=NT)
        NP = 4
        PX = work[:, 0:NP * T].rearrange("p (k t) -> p k t", k=NP)
        R = work[:, NP * T:(NP + 1) * T]
        O = work[:, (NP + 1) * T:]
        c_tmp = sxx("c_tmp", [P, BW], f32r)
        Ch = sxx("Ch", [P, L], f32r)
        Cl = sxx("Cl", [P, L], f32r)
        Cc = sxx("Cc", [P, L], f32r)
        VX = sxx("VX", [P, NL, PAIRS, 3 * XD])
        Kh, Kl = sxx("Kh", [P, L], f32r), sxx("Kl", [P, L], f32r)
        KA = sxx("KA", [P, 3, L], f32r)
        KB = sxx("KB", [P, 3, L], f32r)
        Qh, Ql = sxx("Qh", [P, T], f32r), sxx("Ql", [P, T], f32r)
        QA = sxx("QA", [P, 3, T], f32r)
        QB = sxx("QB", [P, 3, T], f32r)
        bo_t = sxx("bo_t", [P, D])
        x1_h, x1_l = sxx("x1_h", [P, KC, T], f32r), sxx("x1_l", [P, KC, T], f32r)
        mxp = sxx("mxp", [P, 2, NT, NB])
        mx = sxx("mx", [P, 2, NT])
        mrow = sxx("mrow", [NT, 2, P], f32r)
        O_h, O_l = sxx("O_h", [P, T], f32r), sxx("O_l", [P, T], f32r)
        xs_.close()
        both.close()

        fs = ExitStack()
        sf = stage_buffers(fs)
        x2_h, x2_l = sf("x2_h", [P, KC, B * T], f32r), sf("x2_l", [P, KC, B * T], f32r)
        G_raw = sf("G_raw", [P, KC, P])
        G_h, G_l = sf("G_h", [P, KC, P], f32r), sf("G_l", [P, KC, P], f32r)
        sT = sf("sT", [E, B * T])
        S8 = sf("S8", [P, B * NT, E])
        cmp = sf("cmp", [P, B * NT, E, E])
        cmp2 = sf("cmp2", [P, B * NT, E, E])
        lower = sf("lower", [P, E, E])
        rank = sf("rank", [P, B * NT, E])
        chosen = sf("chosen", [P, B * NT, E])
        smax = sf("smax", [P, B * NT])
        sh = sf("sh", [P, B * NT, E])
        ex = sf("ex", [P, B * NT, E])
        exs = sf("exs", [P, B * NT, E])
        wsum = sf("wsum", [P, B * NT])
        wrec = sf("wrec", [P, B * NT])
        WG = sf("WG", [P, B * NT, E])
        wcol = sf("wcol", [P, 2, B * NT])
        W_raw = sf("W_raw", [P, 3, 1024])
        W_h, W_l = sf("W_h", [P, 2, 3, 1024], f32r), sf("W_l", [P, 2, 3, 1024], f32r)
        gl = sf("gl", [P, 2, T])
        hm = sf("hm", [P, 2, T])
        h_h, h_l = sf("h_h", [P, 2, FC, T], f32r), sf("h_l", [P, 2, FC, T], f32r)
        fs.close()

        def bank(k, n=512, rows=P):
            return PS[0:rows, k, 0:n]

        def as32(ap):
            return ap.bitcast(f32)

        def hold(eng, s, value):
            eng.wait_ge(s, value)
            eng.nop(nofuse=True)

        def split3(pe, o, lh, ll, rh, rl, first, last):
            pe.matmul(o, lh, rh, start=first, stop=False)
            pe.matmul(o, lh, rl, start=False, stop=False)
            return pe.matmul(o, ll, rh, start=False, stop=last)

        ld_w = sem("ld_w")
        ld_xt = sem("ld_xt")
        const_pool = sem("const_pool")
        const_dve = sem("const_dve")
        w_hi = sem("w_hi")
        w_lo = sem("w_lo")
        xt_hi, xt_lo = sem("xt_hi"), sem("xt_lo")
        qk_mm, v_mm = sem("qk_mm"), sem("v_mm")
        v_out = sem("v_out")
        dch = sem("dch")
        cen_ok, sq_ok, ve_ok, rs_ok, nrm_ok, gm_ok, feat_ok = (sem(n) for n in (
            "cen_ok", "sq_ok", "ve_ok", "rs_ok", "nrm_ok", "gm_ok", "feat_ok"))
        hi_ok, lo_ok = sem("hi_ok"), sem("lo_ok")
        tq_mm, tk_mm, qT_ok, kT_ok = sem("tq_mm"), sem("tk_mm"), sem("qT_ok"), sem("kT_ok")
        sc_mm, sqr_ok, mask_ok, av_mm = sem("sc_mm"), sem("sqr_ok"), sem("mask_ok"), sem("av_mm")
        osb_ok, ot_mm, y_ok, yt_mm, yh_ok, yl_ok = (sem(n) for n in (
            "osb_ok", "ot_mm", "y_ok", "yt_mm", "yh_ok", "yl_ok"))
        o_mm, res_ok = sem("o_mm"), sem("res_ok")
        lnv_ok, lnr_ok, x1_ok = sem("lnv_ok"), sem("lnr_ok"), sem("x1_ok")

        ld_w2, ld_bo = sem("ld_w2"), sem("ld_bo")
        xconst = sem("xconst")
        ld_c = [sem(f"ld_c{k}") for k in range(2)]
        ld_h = [sem(f"ld_h{k}") for k in range(3)]
        ld_m = sem("ld_m")
        c_hi, c_lo = sem("c_hi"), sem("c_lo")
        xs_ok, xb_ok = sem("xs_ok"), sem("xb_ok")
        misc_mm, misc_hi, misc_ok = sem("misc_mm"), sem("misc_hi"), sem("misc_ok")
        mx_mm, mx_ok, hmax_ok = sem("mx_mm"), sem("mx_ok"), sem("hmax_ok")
        st_mm, exp_ok, pv_mm = sem("st_mm"), sem("exp_ok"), sem("pv_mm")
        rec_ok, head_ok, oh_ok, ol_ok = sem("rec_ok"), sem("head_ok"), sem("oh_ok"), sem("ol_ok")
        xln_ch, xlnv_ok, xlnr_ok, x2_ok = sem("xln_ch"), sem("xlnv_ok"), sem("xlnr_ok"), sem("x2_ok")

        ld_g, gz_ok, gate_hi, gate_lo, low_ok = (sem(n) for n in ("ld_g", "gz_ok", "gate_hi", "gate_lo", "low_ok"))
        ft_mm, ft_hi, ft_ok = sem("ft_mm"), sem("ft_hi"), sem("ft_ok")
        gs_mm, gs_ok, gt_mm, route, rt_sh, rt_ex = (sem(n) for n in ("gs_mm", "gs_ok", "gt_mm", "route", "rt_sh", "rt_ex"))
        ld_e, we_hi, we_lo = sem("ld_e"), sem("we_hi"), sem("we_lo")
        h1_mm, h3_mm, silu_ok, hm_ok, hh_ok, hl_ok = (sem(n) for n in (
            "h1_mm", "h3_mm", "silu_ok", "hm_ok", "hh_ok", "hl_ok"))
        dn_mm, acc_ok, wcol_ok = sem("dn_mm"), sem("acc_ok"), sem("wcol_ok")
        fln_ch, flnv_ok, flnr_ok, x3_ok, st_out = (sem(n) for n in ("fln_ch", "flnv_ok", "flnr_ok", "x3_ok", "st_out"))
        UNITS = B * FC

        def beside(h, j):
            steps = []
            if j < 8 and h + 1 < XH:
                steps += [("max", h + 1, 2 * j), ("max", h + 1, 2 * j + 1)]
            if j == 10 and h + 1 < XH:
                steps += [("mrow", h + 1)]
            if h % 2 == 0 and h + 2 < XH and 1 <= j <= 4:
                steps += [("k", h // 2 + 1, j - 1)]
            if h % 2 == 0 and h + 2 < XH and j == 5:
                steps += [("q", h // 2 + 1)]
            if h % 2 == 0 and h >= 2 and j == 6:
                steps += [("osplit", h // 2 - 1)]
            if h % 2 == 0 and h >= 2 and j in (8, 9, 11, 12):
                steps += [("wo", h // 2 - 1, (8, 9, 11, 12).index(j))]
            return steps

        PROLOGUE = [("xt", c) for c in range(KC)] + [("q", 0)] + [("k", 0, k) for k in range(NB)] \
            + [("v", j) for j in range(NL)] + [("max", 0, v) for v in range(NT * NB)] + [("mrow", 0)]
        EPILOGUE = [("osplit", PAIRS - 1)] + [("wo", PAIRS - 1, i) for i in range(NT)]
        ALL = PROLOGUE + [s for h in range(XH) for j in range(NL) for s in beside(h, j)] + EPILOGUE
        MISC = {s: n for n, s in enumerate(s for s in ALL if s[0] not in ("max", "osplit"))}
        HIGH = {s: n for n, s in enumerate(s for s in MISC if s[0] in ("xt", "q", "k"))}
        NM, NH = len(MISC), len(HIGH)
        SLOT_LOADS = [len(range(k, XH, 3)) for k in range(3)]
        NMX = NT * NB

        def loaded(b, h):
            return 16 * 6 * (SLOT_LOADS[h % 3] * b + h // 3 + 1)

        def v_ones(j, h):
            return VX[0:LROWS[j], j, h // 2, XD * (h % 2):XD * (h % 2) + 2 * XD]

        block = ctx.enter_context(nc.Block())

        CH_S = 13


        @block.sync
        def _(sp):
            sp.dma_start(xt_raw[:, :, :], xt[0].rearrange("(c p) t -> p c t", p=P)).then_inc(ld_xt, 16)
            sp.dma_start(raw[:, 0:2, 0:3 * D], wqkv.rearrange("(c p) n -> p c n", p=P)).then_inc(ld_w, 16)
            sp.dma_start(raw[:, 0:2, 3 * D:4 * D], wo_s.rearrange("(c p) n -> p c n", p=P)).then_inc(ld_w, 16)
            sp.dma_start(gam[:, :], gamma.partition_broadcast(P)).then_inc(ld_w, 16)
            sp.dma_start(bet[:, :], beta.partition_broadcast(P)).then_inc(ld_w, 16)
            sp.dma_start(X[:, :, :], x.rearrange("b (i p) d -> p (b i) d", p=P)).then_inc(ld_w, 16)
            sp.dma_start(raw[:, 2, :].rearrange("p (c n) -> p c n", c=KC),
                         wq.rearrange("(c p) n -> p c n", p=P)).then_inc(ld_w2, 16)
            sp.dma_start(raw[:, 3, :].rearrange("p (c n) -> p c n", c=PAIRS),
                         wo_x.rearrange("(c p) n -> p c n", p=P)).then_inc(ld_w2, 16)
            sp.wait_ge(w_lo, 1)
            for k, w in ((0, wk), (1, wv)):
                sp.dma_start(raw[:, k, 0:INNER], w[0:P, :]).then_inc(ld_w2, 16)
                for half in range(2):
                    sp.dma_start(raw[64 * half:64 * half + 64, k, INNER:], w[P:C, :]).then_inc(ld_w2, 16)
            with sp.Fori(1, B) as b:
                hold(sp, x1_ok, NT * b)
                sp.dma_start(xt_raw[:, :, :], xt[bass.ds(b, 1)].rearrange("o (c p) t -> p (o c) t", p=P)).then_inc(ld_xt, 16)
            sp.wait_ge(x1_ok, NT * B)
            sp.wait_ge(w_lo, 5)
            sp.dma_start(bo_t[:, :], bo.partition_broadcast(P)).then_inc(ld_bo, 16)

            def head_in(b, h):
                s, half = h % 3, slice(64 * (h % 2), 64 * (h % 2) + 64)
                hold(sp, misc_ok, NM * b + MISC[("q", h // 2)] + 1)
                hold(sp, misc_ok, NM * b + MISC[("k", h // 2, NB - 1)] + 1)
                if h >= 3:
                    hold(sp, st_mm, NL * XH * b + NL * (h - 2))
                for dst, src in ((QA[0:64, s, :], Qh), (QA[64:P, s, :], Ql), (QB[0:64, s, :], Qh),
                                 (KA[0:64, s, :], Kh), (KA[64:P, s, :], Kh), (KB[0:64, s, :], Kl)):
                    sp.dma_start(as32(dst), as32(src[half, :])).then_inc(ld_h[s], 16)

            def maxima_in(b, h):
                hold(sp, misc_ok, NM * b + MISC[("mrow", h)] + 1)
                for i in range(NT):
                    sp.dma_start(as32(QB[64:65, h % 3, P * i:P * i + P]), as32(mrow[i:i + 1, h % 2, :])).then_inc(ld_m, 16)

            sp.wait_ge(xconst, 4)
            with sp.Fori(0, B) as b:
                hold(sp, x2_ok, NT * b + 1)
                for k in range(NB):
                    if k >= 2:
                        hold(sp, c_lo, 8 * b + 2 * (k - 1))
                    n = BEDGE[k + 1] - BEDGE[k]
                    cols = slice(BEDGE[k], BEDGE[k + 1])
                    cb = ctxt[bass.ds(b, 1)].rearrange("o c l -> (o c) l")
                    sp.dma_start(c_raw[:, k % 2, 0, 0:n], cb[0:P, cols]).then_inc(ld_c[k % 2], 16)
                    for half in range(2):
                        sp.dma_start(c_raw[64 * half:64 * half + 64, k % 2, 1, 0:n], cb[P:C, cols])\
                            .then_inc(ld_c[k % 2], 16)
                head_in(b, 0)
                head_in(b, 1)
                maxima_in(b, 0)
                for h in range(0, XH, 2):
                    if h + 2 < XH:
                        head_in(b, h + 2)
                    maxima_in(b, h + 1)
                    if h + 3 < XH:
                        head_in(b, h + 3)
                        maxima_in(b, h + 2)
            sp.wait_ge(x2_ok, NT * B + 1)
            sp.wait_ge(gz_ok, 1)
            sp.dma_start(G_raw[:, :, 0:E], gate.rearrange("(c p) e -> p c e", p=P)).then_inc(ld_g, 16)

            def load_expert(e):
                for k, w in enumerate((w1, w3, w2)):
                    src = w[bass.ds(e, 1)].rearrange("o (c p) n -> p (o c) n", p=P)
                    sp.dma_start(W_raw[:, k, :].rearrange("p (c n) -> p c n", c=src.shape[1]), src).then_inc(ld_e, 16)

            load_expert(0)
            with sp.Fori(1, E) as e:
                hold(sp, we_lo, 3 * e)
                load_expert(e)
            for tb in range(B):
                sp.wait_ge(x3_ok, NT * (tb + 1))
                sp.dma_start(out[tb].rearrange("(i p) d -> p i d", p=P), X[:, NT * tb:NT * tb + NT, :]).then_inc(st_out, 16)
            sp.wait_ge(st_out, 16 * B)

        N_LDW = 5

        @block.gpsimd
        def _(pool):
            pool.memset(ident[:, :], 0.0).then_inc(const_pool, 1)
            pool.memset(neg_half[:, :], -0.5).then_inc(const_pool, 1)
            pool.wait_ge(const_pool, 2)
            pool.affine_select(out=ident[:, :], in_=ident[:, :], compare_op=ALU.not_equal, fill=1.0,
                               base=0, pattern=[[-1, P]], channel_multiplier=1).then_inc(const_pool, 1)
            pool.wait_ge(ld_w, 16 * N_LDW)
            with pool.Fori(0, B) as b:
                pool.wait_ge(ve_ok, b + 1)
                pool.tensor_tensor(g_rs[:, :], g_var[:, :], neg_half[:, :], ALU.pow).then_inc(rs_ok, 1)
                for i in range(NT):
                    pool.wait_ge(nrm_ok, NT * b + i + 1)
                    v = cen[:, i, :].rearrange("p (g f) -> p g f", f=SF)
                    w = sq[:, i, :].rearrange("p (g f) -> p g f", f=SF)
                    pool.tensor_tensor(v, v, gam[:, :].unsqueeze(1).broadcast_to([P, 32, SF]), ALU.mult)\
                        .then_inc(gm_ok, 1)
                    pool.wait_ge(gm_ok, NT * b + i + 1)
                    pool.tensor_tensor(w, v, bet[:, :].unsqueeze(1).broadcast_to([P, 32, SF]), ALU.add)\
                        .then_inc(feat_ok, 1)
                for n in range(QUADS * NT * 4):
                    c = (n // 4) % NT
                    hold(pool, sqr_ok, 64 * b + n + 1)
                    blk = A[:, n % 8, P * c:P * c + P]
                    pool.affine_select(out=blk, in_=blk, compare_op=ALU.is_ge, fill=0.0, base=0,
                                       pattern=[[1, P]], channel_multiplier=-1).then_inc(mask_ok, 1)
                pool.wait_ge(lnv_ok, b + 1)
                pool.tensor_tensor(ln_rs[:, :], ln_ve[:, :], neg_half[:, 0:NT], ALU.pow).then_inc(lnr_ok, 1)
            pool.wait_ge(x1_ok, NT * B)
            pool.wait_ge(w_lo, 5)
            pool.memset(as32(KB[64:P, :, :]), 0.0).then_inc(xconst, 1)
            pool.wait_ge(xconst, 1)
            pool.memset(as32(QB[64:P, :, :]), 0.0).then_inc(xconst, 1)
            pool.wait_ge(xconst, 2)
            pool.memset(VX[:, :, :, XD:2 * XD], 1.0).then_inc(xconst, 1)
            pool.wait_ge(xconst, 3)
            pool.memset(as32(KB[64:65, :, :]), 1.0).then_inc(xconst, 1)
            with pool.Fori(0, B) as b:
                pool.wait_ge(xlnv_ok, b + 1)
                pool.tensor_tensor(ln_rs[:, :], ln_ve[:, :], neg_half[:, 0:NT], ALU.pow).then_inc(xlnr_ok, 1)
            pool.wait_ge(x2_ok, NT * B + 1)
            pool.memset(lower[:, :, :], 1.0).then_inc(low_ok, 1)
            pool.wait_ge(low_ok, 1)
            pool.affine_select(out=lower[:, :, :], in_=lower[:, :, :], compare_op=ALU.is_gt, fill=0.0, base=0,
                               pattern=[[1, E], [-1, E]], channel_multiplier=0).then_inc(low_ok, 1)

            def split_expert(e, k):
                for m in range(3):
                    pool.wait_ge(we_hi, 3 * e + m + 1)
                    pool.tensor_tensor(W_l[:, k, m, :], W_raw[:, m, :], as32(W_h[:, k, m, :]), ALU.subtract)\
                        .then_inc(we_lo, 1)

            with pool.Fori(0, E // 2) as ee:
                split_expert(2 * ee, 0)
                split_expert(2 * ee + 1, 1)
            for tb in range(B):
                pool.wait_ge(flnv_ok, tb + 1)
                pool.tensor_tensor(ln_rs[:, :], ln_ve[:, :], neg_half[:, 0:NT], ALU.pow).then_inc(flnr_ok, 1)

        @block.scalar
        def _(act):
            act.wait_ge(ld_w, 16 * N_LDW)
            act.copy(WSh[:, :, :], raw[:, 0:2, :]).then_inc(w_hi, 1)
            with act.Fori(0, B) as b:
                act.wait_ge(ld_xt, 16 * b + 16)
                act.copy(xt_h[:, :, :], xt_raw[:, :, :]).then_inc(xt_hi, 1)
                for i in range(NT):
                    act.wait_ge(v_mm, NT * b + i + 1)
                    act.copy(VS[:, i, :, 0:SF], bank(4 + i, D).rearrange("p (h f) -> p h f", f=SF)).then_inc(v_out, 1)
                for i in range(NT):
                    act.wait_ge(cen_ok, NT * b + i + 1)
                    act.activation(sq[:, i, :], cen[:, i, :], ACT.Square).then_inc(sq_ok, 1)
                for i in range(NT):
                    act.wait_ge(feat_ok, NT * b + i + 1)
                    f = sq[:, i, :].rearrange("p (s h f) -> p s h f", s=2, f=SF)
                    act.copy(QX[:, i, :, 0:2, :], f[:, 0].unsqueeze(2).broadcast_to([P, SH, 2, SF])).then_inc(hi_ok, 1)
                    act.copy(KX[:, i, :, 0:4:2, :], f[:, 1].unsqueeze(2).broadcast_to([P, SH, 2, SF])).then_inc(hi_ok, 1)
                if True:
                    def turn(g):
                        for q in range(2):
                            act.wait_ge(tq_mm, 8 * b + 2 * g + q + 1)
                            act.copy(qT[:, g % 2, q, :], bank(q)).then_inc(qT_ok, 1)
                    turn(0)
                    for g in range(QUADS):
                        for c in range(NT):
                            for j in range(4):
                                n = 16 * g + 4 * c + j
                                act.wait_ge(sc_mm, 64 * b + n + 1)
                                if n >= 8:
                                    act.wait_ge(av_mm, 16 * b + (n - 8) // 4 + 1)
                                act.activation(A[:, n % 8, P * c:T], PS[:, 4 + n % 2, P * c:T], ACT.Square,
                                               scale=0.25).then_inc(sqr_ok, 1)
                            if c == 0 and g + 1 < QUADS:
                                turn(g + 1)
                for c in range(KC):
                    act.wait_ge(yt_mm, KC * b + c + 1)
                    act.copy(y_h[:, c, :], bank(c)).then_inc(yh_ok, 1)

            act.wait_ge(ld_w2, 16 * 8)
            for dst, k in ((WKh, 0), (WVh, 1), (WQh, 2)):
                act.copy(dst[:, :, :], raw[:, k, :].rearrange("p (c n) -> p c n", c=2)).then_inc(w_hi, 1)
            act.copy(WOh[:, :, :], raw[:, 3, :].rearrange("p (c n) -> p c n", c=PAIRS)).then_inc(w_hi, 1)

            def high(b, s):
                kind, bk = s[0], bank(6 + MISC[s] % 2)
                act.wait_ge(misc_mm, NM * b + MISC[s] + 1)
                if kind == "xt":
                    ins = act.copy(x1_h[:, s[1], :], bk)
                if kind == "q":
                    if s[1] >= 1:
                        act.wait_ge(ld_h[(2 * s[1] - 2) % 3], loaded(b, 2 * s[1] - 2))
                        act.wait_ge(ld_h[(2 * s[1] - 1) % 3], loaded(b, 2 * s[1] - 1))
                    ins = act.copy(Qh[:, :], bk)
                if kind == "k":
                    lo, hi = BEDGE[s[2]], BEDGE[s[2] + 1]
                    if s[1] >= 1:
                        act.wait_ge(ld_h[(2 * s[1] - 2) % 3], loaded(b, 2 * s[1] - 2))
                        act.wait_ge(ld_h[(2 * s[1] - 1) % 3], loaded(b, 2 * s[1] - 1))
                    ins = act.copy(Kh[:, lo:hi], bk[:, lo - BSTART[s[2]]:hi - BSTART[s[2]]])
                ins.then_inc(misc_hi, 1)

            def split_out(b, p):
                act.wait_ge(head_ok, XH * b + 2 * p + 2)
                if p >= 1:
                    act.wait_ge(misc_mm, NM * b + MISC[("wo", p - 1, NT - 1)] + 1)
                act.copy(O_h[:, :], O[:, :]).then_inc(oh_ok, 1)

            with act.Fori(0, B) as b:
                for k in range(NB):
                    n, lo, hi = BEDGE[k + 1] - BEDGE[k], BEDGE[k], BEDGE[k + 1]
                    act.wait_ge(ld_c[k % 2], 48 * (2 * b + k // 2 + 1))
                    act.copy(Ch[:, lo:hi], c_raw[:, k % 2, 0, 0:n]).then_inc(c_hi, 1)
                    act.copy(Cc[0:64, lo:hi], c_raw[0:64, k % 2, 1, 0:n]).then_inc(c_hi, 1)
                    if k >= 1:
                        act.wait_ge(c_lo, 8 * b + 2 * k)
                    act.copy(c_tmp[64:P, 0:n], c_raw[64:P, k % 2, 1, 0:n]).then_inc(c_hi, 1)
                for s in PROLOGUE:
                    if s in HIGH:
                        high(b, s)
                for h in range(XH):
                    for j in range(NL):
                        u = NL * h + j
                        act.wait_ge(st_mm, NL * XH * b + u + 1)
                        if u >= NP:
                            act.wait_ge(pv_mm, NL * XH * b + u - NP + 1)
                        r = LROWS[j]
                        act.activation(PX[0:r, u % NP, :], bank(u % 2, rows=r), ACT.Exp, scale=XD ** -0.5)\
                            .then_inc(exp_ok, 1)
                        for s in beside(h, j):
                            if s in HIGH:
                                high(b, s)
                            if s[0] == "osplit":
                                split_out(b, s[1])
                split_out(b, PAIRS - 1)

            act.wait_ge(ld_g, 16)
            act.copy(G_h[:, :, :], G_raw[:, :, :]).then_inc(gate_hi, 1)

            def split_expert(e, k, again):
                if again:
                    act.wait_ge(dn_mm, 4 * B * (e - 1))
                for m in range(3):
                    act.wait_ge(ld_e, 48 * e + 48)
                    act.copy(W_h[:, k, m, :], W_raw[:, m, :]).then_inc(we_hi, 1)

            split_expert(0, 0, False)
            for n in range(B * KC):
                act.wait_ge(ft_mm, n + 1)
                act.copy(x2_h[:, n % KC, T * (n // KC):T * (n // KC + 1)], bank(n % 2)).then_inc(ft_hi, 1)
            for tb in range(B):
                act.wait_ge(gs_mm, tb + 1)
                act.copy(sT[:, T * tb:T * tb + T], bank(2 + tb % 2, rows=E)).then_inc(gs_ok, 1)
            act.wait_ge(rt_sh, 1)
            act.activation(ex[:, :, :], sh[:, :, :], ACT.Exp).then_inc(rt_ex, 1)

            def hidden(u, n):
                act.wait_ge(h1_mm, u + 1)
                if n >= 2:
                    act.wait_ge(hm_ok, u - 1)
                act.activation(gl[:, n % 2, :], bank(n % 2), ACT.Silu).then_inc(silu_ok, 1)

            def hidden_hi(u, n, g, later):
                act.wait_ge(hm_ok, u + 1)
                if later:
                    act.wait_ge(dn_mm, 4 * (g - 1))
                act.copy(h_h[:, (n // FC) % 2, n % FC, :], hm[:, n % 2, :]).then_inc(hh_ok, 1)

            def two_experts(ee, first, last):
                for n in range(2 * UNITS):
                    u, g = 2 * UNITS * ee + n, 2 * B * ee + n // FC
                    hidden(u, n)
                    if n >= 1:
                        hidden_hi(u - 1, n - 1, 2 * B * ee + (n - 1) // FC, not first or (n - 1) // FC >= 2)
                    if n == 2 * FC:
                        split_expert(2 * ee + 1, 1, not first)
                    if n == UNITS + 2 * FC and not last:
                        split_expert(2 * ee + 2, 0, True)
                n = 2 * UNITS - 1
                hidden_hi(2 * UNITS * ee + n, n, 2 * B * ee + n // FC, True)

            two_experts(0, True, False)
            with act.Fori(1, E // 2 - 1) as ee:
                two_experts(ee, False, False)
            two_experts(E // 2 - 1, False, True)

        @block.vector
        def _(dve):
            dve.memset(VS[:, :, :, SF:], 1.0).then_inc(const_dve, 1)
            dve.memset(as32(kT[64:P, :, 0:4:2, :]), 0.0).then_inc(const_dve, 1)
            dve.memset(as32(kT[0:64, :, 1:4:2, :]), 0.0).then_inc(const_dve, 1)
            dve.wait_ge(ld_w, 16 * N_LDW)
            dve.wait_ge(w_hi, 1)
            dve.tensor_tensor(WSl[:, :, :], raw[:, 0:2, :], as32(WSh[:, :, :]), ALU.subtract).then_inc(w_lo, 1)
            with dve.Fori(0, B) as b:
                link_at = [0]

                def link(ins):
                    link_at[0] += 1
                    ins.then_inc(dch, 1)
                    dve.wait_ge(dch, CH_S * b + link_at[0])

                dve.wait_ge(ld_xt, 16 * b + 16)
                dve.wait_ge(xt_hi, b + 1)
                dve.tensor_tensor(xt_l[:, :, :], xt_raw[:, :, :], as32(xt_h[:, :, :]), ALU.subtract).then_inc(xt_lo, 1)
                for i in range(NT):
                    dve.wait_ge(qk_mm, NT * b + i + 1)
                    ins = dve.tensor_reduce(g_sum[:, 32 * i:32 * i + 32],
                                            bank(i).rearrange("p (g f) -> p g f", f=SF), AX, ALU.add)
                    if i == NT - 1:
                        link(ins)
                link(dve.tensor_scalar(g_sum[:, :], g_sum[:, :], -1.0 / SF, None, ALU.mult))
                for i in range(NT):
                    dve.tensor_tensor(cen[:, i, :].rearrange("p (g f) -> p g f", f=SF),
                                      bank(i).rearrange("p (g f) -> p g f", f=SF),
                                      g_sum[:, 32 * i:32 * i + 32].unsqueeze(2).broadcast_to([P, 32, SF]),
                                      ALU.add).then_inc(cen_ok, 1)
                for i in range(NT):
                    dve.wait_ge(sq_ok, NT * b + i + 1)
                    ins = dve.tensor_reduce(g_var[:, 32 * i:32 * i + 32],
                                            sq[:, i, :].rearrange("p (g f) -> p g f", f=SF), AX, ALU.add)
                    if i == NT - 1:
                        link(ins)
                dve.tensor_scalar(g_var[:, :], g_var[:, :], 1.0 / SF, LN_EPS, ALU.mult, ALU.add).then_inc(ve_ok, 1)
                dve.wait_ge(rs_ok, b + 1)
                for i in range(NT):
                    v = cen[:, i, :].rearrange("p (g f) -> p g f", f=SF)
                    dve.tensor_tensor(v, v, g_rs[:, 32 * i:32 * i + 32].unsqueeze(2).broadcast_to([P, 32, SF]),
                                      ALU.mult).then_inc(nrm_ok, 1)
                for i in range(NT):
                    f = sq[:, i, :].rearrange("p (s h f) -> p s h f", s=2, f=SF)
                    dve.wait_ge(hi_ok, 8 * b + 2 * i + 1)
                    dve.tensor_tensor(QX[:, i, :, 2:4, :], f[:, 0].unsqueeze(2).broadcast_to([P, SH, 2, SF]),
                                      as32(QX[:, i, :, 0:2, :]), ALU.subtract).then_inc(lo_ok, 1)
                    dve.wait_ge(hi_ok, 8 * b + 2 * i + 2)
                    dve.tensor_tensor(KX[:, i, :, 1:4:2, :], f[:, 1].unsqueeze(2).broadcast_to([P, SH, 2, SF]),
                                      as32(KX[:, i, :, 0:4:2, :]), ALU.subtract).then_inc(lo_ok, 1)

                def turn(g):
                    for q in range(2):
                        dve.wait_ge(tk_mm, 8 * b + 2 * g + q + 1)
                        dve.tensor_copy(kT[0:64, g % 2, 2 * q, :], bank(2 + q, rows=64)).then_inc(kT_ok, 1)
                        dve.tensor_copy(kT[64:P, g % 2, 2 * q + 1, :], PS[64:P, 2 + q, :]).then_inc(kT_ok, 1)

                def quad_out(g):
                    dve.wait_ge(av_mm, 16 * b + 4 * g + 4)
                    if g >= 2:
                        dve.wait_ge(ot_mm, QUADS * b + g - 1)
                    dve.tensor_copy(osb[:, g % 2, :], bank(6)).then_inc(osb_ok, 1)

                def quad_norm(g):
                    dve.wait_ge(ot_mm, QUADS * b + g + 1)
                    o = bank(7).rearrange("p (i j f) -> p i j f", i=NT, j=4)
                    link(dve.tensor_scalar(den[:, :].rearrange("p (i j) -> p i j", j=4), o[:, :, :, SF], DEN_EPS, None,
                                           ALU.add))
                    link(dve.reciprocal(rden[:, :], den[:, :]))
                    dve.tensor_tensor(y[:, :, 4 * SF * g:4 * SF * g + 4 * SF].rearrange("p i (j f) -> p i j f", f=SF),
                                      o[:, :, :, 0:SF],
                                      rden[:, :].rearrange("p (i j) -> p i j", j=4).unsqueeze(3)
                                      .broadcast_to([P, NT, 4, SF]), ALU.mult).then_inc(y_ok, 1)

                turn(0)
                for g in range(QUADS):
                    if g + 1 < QUADS:
                        turn(g + 1)
                    if g >= 1:
                        quad_norm(g - 1)
                    quad_out(g)
                quad_norm(QUADS - 1)
                for c in range(KC):
                    dve.wait_ge(yh_ok, KC * b + c + 1)
                    dve.tensor_tensor(y_l[:, c, :], bank(c), as32(y_h[:, c, :]), ALU.subtract).then_inc(yl_ok, 1)
                for i in range(NT):
                    xi = X[:, bass.ds(NT * b + i, 1), :].rearrange("p o d -> p (o d)")
                    dve.wait_ge(o_mm, NT * b + i + 1)
                    dve.tensor_tensor(xi, bank(2 + i % 2, D), xi, ALU.add).then_inc(res_ok, 1)
                    hold(dve, res_ok, NT * b + i + 1)
                    ins = dve.bn_stats(ln_st[:, i, :], xi)
                    if i == NT - 1:
                        link(ins)
                dve.nop(nofuse=True)
                for i in range(NT):
                    ins = dve.bn_aggr(ln_mv[:, i, :], ln_st[:, i, :])
                link(ins)
                dve.tensor_scalar(ln_ve[:, :], ln_mv[:, :, 1], LN_EPS, None, ALU.add).then_inc(lnv_ok, 1)
                dve.wait_ge(lnr_ok, b + 1)
                for i in range(NT):
                    xi = X[:, bass.ds(NT * b + i, 1), :].rearrange("p o d -> p (o d)")
                    dve.tensor_scalar(xi, xi, ln_mv[:, i, 0:1], ln_rs[:, i:i + 1], ALU.subtract, ALU.mult)\
                        .then_inc(x1_ok, 1)
            for n, (dst, high, k) in enumerate(((WKl, WKh, 0), (WVl, WVh, 1), (WQl, WQh, 2), (WOl, WOh, 3))):
                c = PAIRS if k == 3 else 2
                dve.wait_ge(w_hi, n + 2)
                dve.tensor_tensor(dst[:, :, :], raw[:, k, :].rearrange("p (c n) -> p c n", c=c), as32(high[:, :, :]),
                                  ALU.subtract).then_inc(w_lo, 1)
            dve.wait_ge(x1_ok, NT * B)
            dve.wait_ge(ld_bo, 16)
            dve.tensor_copy(ln_ve[:, :], ln_ve[:, :]).then_inc(x2_ok, 1)

            def step(b, s):
                kind = s[0]
                if kind == "max":
                    h, v = s[1], s[2]
                    n = NMX * h + v
                    dve.wait_ge(mx_mm, NMX * XH * b + n + 1)
                    if h >= 2 and v == 0:
                        dve.wait_ge(hmax_ok, XH * b + h - 1)
                    dve.tensor_reduce(mxp[:, h % 2, v // NB, v % NB:v % NB + 1], bank(2 + n % 2, BW), AX, ALU.max)\
                        .then_inc(mx_ok, 1)
                    if v == NMX - 1:
                        dve.wait_ge(mx_ok, NMX * XH * b + n + 1)
                        if h >= 2:
                            dve.wait_ge(misc_mm, NM * b + MISC[("mrow", h - 2)] + 1)
                        dve.tensor_reduce(mx[:, h % 2, :], mxp[:, h % 2, :, :], AX, ALU.max).then_inc(hmax_ok, 1)
                    return
                if kind == "osplit":
                    dve.wait_ge(oh_ok, PAIRS * b + s[1] + 1)
                    if s[1] >= 1:
                        dve.wait_ge(misc_mm, NM * b + MISC[("wo", s[1] - 1, NT - 1)] + 1)
                    dve.tensor_tensor(O_l[:, :], O[:, :], as32(O_h[:, :]), ALU.subtract).then_inc(ol_ok, 1)
                    return
                bk = bank(6 + MISC[s] % 2)
                if s in HIGH:
                    dve.wait_ge(misc_hi, NH * b + HIGH[s] + 1)
                else:
                    dve.wait_ge(misc_mm, NM * b + MISC[s] + 1)
                if kind == "xt":
                    ins = dve.tensor_tensor(x1_l[:, s[1], :], bk, as32(x1_h[:, s[1], :]), ALU.subtract)
                if kind == "q":
                    ins = dve.tensor_tensor(Ql[:, :], bk, as32(Qh[:, :]), ALU.subtract)
                if kind == "k":
                    lo, hi = BEDGE[s[2]], BEDGE[s[2] + 1]
                    ins = dve.tensor_tensor(Kl[:, lo:hi], bk[:, lo - BSTART[s[2]]:hi - BSTART[s[2]]],
                                            as32(Kh[:, lo:hi]), ALU.subtract)
                if kind == "v":
                    r = LROWS[s[1]]
                    dst = VX[0:r, s[1], :, :].rearrange("p q (three d) -> p q three d", d=XD)[:, :, 0:3:2, :]
                    ins = dve.tensor_copy(dst, bank(6 + MISC[s] % 2, rows=r).rearrange("p (q two d) -> p q two d",
                                                                                       two=2, d=XD))
                if kind == "mrow":
                    h = s[1]
                    if h >= 2:
                        dve.wait_ge(ld_m, 16 * NT * (XH * b + h - 1))
                    ins = dve.tensor_scalar(mrow[:, h % 2, :], bank(6 + MISC[s] % 2, P, NT), -1.0, None, ALU.mult)
                if kind == "wo":
                    xi = X[:, bass.ds(NT * b + s[2], 1), :].rearrange("p o d -> p (o d)")
                    if s[1] >= 1:
                        dve.wait_ge(misc_ok, NM * b + MISC[("wo", s[1] - 1, s[2])] + 1)
                    ins = dve.tensor_tensor(xi, bank(6 + MISC[s] % 2, D), xi, ALU.add)
                ins.then_inc(misc_ok, 1)

            def head_out(b, h):
                bk, p = 4 + h % 2, h // 2
                val = slice(64 * (h % 2), 64 * (h % 2) + 64)
                tot = slice(64 - 64 * (h % 2), 128 - 64 * (h % 2))
                dve.wait_ge(pv_mm, NL * (XH * b + h + 1))
                if h >= 2:
                    dve.wait_ge(head_ok, XH * b + h - 1)
                    dve.wait_ge(ol_ok, PAIRS * b + p)
                dve.reciprocal(R[val, :], PS[tot, bk, :]).then_inc(rec_ok, 1)
                dve.wait_ge(rec_ok, XH * b + h + 1)
                dve.tensor_tensor(O[val, :], PS[val, bk, :], R[val, :], ALU.mult).then_inc(head_ok, 1)

            with dve.Fori(0, B) as b:
                xb = X[:, bass.ds(NT * b, NT), :]
                dve.wait_ge(x2_ok, NT * b + 1)
                dve.tensor_copy(xs[:, :, :], xb).then_inc(xs_ok, 1)
                dve.wait_ge(xs_ok, b + 1)
                dve.tensor_tensor(xb, xb, bo_t[:, :].unsqueeze(1).broadcast_to([P, NT, D]), ALU.add).then_inc(xb_ok, 1)
                for k in range(NB):
                    n, lo, hi = BEDGE[k + 1] - BEDGE[k], BEDGE[k], BEDGE[k + 1]
                    dve.wait_ge(c_hi, 12 * b + 3 * k + 1)
                    dve.tensor_tensor(Cl[:, lo:hi], c_raw[:, k % 2, 0, 0:n], as32(Ch[:, lo:hi]), ALU.subtract)\
                        .then_inc(c_lo, 1)
                    dve.wait_ge(c_hi, 12 * b + 3 * k + 3)
                    dve.tensor_tensor(Cc[64:P, lo:hi], c_raw[64:P, k % 2, 1, 0:n], as32(c_tmp[64:P, 0:n]), ALU.subtract)\
                        .then_inc(c_lo, 1)
                dve.wait_ge(xb_ok, b + 1)
                for s in PROLOGUE:
                    step(b, s)
                for h in range(XH):
                    for j in range(NL):
                        for s in beside(h, j):
                            step(b, s)
                    head_out(b, h)
                for s in EPILOGUE:
                    step(b, s)
                for i in range(NT):
                    xi = X[:, bass.ds(NT * b + i, 1), :].rearrange("p o d -> p (o d)")
                    hold(dve, misc_ok, NM * b + MISC[("wo", PAIRS - 1, i)] + 1)
                    ins = dve.bn_stats(ln_st[:, i, :], xi)
                ins.then_inc(xln_ch, 1)
                hold(dve, xln_ch, 2 * b + 1)
                for i in range(NT):
                    ins = dve.bn_aggr(ln_mv[:, i, :], ln_st[:, i, :])
                ins.then_inc(xln_ch, 1)
                dve.wait_ge(xln_ch, 2 * b + 2)
                dve.tensor_scalar(ln_ve[:, :], ln_mv[:, :, 1], LN_EPS, None, ALU.add).then_inc(xlnv_ok, 1)
                dve.wait_ge(xlnr_ok, b + 1)
                for i in range(NT):
                    xi = X[:, bass.ds(NT * b + i, 1), :].rearrange("p o d -> p (o d)")
                    dve.tensor_scalar(xi, xi, ln_mv[:, i, 0:1], ln_rs[:, i:i + 1], ALU.subtract, ALU.mult)\
                        .then_inc(x2_ok, 1)

            dve.wait_ge(x2_ok, NT * B + 1)
            dve.memset(G_raw[:, :, :], 0.0).then_inc(gz_ok, 1)
            dve.wait_ge(gate_hi, 1)
            dve.tensor_tensor(G_l[:, :, :], G_raw[:, :, :], as32(G_h[:, :, :]), ALU.subtract).then_inc(gate_lo, 1)
            for n in range(B * KC):
                cols = slice(T * (n // KC), T * (n // KC + 1))
                dve.wait_ge(ft_hi, n + 1)
                dve.tensor_tensor(x2_l[:, n % KC, cols], bank(n % 2), as32(x2_h[:, n % KC, cols]), ALU.subtract)\
                    .then_inc(ft_ok, 1)
            routed = [0]

            def rt(ins):
                routed[0] += 1
                ins.then_inc(route, 1)
                dve.wait_ge(route, routed[0])

            NTT = B * NT
            dve.wait_ge(gt_mm, 1)
            rt(dve.tensor_copy(S8[:, :, :], bank(4, NTT * E).rearrange("p (t e) -> p t e", e=E)))
            rt(dve.tensor_reduce(smax[:, :], S8[:, :, :], AX, ALU.max))
            dve.tensor_tensor(sh[:, :, :], S8[:, :, :], smax[:, :].unsqueeze(2).broadcast_to([P, NTT, E]),
                              ALU.subtract).then_inc(rt_sh, 1)
            own = S8[:, :, :].unsqueeze(3).broadcast_to([P, NTT, E, E])
            other = S8[:, :, :].unsqueeze(2).broadcast_to([P, NTT, E, E])
            rt(dve.tensor_tensor(cmp[:, :, :, :], other, own, ALU.is_gt))
            rt(dve.tensor_tensor(cmp2[:, :, :, :], other, own, ALU.is_equal))
            dve.wait_ge(low_ok, 2)
            flat = "p t e f -> p t (e f)"
            low = lower[:, :, :].rearrange("p e f -> p (e f)").unsqueeze(1).broadcast_to([P, NTT, E * E])
            rt(dve.tensor_tensor(cmp2[:, :, :, :].rearrange(flat), cmp2[:, :, :, :].rearrange(flat), low, ALU.mult))
            rt(dve.tensor_tensor(cmp[:, :, :, :], cmp[:, :, :, :], cmp2[:, :, :, :], ALU.add))
            rt(dve.tensor_reduce(rank[:, :, :], cmp[:, :, :, :], AX, ALU.add))
            rt(dve.tensor_scalar(chosen[:, :, :], rank[:, :, :], 1.5, None, ALU.is_lt))
            dve.wait_ge(rt_ex, 1)
            rt(dve.tensor_tensor(exs[:, :, :], ex[:, :, :], chosen[:, :, :], ALU.mult))
            rt(dve.tensor_reduce(wsum[:, :], exs[:, :, :], AX, ALU.add))
            rt(dve.reciprocal(wrec[:, :], wsum[:, :]))
            rt(dve.tensor_tensor(WG[:, :, :], exs[:, :, :], wrec[:, :].unsqueeze(2).broadcast_to([P, NTT, E]), ALU.mult))

            def hidden(u, n):
                dve.wait_ge(silu_ok, u + 1)
                dve.wait_ge(h3_mm, u + 1)
                if n >= 2:
                    dve.wait_ge(hh_ok, u - 1)
                    dve.wait_ge(hl_ok, u - 1)
                dve.tensor_tensor(hm[:, n % 2, :], bank(2 + n % 2), gl[:, n % 2, :], ALU.mult).then_inc(hm_ok, 1)

            def hidden_lo(u, n):
                dve.wait_ge(hh_ok, u + 1)
                dve.tensor_tensor(h_l[:, (n // FC) % 2, n % FC, :], hm[:, n % 2, :],
                                  as32(h_h[:, (n // FC) % 2, n % FC, :]), ALU.subtract).then_inc(hl_ok, 1)

            def collect(ee, blk):
                k, tb = blk // B, blk % B
                for i in range(NT):
                    t, a = NT * tb + i, NT * (2 * B * ee + blk) + i
                    dve.wait_ge(dn_mm, a + 1)
                    if blk >= B:
                        dve.wait_ge(acc_ok, a + 1 - NT * B)
                    dve.scalar_tensor_tensor(out=X[:, t, :], in0=bank(4 + i % 2, D), scalar=wcol[:, k, t:t + 1],
                                             in1=X[:, t, :], op0=ALU.mult, op1=ALU.add).then_inc(acc_ok, 1)

            def layer_norm_out(tb):
                dve.wait_ge(acc_ok, NT * B * (E - 1) + NT * tb + NT)
                for i in range(NT):
                    ins = dve.bn_stats(ln_st[:, i, :], X[:, NT * tb + i, :])
                ins.then_inc(fln_ch, 1)
                dve.wait_ge(fln_ch, 2 * tb + 1)
                for i in range(NT):
                    ins = dve.bn_aggr(ln_mv[:, i, :], ln_st[:, i, :])
                ins.then_inc(fln_ch, 1)
                dve.wait_ge(fln_ch, 2 * tb + 2)
                dve.tensor_scalar(ln_ve[:, :], ln_mv[:, :, 1], LN_EPS, None, ALU.add).then_inc(flnv_ok, 1)
                dve.wait_ge(flnr_ok, tb + 1)
                for i in range(NT):
                    xi = X[:, NT * tb + i, :]
                    dve.tensor_scalar(xi, xi, ln_mv[:, i, 0:1], ln_rs[:, i:i + 1], ALU.subtract, ALU.mult)\
                        .then_inc(x3_ok, 1)

            def two_experts(ee, first, last):
                if not first:
                    dve.wait_ge(acc_ok, 2 * NT * B * ee)
                dve.tensor_copy(wcol[:, :, :], WG[:, :, bass.ds(2 * ee, 2)].rearrange("p t k -> p k t")).then_inc(wcol_ok, 1)
                dve.wait_ge(wcol_ok, ee + 1)
                for n in range(2 * UNITS):
                    u = 2 * UNITS * ee + n
                    hidden(u, n)
                    if n >= 1:
                        hidden_lo(u - 1, n - 1)
                    if n % FC == FC - 1 and n >= FC:
                        collect(ee, n // FC - 1)
                        if last and n // FC - 1 >= B:
                            layer_norm_out(n // FC - 1 - B)
                hidden_lo(2 * UNITS * (ee + 1) - 1, 2 * UNITS - 1)
                collect(ee, 2 * B - 1)
                if last:
                    layer_norm_out(B - 1)

            two_experts(0, True, False)
            with dve.Fori(1, E // 2 - 1) as ee:
                two_experts(ee, False, False)
            two_experts(E // 2 - 1, False, True)

        @block.tensor
        def _(pe):
            pe.wait_ge(const_pool, 3)
            pe.wait_ge(const_dve, 3)
            pe.wait_ge(w_lo, 1)
            with pe.Fori(0, B) as b:
                pe.wait_ge(xt_hi, b + 1)
                pe.wait_ge(xt_lo, b + 1)
                for i in range(NT):
                    t = slice(P * i, P * i + P)
                    for c in range(KC):
                        mm = split3(pe, bank(i), xt_h[:, c, t], xt_l[:, c, t], WSh[:, c, 0:2 * D], WSl[:, c, 0:2 * D],
                                    c == 0, c == KC - 1)
                    mm.then_inc(qk_mm, 1)
                for i in range(NT):
                    t = slice(P * i, P * i + P)
                    for c in range(KC):
                        mm = split3(pe, bank(4 + i, D), xt_h[:, c, t], xt_l[:, c, t], WSh[:, c, 2 * D:3 * D],
                                    WSl[:, c, 2 * D:3 * D], c == 0, c == KC - 1)
                    mm.then_inc(v_mm, 1)

                def turn(g):
                    for src, bk, done in ((QX, 0, tq_mm), (KX, 2, tk_mm)):
                        for q in range(2):
                            h = 4 * g + 2 * q
                            for i in range(NT):
                                mm = pe.transpose(PS[:, bk + q, P * i:P * i + P],
                                                  as32(src[:, i, h:h + 2, :, :]).rearrange("p h s f -> p (h s f)"),
                                                  ident[:, :])
                            mm.then_inc(done, 1)

                def scores(g, c):
                    for j in range(4):
                        n = 16 * g + 4 * c + j
                        if n >= 2:
                            pe.wait_ge(sqr_ok, 64 * b + n - 1)
                        pe.matmul(PS[:, 4 + n % 2, P * c:T], kT[:, g % 2, j, P * c:P * c + P],
                                  qT[:, g % 2, j // 2, P * c:T], start=True, stop=True).then_inc(sc_mm, 1)

                def values(g, c):
                    pe.wait_ge(mask_ok, 64 * b + 16 * g + 4 * c + 4)
                    if c == 0 and g >= 1:
                        pe.wait_ge(osb_ok, QUADS * b + g)
                    for j in range(4):
                        n = 16 * g + 4 * c + j
                        mm = pe.matmul(PS[32 * j:32 * j + 32, 6, P * c:T], VS[:, c, 4 * g + j, :], A[:, n % 8, P * c:T],
                                       start=(c == 0), stop=(c == NT - 1))
                    mm.then_inc(av_mm, 1)

                def back(g):
                    pe.wait_ge(osb_ok, QUADS * b + g + 1)
                    if g >= 1:
                        pe.wait_ge(y_ok, QUADS * b + g)
                    for i in range(NT):
                        mm = pe.transpose(PS[:, 7, P * i:P * i + P], osb[:, g % 2, P * i:P * i + P], ident[:, :])
                    mm.then_inc(ot_mm, 1)

                pe.wait_ge(lo_ok, 8 * b + 8)
                pe.wait_ge(v_out, NT * b + NT)
                turn(0)
                for g in range(QUADS):
                    pe.wait_ge(qT_ok, 8 * b + 2 * g + 2)
                    pe.wait_ge(kT_ok, 16 * b + 4 * g + 4)
                    scores(g, 0)
                    if g + 1 < QUADS:
                        turn(g + 1)
                    for c in range(NT):
                        if c + 1 < NT:
                            scores(g, c + 1)
                        if c == 1 and g >= 1:
                            back(g - 1)
                        values(g, c)
                back(QUADS - 1)
                pe.wait_ge(y_ok, QUADS * b + QUADS)
                for c in range(KC):
                    for i in range(NT):
                        mm = pe.transpose(PS[:, c, P * i:P * i + P], y[:, i, P * c:P * c + P], ident[:, :])
                    mm.then_inc(yt_mm, 1)
                pe.wait_ge(yl_ok, KC * b + KC)
                for i in range(NT):
                    t = slice(P * i, P * i + P)
                    if i >= 2:
                        pe.wait_ge(res_ok, NT * b + i - 1)
                    for c in range(KC):
                        mm = split3(pe, bank(2 + i % 2, D), y_h[:, c, t], y_l[:, c, t], WSh[:, c, 3 * D:], WSl[:, c, 3 * D:],
                                    c == 0, c == KC - 1)
                    mm.then_inc(o_mm, 1)

            def context_product(o, lhs, rhs, first_is_weight):
                ops = []
                for wc, cc in (((0, "h"), Ch), ((0, "h"), Cl), ((0, "l"), Ch), ((1, "h"), Cc), ((1, "l"), Cc)):
                    ops.append((lhs(wc), rhs(cc)) if first_is_weight else (lhs(cc), rhs(wc)))
                for n, (l, r) in enumerate(ops):
                    mm = pe.matmul(o, l, r, start=(n == 0), stop=(n == len(ops) - 1))
                return mm

            def step(b, s):
                kind = s[0]
                if kind == "osplit":
                    return
                if kind == "max":
                    h, v = s[1], s[2]
                    n, i, k = NMX * h + v, v // NB, v % NB
                    if v == 0:
                        pe.wait_ge(ld_h[h % 3], loaded(b, h))
                    if n >= 2:
                        pe.wait_ge(mx_ok, NMX * XH * b + n - 1)
                    pe.matmul(bank(2 + n % 2, BW), QA[:, h % 3, P * i:P * i + P], KA[:, h % 3, BSTART[k]:BSTART[k] + BW],
                              start=True, stop=True).then_inc(mx_mm, 1)
                    return
                m = MISC[s]
                if m >= 2:
                    pe.wait_ge(misc_ok, NM * b + m - 1)
                bk = bank(6 + m % 2)
                if kind == "xt":
                    pe.wait_ge(xs_ok, b + 1)
                    for i in range(NT):
                        mm = pe.transpose(bk[:, P * i:P * i + P], xs[:, i, P * s[1]:P * s[1] + P], ident[:, :])
                if kind == "q":
                    pe.wait_ge(misc_ok, NM * b + MISC[("xt", KC - 1)] + 1)
                    w = slice(P * s[1], P * s[1] + P)
                    for c in range(KC):
                        mm = split3(pe, bk, WQh[:, c, w], WQl[:, c, w], x1_h[:, c, :], x1_l[:, c, :],
                                    c == 0, c == KC - 1)
                if kind == "k":
                    pe.wait_ge(c_lo, 8 * b + 8)
                    w = slice(P * s[1], P * s[1] + P)
                    cols = slice(BSTART[s[2]], BSTART[s[2]] + BW)
                    mm = context_product(bk[:, 0:BW], lambda wc: (WKh if wc[1] == "h" else WKl)[:, wc[0], w],
                                         lambda cc: cc[:, cols], True)
                if kind == "v":
                    r = LROWS[s[1]]
                    cols = slice(P * s[1], P * s[1] + r)
                    mm = context_product(bk[0:r, :], lambda cc: cc[:, cols],
                                         lambda wc: (WVh if wc[1] == "h" else WVl)[:, wc[0], :], False)
                if kind == "mrow":
                    pe.wait_ge(hmax_ok, XH * b + s[1] + 1)
                    mm = pe.transpose(PS[0:NT, 6 + m % 2, 0:P], mx[:, s[1] % 2, :], ident[:, :])
                if kind == "wo":
                    pe.wait_ge(ol_ok, PAIRS * b + s[1] + 1)
                    t = slice(P * s[2], P * s[2] + P)
                    mm = split3(pe, bk[:, 0:D], O_h[:, t], O_l[:, t], WOh[:, s[1], :], WOl[:, s[1], :], True, True)
                mm.then_inc(misc_mm, 1)

            def scores_t(b, h, j):
                u = NL * h + j
                if j == 0:
                    pe.wait_ge(ld_h[h % 3], loaded(b, h))
                    pe.wait_ge(ld_m, 16 * NT * (XH * b + h + 1))
                if u >= 2:
                    pe.wait_ge(exp_ok, NL * XH * b + u - 1)
                keys = slice(P * j, P * j + LROWS[j])
                o = bank(u % 2, rows=LROWS[j])
                pe.matmul(o, KA[:, h % 3, keys], QA[:, h % 3, :], start=True, stop=False)
                pe.matmul(o, KB[:, h % 3, keys], QB[:, h % 3, :], start=False, stop=True).then_inc(st_mm, 1)

            pe.wait_ge(w_lo, 5)
            pe.wait_ge(xconst, 4)
            with pe.Fori(0, B) as b:
                for s in PROLOGUE:
                    step(b, s)
                pe.wait_ge(misc_ok, NM * b + MISC[("v", NL - 1)] + 1)
                scores_t(b, 0, 0)
                for h in range(XH):
                    for j in range(NL):
                        u = NL * h + j
                        if u + 1 < NL * XH:
                            scores_t(b, (u + 1) // NL, (u + 1) % NL)
                        for s in beside(h, j):
                            step(b, s)
                        pe.wait_ge(exp_ok, NL * XH * b + u + 1)
                        if j == 0 and h >= 2:
                            pe.wait_ge(head_ok, XH * b + h - 1)
                        pe.matmul(bank(4 + h % 2), v_ones(j, h), PX[0:LROWS[j], u % NP, :], start=(j == 0),
                                  stop=(j == NL - 1)).then_inc(pv_mm, 1)
                for s in EPILOGUE:
                    step(b, s)

            pe.wait_ge(x2_ok, NT * B + 1)
            for n in range(B * KC):
                if n >= 2:
                    pe.wait_ge(ft_ok, n - 1)
                for i in range(NT):
                    mm = pe.transpose(PS[:, n % 2, P * i:P * i + P],
                                      X[:, NT * (n // KC) + i, P * (n % KC):P * (n % KC) + P], ident[:, :])
                mm.then_inc(ft_mm, 1)
            pe.wait_ge(gate_lo, 1)
            for tb in range(B):
                cols = slice(T * tb, T * tb + T)
                pe.wait_ge(ft_ok, KC * (tb + 1))
                if tb >= 2:
                    pe.wait_ge(gs_ok, tb - 1)
                for c in range(KC):
                    mm = split3(pe, bank(2 + tb % 2, rows=E), G_h[:, c, 0:E], G_l[:, c, 0:E], x2_h[:, c, cols], x2_l[:, c, cols],
                                c == 0, c == KC - 1)
                mm.then_inc(gs_mm, 1)
            pe.wait_ge(gs_ok, B)
            for t in range(B * NT):
                mm = pe.transpose(PS[:, 4, E * t:E * t + E], sT[:, P * t:P * t + P], ident[0:E, 0:E])
            mm.then_inc(gt_mm, 1)
            pe.wait_ge(route, 1)

            def up(ee, n):
                u, k, tb, f = 2 * UNITS * ee + n, n // UNITS, (n // FC) % B, n % FC
                cols = slice(T * tb, T * tb + T)
                for m, done, free in ((0, h1_mm, silu_ok), (1, h3_mm, hm_ok)):
                    if n >= 2:
                        pe.wait_ge(free, u - 1)
                    for c in range(KC):
                        w = slice(FF * c + P * f, FF * c + P * f + P)
                        mm = split3(pe, bank(2 * m + n % 2), W_h[:, k, m, w], W_l[:, k, m, w], x2_h[:, c, cols],
                                    x2_l[:, c, cols], c == 0, c == KC - 1)
                    mm.then_inc(done, 1)

            def down(ee, blk):
                k = blk // B
                pe.wait_ge(hl_ok, FC * (2 * B * ee + blk + 1))
                for i in range(NT):
                    a, t = NT * (2 * B * ee + blk) + i, slice(P * i, P * i + P)
                    if NT * blk + i >= 2:
                        pe.wait_ge(acc_ok, a - 1)
                    for f in range(FC):
                        w = slice(D * f, D * f + D)
                        mm = split3(pe, bank(4 + i % 2, D), h_h[:, blk % 2, f, t], h_l[:, blk % 2, f, t], W_h[:, k, 2, w],
                                    W_l[:, k, 2, w], f == 0, f == FC - 1)
                    mm.then_inc(dn_mm, 1)

            def two_experts(ee, first):
                for n in range(2 * UNITS):
                    if n % UNITS == 0:
                        pe.wait_ge(we_lo, 3 * (2 * ee + n // UNITS) + 3)
                    up(ee, n)
                    if n % FC == FC - 1 and n >= FC:
                        down(ee, n // FC - 1)
                down(ee, 2 * B - 1)

            two_experts(0, True)
            with pe.Fori(1, E // 2 - 1) as ee:
                two_experts(ee, False)
            two_experts(E // 2 - 1, False)


def kernel(**inputs):
    import numpy as _np
    import concourse.bacc as _bacc
    from concourse import mybir as _mybir
    from concourse.bass_utils import run_bass_kernel_spmd as _run

    a = {k: _np.asarray(v) for k, v in inputs.items()}
    lay = {
        "x": a["x"],
        "xt": a["x"].transpose(0, 2, 1),
        "ctxt": a["ctx_768"].transpose(0, 2, 1),
        "wqkv": _np.concatenate([a["L0_attn_Wq"], a["L0_attn_Wk"], a["L0_attn_Wv"]]).T,
        "wo_s": a["L0_attn_Wo"].T,
        "gamma": a["L0_attn_gamma"],
        "beta": a["L0_attn_beta"],
        "wq": a["L0_xattn_Wq"],
        "wk": a["L0_xattn_Wk"],
        "wv": a["L0_xattn_Wv"],
        "wo_x": a["L0_xattn_Wo"],
        "bo": a["L0_xattn_bo"],
        "gate": a["L0_ffn_gate_w"].T,
        "w1": a["L0_ffn_w1"].transpose(0, 2, 1),
        "w3": a["L0_ffn_w3"].transpose(0, 2, 1),
        "w2": a["L0_ffn_w2"].transpose(0, 2, 1),
    }
    nc = _bacc.Bacc("TRN2", target_bir_lowering=False, num_devices=1)
    arrays, args = {}, []
    for name, v in lay.items():
        v = _np.ascontiguousarray(v)
        arrays[f"in_{name}"] = v
        args.append(nc.dram_tensor(f"in_{name}", v.shape, _mybir.dt.from_np(v.dtype), kind="ExternalInput").ap())
    o = nc.dram_tensor("out_0", (B, T, D), _mybir.dt.float32, kind="ExternalOutput").ap()
    decoder_layer(nc, *args, o)
    r = _run(nc, [arrays], core_ids=[0])
    return r.results[0]["out_0"]
```

```python
import concourse.bass as bass
from concourse import mybir
from contextlib import ExitStack

B, T, D = 4, 512, 256
P = 128
NT = T // P
KC = D // P
SH, SF = 16, 16
L, C = 1601, 192
XH, XD = 8, 64
INNER = XH * XD
E, FF = 8, 512
FC = FF // P
LN_EPS = 1e-5
DEN_EPS = 1e-5
QUADS = SH // 4
PAIRS = XH // 2
NL = (L + P - 1) // P
LROWS = [min(P, L - P * j) for j in range(NL)]
BW = 402
BSTART = [0, 400, 800, L - BW]
BEDGE = [0, 402, 802, 1202, L]
NB = len(BSTART)


def decoder_layer(nc, x, xt, ctxt, wqkv, wo_s, gamma, beta, wq, wk, wv, wo_x, bo, gate, w1, w3, w2, out):
    f32 = mybir.dt.float32
    f32r = mybir.dt.float32r
    ALU = mybir.AluOpType
    ACT = mybir.ActivationFunctionType
    AX = mybir.AxisListType.X

    ctx = ExitStack()
    with ctx:
        def sem(name):
            return ctx.enter_context(nc.semaphore(name))

        def keep(name, shape, dt=f32):
            return ctx.enter_context(nc.sbuf_tensor(name, shape, dt))

        def stage_buffers(stack):
            return lambda name, shape, dt=f32: stack.enter_context(nc.sbuf_tensor(name, shape, dt))

        X = keep("X", [P, B * NT, D])
        ident = keep("ident", [P, P])
        gam = keep("gam", [P, SF])
        bet = keep("bet", [P, SF])
        neg_half = keep("neg_half", [P, 128])
        ln_st = keep("ln_st", [P, NT, 6])
        ln_mv = keep("ln_mv", [P, NT, 2])
        ln_ve = keep("ln_ve", [P, NT])
        ln_rs = keep("ln_rs", [P, NT])

        PS = ctx.enter_context(nc.psum_tensor("PS", [P, 8, 512], f32))

        both = ExitStack()
        sx = stage_buffers(both)
        WQh, WQl = sx("WQh", [P, KC, INNER], f32r), sx("WQl", [P, KC, INNER], f32r)
        WKh, WKl = sx("WKh", [P, 2, INNER], f32r), sx("WKl", [P, 2, INNER], f32r)
        WVh, WVl = sx("WVh", [P, 2, INNER], f32r), sx("WVl", [P, 2, INNER], f32r)
        WOh, WOl = sx("WOh", [P, PAIRS, D], f32r), sx("WOl", [P, PAIRS, D], f32r)

        st = ExitStack()
        ss = stage_buffers(st)
        raw = ss("raw", [P, 4, 1024])
        WSh, WSl = ss("WSh", [P, KC, 4 * D], f32r), ss("WSl", [P, KC, 4 * D], f32r)
        xt_raw = ss("xt_raw", [P, KC, T])
        xt_h, xt_l = ss("xt_h", [P, KC, T], f32r), ss("xt_l", [P, KC, T], f32r)
        cen = ss("cen", [P, 2, 2 * D])
        feat = ss("feat", [P, NT, 2 * D])
        Vn = ss("Vn", [P, NT, D])
        g_mean = ss("g_mean", [P, 2, 32])
        g_var = ss("g_var", [P, 2, 32])
        g_sd = ss("g_sd", [P, 2, 32])
        g_rs = ss("g_rs", [P, 2, 32])
        g_t = ss("g_t", [P, 2, 32])
        QX = ss("QX", [P, NT, SH, 4, SF], f32r)
        KX = ss("KX", [P, NT, SH, 4, SF], f32r)
        qT = ss("qT", [P, 2, 2, T], f32r)
        kT = ss("kT", [P, 2, 4, T], f32r)
        A = ss("A", [P, 8, T])
        VS = ss("VS", [P, NT, SH, 2 * SF])
        osb = ss("osb", [P, 2, T])
        den = ss("den", [P, NT * 4])
        rden = ss("rden", [P, NT * 4])
        y = ss("y", [P, NT, D])
        y_h, y_l = ss("y_h", [P, KC, T], f32r), ss("y_l", [P, KC, T], f32r)
        st.close()

        xs_ = ExitStack()
        sxx = stage_buffers(xs_)
        work = sxx("work", [P, 6 * T])
        c_raw = work[:, 0:4 * BW].rearrange("p (k r n) -> p k r n", k=2, r=2)
        xs = work[:, 4 * BW:4 * BW + NT * D].rearrange("p (i d) -> p i d", i=NT)
        NP = 4
        PX = work[:, 0:NP * T].rearrange("p (k t) -> p k t", k=NP)
        R = work[:, NP * T:(NP + 1) * T]
        O = work[:, (NP + 1) * T:]
        c_tmp = sxx("c_tmp", [P, BW], f32r)
        Ch = sxx("Ch", [P, L], f32r)
        Cl = sxx("Cl", [P, L], f32r)
        Cc = sxx("Cc", [P, L], f32r)
        VX = sxx("VX", [P, NL, PAIRS, 3 * XD])
        Kh, Kl = sxx("Kh", [P, L], f32r), sxx("Kl", [P, L], f32r)
        KA = sxx("KA", [P, 3, L], f32r)
        KB = sxx("KB", [P, 3, L], f32r)
        Qh, Ql = sxx("Qh", [P, T], f32r), sxx("Ql", [P, T], f32r)
        QA = sxx("QA", [P, 3, T], f32r)
        QB = sxx("QB", [P, 3, T], f32r)
        bo_t = sxx("bo_t", [P, D])
        x1_h, x1_l = sxx("x1_h", [P, KC, T], f32r), sxx("x1_l", [P, KC, T], f32r)
        mxp = sxx("mxp", [P, 2, NT, NB])
        mx = sxx("mx", [P, 2, NT])
        mrow = sxx("mrow", [NT, 2, P], f32r)
        O_h, O_l = sxx("O_h", [P, T], f32r), sxx("O_l", [P, T], f32r)
        xs_.close()
        both.close()

        fs = ExitStack()
        sf = stage_buffers(fs)
        x2_h, x2_l = sf("x2_h", [P, KC, B * T], f32r), sf("x2_l", [P, KC, B * T], f32r)
        G_raw = sf("G_raw", [P, KC, P])
        G_h, G_l = sf("G_h", [P, KC, P], f32r), sf("G_l", [P, KC, P], f32r)
        sT = sf("sT", [E, B * T])
        S8 = sf("S8", [P, B * NT, E])
        cmp = sf("cmp", [P, B * NT, E, E])
        cmp2 = sf("cmp2", [P, B * NT, E, E])
        lower = sf("lower", [P, E, E])
        rank = sf("rank", [P, B * NT, E])
        chosen = sf("chosen", [P, B * NT, E])
        smax = sf("smax", [P, B * NT])
        sh = sf("sh", [P, B * NT, E])
        ex = sf("ex", [P, B * NT, E])
        exs = sf("exs", [P, B * NT, E])
        wsum = sf("wsum", [P, B * NT])
        wrec = sf("wrec", [P, B * NT])
        WG = sf("WG", [P, B * NT, E])
        wcol = sf("wcol", [P, 2, B * NT])
        W_raw = sf("W_raw", [P, 3, 1024])
        W_h, W_l = sf("W_h", [P, 2, 3, 1024], f32r), sf("W_l", [P, 2, 3, 1024], f32r)
        gl = sf("gl", [P, 2, T])
        hm = sf("hm", [P, 2, T])
        h_h, h_l = sf("h_h", [P, 2, FC, T], f32r), sf("h_l", [P, 2, FC, T], f32r)
        fs.close()

        def bank(k, n=512, rows=P):
            return PS[0:rows, k, 0:n]

        def as32(ap):
            return ap.bitcast(f32)

        def hold(eng, s, value):
            eng.wait_ge(s, value)
            eng.nop(nofuse=True)

        def split3(pe, o, lh, ll, rh, rl, first, last):
            pe.matmul(o, lh, rh, start=first, stop=False)
            pe.matmul(o, lh, rl, start=False, stop=False)
            return pe.matmul(o, ll, rh, start=False, stop=last)

        ld_w = sem("ld_w")
        ld_w2 = sem("ld_w2")
        ld_x = sem("ld_x")
        ld_xt = sem("ld_xt")
        const_pool = sem("const_pool")
        const_dve = sem("const_dve")
        w_hi = sem("w_hi")
        w_lo = sem("w_lo")
        xt_hi, xt_lo = sem("xt_hi"), sem("xt_lo")
        qk_mm, v_mm = sem("qk_mm"), sem("v_mm")
        v_out, vs_ok = sem("v_out"), sem("vs_ok")
        fch = sem("fch")
        nch = sem("nch")
        lch = sem("lch")
        cen_ok, sq_ok, var_ok, sd_ok, fn_ok, nrm_ok, gm_ok, feat_ok = (sem(n) for n in (
            "cen_ok", "sq_ok", "var_ok", "sd_ok", "fn_ok", "nrm_ok", "gm_ok", "feat_ok"))
        hi_ok, lo_ok = sem("hi_ok"), sem("lo_ok")
        tq_mm, tk_mm, qT_ok, kT_ok = sem("tq_mm"), sem("tk_mm"), sem("qT_ok"), sem("kT_ok")
        sc_mm, sqr_ok, mask_ok, av_mm = sem("sc_mm"), sem("sqr_ok"), sem("mask_ok"), sem("av_mm")
        osb_ok, ot_mm, y_ok, yt_mm, yh_ok, yl_ok = (sem(n) for n in (
            "osb_ok", "ot_mm", "y_ok", "yt_mm", "yh_ok", "yl_ok"))
        o_mm, res_ok = sem("o_mm"), sem("res_ok")
        lnv_ok, lnr_ok, x1_ok = sem("lnv_ok"), sem("lnr_ok"), sem("x1_ok")

        ld_bo = sem("ld_bo")
        xconst = sem("xconst")
        ld_c = [sem(f"ld_c{k}") for k in range(2)]
        ld_h = [sem(f"ld_h{k}") for k in range(3)]
        ld_m = sem("ld_m")
        c_hi, c_lo = sem("c_hi"), sem("c_lo")
        xs_ok, xb_ok = sem("xs_ok"), sem("xb_ok")
        misc_mm, misc_hi, misc_ok = sem("misc_mm"), sem("misc_hi"), sem("misc_ok")
        mx_mm, mx_ok, hmax_ok = sem("mx_mm"), sem("mx_ok"), sem("hmax_ok")
        st_mm, exp_ok, pv_mm = sem("st_mm"), sem("exp_ok"), sem("pv_mm")
        rec_ok, head_ok, oh_ok, ol_ok = sem("rec_ok"), sem("head_ok"), sem("oh_ok"), sem("ol_ok")
        xln_ch, xlnv_ok, xlnr_ok, x2_ok = sem("xln_ch"), sem("xlnv_ok"), sem("xlnr_ok"), sem("x2_ok")

        ld_g, gz_ok, gate_hi, gate_lo, low_ok = (sem(n) for n in ("ld_g", "gz_ok", "gate_hi", "gate_lo", "low_ok"))
        ft_mm, ft_hi, ft_ok = sem("ft_mm"), sem("ft_hi"), sem("ft_ok")
        gs_mm, gs_ok, gt_mm, route, rt_sh, rt_ex = (sem(n) for n in ("gs_mm", "gs_ok", "gt_mm", "route", "rt_sh", "rt_ex"))
        ld_e, we_hi, we_lo = sem("ld_e"), sem("we_hi"), sem("we_lo")
        h1_mm, h3_mm, silu_ok, hm_ok, hh_ok, hl_ok = (sem(n) for n in (
            "h1_mm", "h3_mm", "silu_ok", "hm_ok", "hh_ok", "hl_ok"))
        dn_mm, acc_ok, wcol_ok = sem("dn_mm"), sem("acc_ok"), sem("wcol_ok")
        fln_ch, flnv_ok, flnr_ok, x3_ok, st_out = (sem(n) for n in ("fln_ch", "flnv_ok", "flnr_ok", "x3_ok", "st_out"))
        UNITS = B * FC

        def beside(h, j):
            steps = []
            if 2 <= j < 10 and h + 1 < XH:
                steps += [("max", h + 1, 2 * j - 4), ("max", h + 1, 2 * j - 3)]
            if j == 10 and h + 1 < XH:
                steps += [("mrow", h + 1)]
            if h % 2 == 0 and h + 2 < XH and 1 <= j <= 4:
                steps += [("k", h // 2 + 1, j - 1)]
            if h % 2 == 0 and h + 2 < XH and j == 5:
                steps += [("q", h // 2 + 1)]
            if h % 2 == 0 and h >= 2 and j == 6:
                steps += [("osplit", h // 2 - 1)]
            if h % 2 == 0 and h >= 2 and j in (8, 9, 11, 12):
                steps += [("wo", h // 2 - 1, (8, 9, 11, 12).index(j))]
            return steps

        PROLOGUE = [("xt", c) for c in range(KC)] + [("q", 0)] + [("k", 0, k) for k in range(NB)] \
            + [("v", j) for j in range(NL)] + [("max", 0, v) for v in range(NT * NB)] + [("mrow", 0)]
        EPILOGUE = [("osplit", PAIRS - 1)] + [("wo", PAIRS - 1, i) for i in range(NT)]
        ALL = PROLOGUE + [s for h in range(XH) for j in range(NL) for s in beside(h, j)] + EPILOGUE
        MISC = {s: n for n, s in enumerate(s for s in ALL if s[0] not in ("max", "osplit"))}
        HIGH = {s: n for n, s in enumerate(s for s in MISC if s[0] in ("xt", "q", "k"))}
        NM, NH = len(MISC), len(HIGH)
        SLOT_LOADS = [len(range(k, XH, 3)) for k in range(3)]
        NMX = NT * NB

        def loaded(b, h):
            return 16 * 6 * (SLOT_LOADS[h % 3] * b + h // 3 + 1)

        def v_ones(j, h):
            return VX[0:LROWS[j], j, h // 2, XD * (h % 2):XD * (h % 2) + 2 * XD]

        block = ctx.enter_context(nc.Block())

        FCH = 7

        @block.sync
        def _(sp):
            sp.dma_start(xt_raw[:, :, :], xt[0].rearrange("(c p) t -> p c t", p=P)).then_inc(ld_xt, 16)
            sp.dma_start(raw[:, 0:2, 0:3 * D], wqkv.rearrange("(c p) n -> p c n", p=P)).then_inc(ld_w, 16)
            sp.dma_start(raw[:, 0:2, 3 * D:4 * D], wo_s.rearrange("(c p) n -> p c n", p=P)).then_inc(ld_w, 16)
            sp.dma_start(gam[:, :], gamma.partition_broadcast(P)).then_inc(ld_w, 16)
            sp.dma_start(bet[:, :], beta.partition_broadcast(P)).then_inc(ld_w, 16)
            sp.dma_start(X[:, :, :], x.rearrange("b (i p) d -> p (b i) d", p=P)).then_inc(ld_x, 16)
            sp.dma_start(raw[:, 2, :].rearrange("p (c n) -> p c n", c=KC),
                         wq.rearrange("(c p) n -> p c n", p=P)).then_inc(ld_w2, 16)
            sp.dma_start(raw[:, 3, :].rearrange("p (c n) -> p c n", c=PAIRS),
                         wo_x.rearrange("(c p) n -> p c n", p=P)).then_inc(ld_w2, 16)
            sp.wait_ge(w_lo, 1)
            for k, w in ((0, wk), (1, wv)):
                sp.dma_start(raw[:, k, 0:INNER], w[0:P, :]).then_inc(ld_w2, 16)
                for half in range(2):
                    sp.dma_start(raw[64 * half:64 * half + 64, k, INNER:], w[P:C, :]).then_inc(ld_w2, 16)
            with sp.Fori(1, B) as b:
                hold(sp, xt_lo, b)
                sp.dma_start(xt_raw[:, :, :], xt[bass.ds(b, 1)].rearrange("o (c p) t -> p (o c) t", p=P)).then_inc(ld_xt, 16)
            sp.wait_ge(x1_ok, NT * B)
            sp.wait_ge(w_lo, 5)
            sp.dma_start(bo_t[:, :], bo.partition_broadcast(P)).then_inc(ld_bo, 16)

            def head_in(b, h):
                s, half = h % 3, slice(64 * (h % 2), 64 * (h % 2) + 64)
                hold(sp, misc_ok, NM * b + MISC[("q", h // 2)] + 1)
                hold(sp, misc_ok, NM * b + MISC[("k", h // 2, NB - 1)] + 1)
                if h >= 3:
                    hold(sp, st_mm, NL * XH * b + NL * (h - 2))
                for dst, src in ((QA[0:64, s, :], Qh), (QA[64:P, s, :], Ql), (QB[0:64, s, :], Qh),
                                 (KA[0:64, s, :], Kh), (KA[64:P, s, :], Kh), (KB[0:64, s, :], Kl)):
                    sp.dma_start(as32(dst), as32(src[half, :])).then_inc(ld_h[s], 16)

            def maxima_in(b, h):
                hold(sp, misc_ok, NM * b + MISC[("mrow", h)] + 1)
                for i in range(NT):
                    sp.dma_start(as32(QB[64:65, h % 3, P * i:P * i + P]), as32(mrow[i:i + 1, h % 2, :])).then_inc(ld_m, 16)

            sp.wait_ge(xconst, 4)
            with sp.Fori(0, B) as b:
                hold(sp, x2_ok, NT * b + 1)
                for k in range(NB):
                    if k >= 2:
                        hold(sp, c_lo, 8 * b + 2 * (k - 1))
                    n = BEDGE[k + 1] - BEDGE[k]
                    cols = slice(BEDGE[k], BEDGE[k + 1])
                    cb = ctxt[bass.ds(b, 1)].rearrange("o c l -> (o c) l")
                    sp.dma_start(c_raw[:, k % 2, 0, 0:n], cb[0:P, cols]).then_inc(ld_c[k % 2], 16)
                    for half in range(2):
                        sp.dma_start(c_raw[64 * half:64 * half + 64, k % 2, 1, 0:n], cb[P:C, cols])\
                            .then_inc(ld_c[k % 2], 16)
                head_in(b, 0)
                head_in(b, 1)
                maxima_in(b, 0)
                for h in range(0, XH, 2):
                    if h + 2 < XH:
                        head_in(b, h + 2)
                    maxima_in(b, h + 1)
                    if h + 3 < XH:
                        head_in(b, h + 3)
                        maxima_in(b, h + 2)
            sp.wait_ge(x2_ok, NT * B + 1)
            sp.wait_ge(gz_ok, 1)
            sp.dma_start(G_raw[:, :, 0:E], gate.rearrange("(c p) e -> p c e", p=P)).then_inc(ld_g, 16)

            def load_expert(e):
                for k, w in enumerate((w1, w3, w2)):
                    src = w[bass.ds(e, 1)].rearrange("o (c p) n -> p (o c) n", p=P)
                    sp.dma_start(W_raw[:, k, :].rearrange("p (c n) -> p c n", c=src.shape[1]), src).then_inc(ld_e, 16)

            load_expert(0)
            with sp.Fori(1, E) as e:
                hold(sp, we_lo, 3 * e)
                load_expert(e)
            for tb in range(B):
                sp.wait_ge(x3_ok, NT * (tb + 1))
                sp.dma_start(out[tb].rearrange("(i p) d -> p i d", p=P), X[:, NT * tb:NT * tb + NT, :]).then_inc(st_out, 16)
            sp.wait_ge(st_out, 16 * B)

        N_LDW = 4

        @block.gpsimd
        def _(pool):
            pool.memset(ident[:, :], 0.0).then_inc(const_pool, 1)
            pool.memset(neg_half[:, :], -0.5).then_inc(const_pool, 1)
            pool.wait_ge(const_pool, 2)
            pool.affine_select(out=ident[:, :], in_=ident[:, :], compare_op=ALU.not_equal, fill=1.0,
                               base=0, pattern=[[-1, P]], channel_multiplier=1).then_inc(const_pool, 1)
            pool.wait_ge(ld_w, 16 * N_LDW)

            def affine(t, i):
                pool.wait_ge(nrm_ok, NT * t + i + 1)
                v = cen[:, i % 2, :].rearrange("p (g f) -> p g f", f=SF)
                w = feat[:, i, :].rearrange("p (g f) -> p g f", f=SF)
                pool.tensor_tensor(v, v, gam[:, :].unsqueeze(1).broadcast_to([P, 32, SF]), ALU.mult).then_inc(gm_ok, 1)
                pool.wait_ge(gm_ok, NT * t + i + 1)
                pool.tensor_tensor(w, v, bet[:, :].unsqueeze(1).broadcast_to([P, 32, SF]), ALU.add)\
                    .then_inc(feat_ok, 1)

            def attention(b, more):
                for g in range(QUADS):
                    for n in range(16 * g, 16 * g + 16):
                        c = (n // 4) % NT
                        hold(pool, sqr_ok, 64 * b + n + 1)
                        blk = A[:, n % 8, P * c:P * c + P]
                        pool.affine_select(out=blk, in_=blk, compare_op=ALU.is_ge, fill=0.0, base=0,
                                           pattern=[[1, P]], channel_multiplier=-1).then_inc(mask_ok, 1)
                    if more and g >= 1:
                        affine(b + 1, g - 1)
                if more:
                    affine(b + 1, NT - 1)
                pool.wait_ge(lnv_ok, b + 1)
                pool.tensor_tensor(ln_rs[:, :], ln_ve[:, :], neg_half[:, 0:NT], ALU.pow).then_inc(lnr_ok, 1)

            for i in range(NT):
                affine(0, i)
            with pool.Fori(0, B - 1) as b:
                attention(b, True)
            attention(B - 1, False)
            pool.wait_ge(x1_ok, NT * B)
            pool.wait_ge(w_lo, 5)
            pool.memset(as32(KB[64:P, :, :]), 0.0).then_inc(xconst, 1)
            pool.wait_ge(xconst, 1)
            pool.memset(as32(QB[64:P, :, :]), 0.0).then_inc(xconst, 1)
            pool.wait_ge(xconst, 2)
            pool.memset(VX[:, :, :, XD:2 * XD], 1.0).then_inc(xconst, 1)
            pool.wait_ge(xconst, 3)
            pool.memset(as32(KB[64:65, :, :]), 1.0).then_inc(xconst, 1)
            with pool.Fori(0, B) as b:
                pool.wait_ge(xlnv_ok, b + 1)
                pool.tensor_tensor(ln_rs[:, :], ln_ve[:, :], neg_half[:, 0:NT], ALU.pow).then_inc(xlnr_ok, 1)
            pool.wait_ge(x2_ok, NT * B + 1)
            pool.memset(lower[:, :, :], 1.0).then_inc(low_ok, 1)
            pool.wait_ge(low_ok, 1)
            pool.affine_select(out=lower[:, :, :], in_=lower[:, :, :], compare_op=ALU.is_gt, fill=0.0, base=0,
                               pattern=[[1, E], [-1, E]], channel_multiplier=0).then_inc(low_ok, 1)

            def split_expert(e, k):
                for m in range(3):
                    pool.wait_ge(we_hi, 3 * e + m + 1)
                    pool.tensor_tensor(W_l[:, k, m, :], W_raw[:, m, :], as32(W_h[:, k, m, :]), ALU.subtract)\
                        .then_inc(we_lo, 1)

            with pool.Fori(0, E // 2) as ee:
                split_expert(2 * ee, 0)
                split_expert(2 * ee + 1, 1)
            for tb in range(B):
                pool.wait_ge(flnv_ok, tb + 1)
                pool.tensor_tensor(ln_rs[:, :], ln_ve[:, :], neg_half[:, 0:NT], ALU.pow).then_inc(flnr_ok, 1)

        @block.scalar
        def _(act):
            act.wait_ge(ld_w, 16 * N_LDW)
            act.copy(WSh[:, :, :], raw[:, 0:2, :]).then_inc(w_hi, 1)

            def x_high(t):
                act.wait_ge(ld_xt, 16 * t + 16)
                act.copy(xt_h[:, :, :], xt_raw[:, :, :]).then_inc(xt_hi, 1)

            def squares(t, i, wait):
                act.wait_ge(v_mm, NT * t + i + 1)
                if wait:
                    act.wait_ge(vs_ok, t)
                    act.wait_ge(lo_ok, 8 * t)
                act.copy(Vn[:, i, :], bank(3, D)).then_inc(v_out, 1)
                act.wait_ge(cen_ok, NT * t + i + 1)
                act.activation(feat[:, i, :], cen[:, i % 2, :], ACT.Square).then_inc(sq_ok, 1)

            def deviation(t, i):
                act.wait_ge(var_ok, NT * t + i + 1)
                act.activation(g_sd[:, i % 2, :], g_var[:, i % 2, :], ACT.Sqrt).then_inc(sd_ok, 1)

            def high(t, i):
                act.wait_ge(feat_ok, NT * t + i + 1)
                f = feat[:, i, :].rearrange("p (s h f) -> p s h f", s=2, f=SF)
                act.copy(QX[:, i, :, 0:2, :], f[:, 0].unsqueeze(2).broadcast_to([P, SH, 2, SF])).then_inc(hi_ok, 1)
                act.copy(KX[:, i, :, 0:4:2, :], f[:, 1].unsqueeze(2).broadcast_to([P, SH, 2, SF])).then_inc(hi_ok, 1)

            def values_in(t):
                act.wait_ge(v_out, NT * t + NT)
                act.copy(VS[:, :, :, 0:SF], Vn[:, :, :].rearrange("p i (h f) -> p i h f", f=SF)).then_inc(vs_ok, 1)

            def turn(b, g):
                for q in range(2):
                    act.wait_ge(tq_mm, 8 * b + 2 * g + q + 1)
                    act.copy(qT[:, g % 2, q, :], bank(0)).then_inc(qT_ok, 1)

            def attention(b, more):
                if more:
                    x_high(b + 1)
                turn(b, 0)
                for g in range(QUADS):
                    for c in range(NT):
                        for j in range(4):
                            n = 16 * g + 4 * c + j
                            act.wait_ge(sc_mm, 64 * b + n + 1)
                            if n >= 8:
                                act.wait_ge(av_mm, 16 * b + (n - 8) // 4 + 1)
                            act.activation(A[:, n % 8, P * c:T], PS[:, 4 + n % 2, P * c:T], ACT.Square,
                                           scale=0.25).then_inc(sqr_ok, 1)
                        if c == 0 and g + 1 < QUADS:
                            turn(b, g + 1)
                        if more and c == 1 and g >= 1:
                            deviation(b + 1, g - 1)
                        if more and c == 2 and g == QUADS - 1:
                            act.wait_ge(tk_mm, 8 * b + 8)
                            high(b + 1, 0)
                            high(b + 1, 1)
                    if more:
                        squares(b + 1, g, True)
                if more:
                    deviation(b + 1, NT - 1)
                    act.wait_ge(av_mm, 16 * b + 16)
                    values_in(b + 1)
                    high(b + 1, 2)
                    high(b + 1, 3)
                for c in range(KC):
                    act.wait_ge(yt_mm, KC * b + c + 1)
                    act.copy(y_h[:, c, :], bank(c)).then_inc(yh_ok, 1)

            x_high(0)
            for i in range(NT):
                squares(0, i, False)
                deviation(0, i)
            for i in range(NT):
                high(0, i)
            values_in(0)
            with act.Fori(0, B - 1) as b:
                attention(b, True)
            attention(B - 1, False)
            act.wait_ge(ld_w2, 16 * 8)
            for dst, k in ((WKh, 0), (WVh, 1), (WQh, 2)):
                act.copy(dst[:, :, :], raw[:, k, :].rearrange("p (c n) -> p c n", c=2)).then_inc(w_hi, 1)
            act.copy(WOh[:, :, :], raw[:, 3, :].rearrange("p (c n) -> p c n", c=PAIRS)).then_inc(w_hi, 1)

            def high(b, s):
                kind, bk = s[0], bank(6 + MISC[s] % 2)
                act.wait_ge(misc_mm, NM * b + MISC[s] + 1)
                if kind == "xt":
                    ins = act.copy(x1_h[:, s[1], :], bk)
                if kind == "q":
                    if s[1] >= 1:
                        act.wait_ge(ld_h[(2 * s[1] - 2) % 3], loaded(b, 2 * s[1] - 2))
                        act.wait_ge(ld_h[(2 * s[1] - 1) % 3], loaded(b, 2 * s[1] - 1))
                    ins = act.copy(Qh[:, :], bk)
                if kind == "k":
                    lo, hi = BEDGE[s[2]], BEDGE[s[2] + 1]
                    if s[1] >= 1:
                        act.wait_ge(ld_h[(2 * s[1] - 2) % 3], loaded(b, 2 * s[1] - 2))
                        act.wait_ge(ld_h[(2 * s[1] - 1) % 3], loaded(b, 2 * s[1] - 1))
                    ins = act.copy(Kh[:, lo:hi], bk[:, lo - BSTART[s[2]]:hi - BSTART[s[2]]])
                ins.then_inc(misc_hi, 1)

            def split_out(b, p):
                act.wait_ge(head_ok, XH * b + 2 * p + 2)
                if p >= 1:
                    act.wait_ge(misc_mm, NM * b + MISC[("wo", p - 1, NT - 1)] + 1)
                act.copy(O_h[:, :], O[:, :]).then_inc(oh_ok, 1)

            with act.Fori(0, B) as b:
                for k in range(NB):
                    n, lo, hi = BEDGE[k + 1] - BEDGE[k], BEDGE[k], BEDGE[k + 1]
                    act.wait_ge(ld_c[k % 2], 48 * (2 * b + k // 2 + 1))
                    act.copy(Ch[:, lo:hi], c_raw[:, k % 2, 0, 0:n]).then_inc(c_hi, 1)
                    act.copy(Cc[0:64, lo:hi], c_raw[0:64, k % 2, 1, 0:n]).then_inc(c_hi, 1)
                    if k >= 1:
                        act.wait_ge(c_lo, 8 * b + 2 * k)
                    act.copy(c_tmp[64:P, 0:n], c_raw[64:P, k % 2, 1, 0:n]).then_inc(c_hi, 1)
                for s in PROLOGUE:
                    if s in HIGH:
                        high(b, s)
                for h in range(XH):
                    for j in range(NL):
                        u = NL * h + j
                        act.wait_ge(st_mm, NL * XH * b + u + 1)
                        if u >= NP:
                            act.wait_ge(pv_mm, NL * XH * b + u - NP + 1)
                        r = LROWS[j]
                        act.activation(PX[0:r, u % NP, :], bank(u % 2, rows=r), ACT.Exp, scale=XD ** -0.5)\
                            .then_inc(exp_ok, 1)
                        for s in beside(h, j):
                            if s in HIGH:
                                high(b, s)
                            if s[0] == "osplit":
                                split_out(b, s[1])
                split_out(b, PAIRS - 1)

            act.wait_ge(ld_g, 16)
            act.copy(G_h[:, :, :], G_raw[:, :, :]).then_inc(gate_hi, 1)

            def split_expert(e, k, again):
                if again:
                    act.wait_ge(dn_mm, 4 * B * (e - 1))
                for m in range(3):
                    act.wait_ge(ld_e, 48 * e + 48)
                    act.copy(W_h[:, k, m, :], W_raw[:, m, :]).then_inc(we_hi, 1)

            split_expert(0, 0, False)
            for n in range(B * KC):
                act.wait_ge(ft_mm, n + 1)
                act.copy(x2_h[:, n % KC, T * (n // KC):T * (n // KC + 1)], bank(n % 2)).then_inc(ft_hi, 1)
            for tb in range(B):
                act.wait_ge(gs_mm, tb + 1)
                act.copy(sT[:, T * tb:T * tb + T], bank(2 + tb % 2, rows=E)).then_inc(gs_ok, 1)
            act.wait_ge(rt_sh, 1)
            act.activation(ex[:, :, :], sh[:, :, :], ACT.Exp).then_inc(rt_ex, 1)

            def hidden(u, n):
                act.wait_ge(h1_mm, u + 1)
                if n >= 2:
                    act.wait_ge(hm_ok, u - 1)
                act.activation(gl[:, n % 2, :], bank(n % 2), ACT.Silu).then_inc(silu_ok, 1)

            def hidden_hi(u, n, g, later):
                act.wait_ge(hm_ok, u + 1)
                if later:
                    act.wait_ge(dn_mm, 4 * (g - 1))
                act.copy(h_h[:, (n // FC) % 2, n % FC, :], hm[:, n % 2, :]).then_inc(hh_ok, 1)

            def two_experts(ee, first, last):
                for n in range(2 * UNITS):
                    u, g = 2 * UNITS * ee + n, 2 * B * ee + n // FC
                    hidden(u, n)
                    if n >= 1:
                        hidden_hi(u - 1, n - 1, 2 * B * ee + (n - 1) // FC, not first or (n - 1) // FC >= 2)
                    if n == 2 * FC:
                        split_expert(2 * ee + 1, 1, not first)
                    if n == UNITS + 2 * FC and not last:
                        split_expert(2 * ee + 2, 0, True)
                n = 2 * UNITS - 1
                hidden_hi(2 * UNITS * ee + n, n, 2 * B * ee + n // FC, True)

            two_experts(0, True, False)
            with act.Fori(1, E // 2 - 1) as ee:
                two_experts(ee, False, False)
            two_experts(E // 2 - 1, False, True)

        @block.vector
        def _(dve):
            dve.memset(VS[:, :, :, SF:], 1.0).then_inc(const_dve, 1)
            dve.memset(as32(kT[64:P, :, 0:4:2, :]), 0.0).then_inc(const_dve, 1)
            dve.memset(as32(kT[0:64, :, 1:4:2, :]), 0.0).then_inc(const_dve, 1)
            dve.wait_ge(ld_w, 16 * N_LDW)
            dve.wait_ge(w_hi, 1)
            dve.tensor_tensor(WSl[:, :, :], raw[:, 0:2, :], as32(WSh[:, :, :]), ALU.subtract).then_inc(w_lo, 1)

            def x_low(t):
                dve.wait_ge(xt_hi, t + 1)
                dve.tensor_tensor(xt_l[:, :, :], xt_raw[:, :, :], as32(xt_h[:, :, :]), ALU.subtract).then_inc(xt_lo, 1)

            def chain(ins, s, value):
                ins.then_inc(s, 1)
                dve.wait_ge(s, value)

            def centre(t, i, wait):
                at = FCH * (NT * t + i)
                v = bank(2).rearrange("p (g f) -> p g f", f=SF)
                dve.wait_ge(qk_mm, NT * t + i + 1)
                chain(dve.tensor_reduce(g_mean[:, i % 2, :], v, AX, ALU.add), fch, at + 1)
                chain(dve.tensor_scalar(g_mean[:, i % 2, :], g_mean[:, i % 2, :], -1.0 / SF, None, ALU.mult), fch, at + 2)
                if wait:
                    dve.wait_ge(feat_ok, NT * t + i - 1)
                dve.tensor_tensor(cen[:, i % 2, :].rearrange("p (g f) -> p g f", f=SF), v,
                                  g_mean[:, i % 2, :].unsqueeze(2).broadcast_to([P, 32, SF]), ALU.add).then_inc(cen_ok, 1)

            def variance(t, i):
                at = FCH * (NT * t + i)
                dve.wait_ge(sq_ok, NT * t + i + 1)
                chain(dve.tensor_reduce(g_var[:, i % 2, :], feat[:, i, :].rearrange("p (g f) -> p g f", f=SF), AX, ALU.add),
                      fch, at + 3)
                dve.tensor_scalar(g_var[:, i % 2, :], g_var[:, i % 2, :], 1.0 / SF, LN_EPS, ALU.mult, ALU.add)\
                    .then_inc(var_ok, 1)

            def normalise(t, i):
                at = FCH * (NT * t + i)
                rs, tt = g_rs[:, i % 2, :], g_t[:, i % 2, :]
                dve.wait_ge(sd_ok, NT * t + i + 1)
                chain(dve.reciprocal(rs, g_sd[:, i % 2, :]), fch, at + 4)
                chain(dve.tensor_tensor(tt, rs, rs, ALU.mult), fch, at + 5)
                chain(dve.tensor_tensor(tt, tt, g_var[:, i % 2, :], ALU.mult), fch, at + 6)
                chain(dve.tensor_scalar(tt, tt, -0.5, 1.5, ALU.mult, ALU.add), fch, at + 7)
                dve.tensor_tensor(rs, rs, tt, ALU.mult).then_inc(fn_ok, 1)
                dve.wait_ge(fn_ok, NT * t + i + 1)
                v = cen[:, i % 2, :].rearrange("p (g f) -> p g f", f=SF)
                dve.tensor_tensor(v, v, rs.unsqueeze(2).broadcast_to([P, 32, SF]), ALU.mult).then_inc(nrm_ok, 1)

            def low(t, i):
                f = feat[:, i, :].rearrange("p (s h f) -> p s h f", s=2, f=SF)
                dve.wait_ge(hi_ok, 8 * t + 2 * i + 1)
                dve.tensor_tensor(QX[:, i, :, 2:4, :], f[:, 0].unsqueeze(2).broadcast_to([P, SH, 2, SF]),
                                  as32(QX[:, i, :, 0:2, :]), ALU.subtract).then_inc(lo_ok, 1)
                dve.wait_ge(hi_ok, 8 * t + 2 * i + 2)
                dve.tensor_tensor(KX[:, i, :, 1:4:2, :], f[:, 1].unsqueeze(2).broadcast_to([P, SH, 2, SF]),
                                  as32(KX[:, i, :, 0:4:2, :]), ALU.subtract).then_inc(lo_ok, 1)

            def turn(b, g):
                for q in range(2):
                    dve.wait_ge(tk_mm, 8 * b + 2 * g + q + 1)
                    dve.tensor_copy(kT[0:64, g % 2, 2 * q, :], bank(1, rows=64)).then_inc(kT_ok, 1)
                    dve.tensor_copy(kT[64:P, g % 2, 2 * q + 1, :], PS[64:P, 1, :]).then_inc(kT_ok, 1)

            def quad_out(b, g):
                dve.wait_ge(av_mm, 16 * b + 4 * g + 4)
                if g >= 2:
                    dve.wait_ge(ot_mm, QUADS * b + g - 1)
                dve.tensor_copy(osb[:, g % 2, :], bank(6)).then_inc(osb_ok, 1)

            def quad_norm(b, g):
                dve.wait_ge(ot_mm, QUADS * b + g + 1)
                at = 2 * (QUADS * b + g)
                o = bank(7).rearrange("p (i j f) -> p i j f", i=NT, j=4)
                chain(dve.tensor_scalar(den[:, :].rearrange("p (i j) -> p i j", j=4), o[:, :, :, SF], DEN_EPS, None,
                                        ALU.add), nch, at + 1)
                chain(dve.reciprocal(rden[:, :], den[:, :]), nch, at + 2)
                dve.tensor_tensor(y[:, :, 4 * SF * g:4 * SF * g + 4 * SF].rearrange("p i (j f) -> p i j f", f=SF),
                                  o[:, :, :, 0:SF],
                                  rden[:, :].rearrange("p (i j) -> p i j", j=4).unsqueeze(3)
                                  .broadcast_to([P, NT, 4, SF]), ALU.mult).then_inc(y_ok, 1)

            def attention(b, more):
                if more:
                    x_low(b + 1)
                turn(b, 0)
                for g in range(QUADS):
                    if g + 1 < QUADS:
                        turn(b, g + 1)
                    if more and g >= 1:
                        variance(b + 1, g - 1)
                    if g >= 1:
                        quad_norm(b, g - 1)
                    if more and g >= 1:
                        normalise(b + 1, g - 1)
                    if more:
                        centre(b + 1, g, True)
                        if g == QUADS - 1:
                            low(b + 1, 0)
                            low(b + 1, 1)
                    quad_out(b, g)
                if more:
                    variance(b + 1, NT - 1)
                quad_norm(b, QUADS - 1)
                if more:
                    normalise(b + 1, NT - 1)
                    low(b + 1, 2)
                    low(b + 1, 3)
                for c in range(KC):
                    dve.wait_ge(yh_ok, KC * b + c + 1)
                    dve.tensor_tensor(y_l[:, c, :], bank(c), as32(y_h[:, c, :]), ALU.subtract).then_inc(yl_ok, 1)
                for i in range(NT):
                    xi = X[:, bass.ds(NT * b + i, 1), :].rearrange("p o d -> p (o d)")
                    dve.wait_ge(o_mm, NT * b + i + 1)
                    dve.tensor_tensor(xi, bank(6 + i % 2, D), xi, ALU.add).then_inc(res_ok, 1)
                for i in range(NT):
                    xi = X[:, bass.ds(NT * b + i, 1), :].rearrange("p o d -> p (o d)")
                    hold(dve, res_ok, NT * b + i + 1)
                    ins = dve.bn_stats(ln_st[:, i, :], xi)
                chain(ins, lch, 2 * b + 1)
                dve.nop(nofuse=True)
                for i in range(NT):
                    ins = dve.bn_aggr(ln_mv[:, i, :], ln_st[:, i, :])
                chain(ins, lch, 2 * b + 2)
                dve.tensor_scalar(ln_ve[:, :], ln_mv[:, :, 1], LN_EPS, None, ALU.add).then_inc(lnv_ok, 1)
                dve.wait_ge(lnr_ok, b + 1)
                for i in range(NT):
                    xi = X[:, bass.ds(NT * b + i, 1), :].rearrange("p o d -> p (o d)")
                    dve.tensor_scalar(xi, xi, ln_mv[:, i, 0:1], ln_rs[:, i:i + 1], ALU.subtract, ALU.mult)\
                        .then_inc(x1_ok, 1)

            x_low(0)
            for i in range(NT):
                centre(0, i, i >= 2)
                variance(0, i)
                normalise(0, i)
            for i in range(NT):
                low(0, i)
            dve.wait_ge(ld_x, 16)
            with dve.Fori(0, B - 1) as b:
                attention(b, True)
            attention(B - 1, False)

            for n, (dst, high, k) in enumerate(((WKl, WKh, 0), (WVl, WVh, 1), (WQl, WQh, 2), (WOl, WOh, 3))):
                c = PAIRS if k == 3 else 2
                dve.wait_ge(w_hi, n + 2)
                dve.tensor_tensor(dst[:, :, :], raw[:, k, :].rearrange("p (c n) -> p c n", c=c), as32(high[:, :, :]),
                                  ALU.subtract).then_inc(w_lo, 1)
            dve.wait_ge(x1_ok, NT * B)
            dve.wait_ge(ld_bo, 16)
            dve.tensor_copy(ln_ve[:, :], ln_ve[:, :]).then_inc(x2_ok, 1)

            def step(b, s):
                kind = s[0]
                if kind == "max":
                    h, v = s[1], s[2]
                    n = NMX * h + v
                    dve.wait_ge(mx_mm, NMX * XH * b + n + 1)
                    if h >= 2 and v == 0:
                        dve.wait_ge(hmax_ok, XH * b + h - 1)
                    dve.tensor_reduce(mxp[:, h % 2, v // NB, v % NB:v % NB + 1], bank(2 + n % 2, BW), AX, ALU.max)\
                        .then_inc(mx_ok, 1)
                    if v == NMX - 1:
                        dve.wait_ge(mx_ok, NMX * XH * b + n + 1)
                        if h >= 2:
                            dve.wait_ge(misc_mm, NM * b + MISC[("mrow", h - 2)] + 1)
                        dve.tensor_reduce(mx[:, h % 2, :], mxp[:, h % 2, :, :], AX, ALU.max).then_inc(hmax_ok, 1)
                    return
                if kind == "osplit":
                    dve.wait_ge(oh_ok, PAIRS * b + s[1] + 1)
                    if s[1] >= 1:
                        dve.wait_ge(misc_mm, NM * b + MISC[("wo", s[1] - 1, NT - 1)] + 1)
                    dve.tensor_tensor(O_l[:, :], O[:, :], as32(O_h[:, :]), ALU.subtract).then_inc(ol_ok, 1)
                    return
                bk = bank(6 + MISC[s] % 2)
                if s in HIGH:
                    dve.wait_ge(misc_hi, NH * b + HIGH[s] + 1)
                else:
                    dve.wait_ge(misc_mm, NM * b + MISC[s] + 1)
                if kind == "xt":
                    ins = dve.tensor_tensor(x1_l[:, s[1], :], bk, as32(x1_h[:, s[1], :]), ALU.subtract)
                if kind == "q":
                    ins = dve.tensor_tensor(Ql[:, :], bk, as32(Qh[:, :]), ALU.subtract)
                if kind == "k":
                    lo, hi = BEDGE[s[2]], BEDGE[s[2] + 1]
                    ins = dve.tensor_tensor(Kl[:, lo:hi], bk[:, lo - BSTART[s[2]]:hi - BSTART[s[2]]],
                                            as32(Kh[:, lo:hi]), ALU.subtract)
                if kind == "v":
                    r = LROWS[s[1]]
                    dst = VX[0:r, s[1], :, :].rearrange("p q (three d) -> p q three d", d=XD)[:, :, 0:3:2, :]
                    ins = dve.tensor_copy(dst, bank(6 + MISC[s] % 2, rows=r).rearrange("p (q two d) -> p q two d",
                                                                                       two=2, d=XD))
                if kind == "mrow":
                    h = s[1]
                    if h >= 2:
                        dve.wait_ge(ld_m, 16 * NT * (XH * b + h - 1))
                    ins = dve.tensor_scalar(mrow[:, h % 2, :], bank(6 + MISC[s] % 2, P, NT), -1.0, None, ALU.mult)
                if kind == "wo":
                    xi = X[:, bass.ds(NT * b + s[2], 1), :].rearrange("p o d -> p (o d)")
                    if s[1] >= 1:
                        dve.wait_ge(misc_ok, NM * b + MISC[("wo", s[1] - 1, s[2])] + 1)
                    ins = dve.tensor_tensor(xi, bank(6 + MISC[s] % 2, D), xi, ALU.add)
                ins.then_inc(misc_ok, 1)

            def head_out(b, h):
                bk, p = 4 + h % 2, h // 2
                val = slice(64 * (h % 2), 64 * (h % 2) + 64)
                tot = slice(64 - 64 * (h % 2), 128 - 64 * (h % 2))
                dve.wait_ge(pv_mm, NL * (XH * b + h + 1))
                if h >= 2:
                    dve.wait_ge(head_ok, XH * b + h - 1)
                    dve.wait_ge(ol_ok, PAIRS * b + p)
                dve.reciprocal(R[val, :], PS[tot, bk, :]).then_inc(rec_ok, 1)
                dve.wait_ge(rec_ok, XH * b + h + 1)
                dve.tensor_tensor(O[val, :], PS[val, bk, :], R[val, :], ALU.mult).then_inc(head_ok, 1)

            with dve.Fori(0, B) as b:
                xb = X[:, bass.ds(NT * b, NT), :]
                dve.wait_ge(x2_ok, NT * b + 1)
                dve.tensor_copy(xs[:, :, :], xb).then_inc(xs_ok, 1)
                dve.wait_ge(xs_ok, b + 1)
                dve.tensor_tensor(xb, xb, bo_t[:, :].unsqueeze(1).broadcast_to([P, NT, D]), ALU.add).then_inc(xb_ok, 1)
                for k in range(NB):
                    n, lo, hi = BEDGE[k + 1] - BEDGE[k], BEDGE[k], BEDGE[k + 1]
                    dve.wait_ge(c_hi, 12 * b + 3 * k + 1)
                    dve.tensor_tensor(Cl[:, lo:hi], c_raw[:, k % 2, 0, 0:n], as32(Ch[:, lo:hi]), ALU.subtract)\
                        .then_inc(c_lo, 1)
                    dve.wait_ge(c_hi, 12 * b + 3 * k + 3)
                    dve.tensor_tensor(Cc[64:P, lo:hi], c_raw[64:P, k % 2, 1, 0:n], as32(c_tmp[64:P, 0:n]), ALU.subtract)\
                        .then_inc(c_lo, 1)
                dve.wait_ge(xb_ok, b + 1)
                for s in PROLOGUE:
                    step(b, s)
                for h in range(XH):
                    for j in range(NL):
                        for s in beside(h, j):
                            step(b, s)
                    head_out(b, h)
                for s in EPILOGUE:
                    step(b, s)
                for i in range(NT):
                    xi = X[:, bass.ds(NT * b + i, 1), :].rearrange("p o d -> p (o d)")
                    hold(dve, misc_ok, NM * b + MISC[("wo", PAIRS - 1, i)] + 1)
                    ins = dve.bn_stats(ln_st[:, i, :], xi)
                ins.then_inc(xln_ch, 1)
                hold(dve, xln_ch, 2 * b + 1)
                for i in range(NT):
                    ins = dve.bn_aggr(ln_mv[:, i, :], ln_st[:, i, :])
                ins.then_inc(xln_ch, 1)
                dve.wait_ge(xln_ch, 2 * b + 2)
                dve.tensor_scalar(ln_ve[:, :], ln_mv[:, :, 1], LN_EPS, None, ALU.add).then_inc(xlnv_ok, 1)
                dve.wait_ge(xlnr_ok, b + 1)
                for i in range(NT):
                    xi = X[:, bass.ds(NT * b + i, 1), :].rearrange("p o d -> p (o d)")
                    dve.tensor_scalar(xi, xi, ln_mv[:, i, 0:1], ln_rs[:, i:i + 1], ALU.subtract, ALU.mult)\
                        .then_inc(x2_ok, 1)

            dve.wait_ge(x2_ok, NT * B + 1)
            dve.memset(G_raw[:, :, :], 0.0).then_inc(gz_ok, 1)
            dve.wait_ge(gate_hi, 1)
            dve.tensor_tensor(G_l[:, :, :], G_raw[:, :, :], as32(G_h[:, :, :]), ALU.subtract).then_inc(gate_lo, 1)
            for n in range(B * KC):
                cols = slice(T * (n // KC), T * (n // KC + 1))
                dve.wait_ge(ft_hi, n + 1)
                dve.tensor_tensor(x2_l[:, n % KC, cols], bank(n % 2), as32(x2_h[:, n % KC, cols]), ALU.subtract)\
                    .then_inc(ft_ok, 1)
            routed = [0]

            def rt(ins):
                routed[0] += 1
                ins.then_inc(route, 1)
                dve.wait_ge(route, routed[0])

            NTT = B * NT
            dve.wait_ge(gt_mm, 1)
            rt(dve.tensor_copy(S8[:, :, :], bank(4, NTT * E).rearrange("p (t e) -> p t e", e=E)))
            rt(dve.tensor_reduce(smax[:, :], S8[:, :, :], AX, ALU.max))
            dve.tensor_tensor(sh[:, :, :], S8[:, :, :], smax[:, :].unsqueeze(2).broadcast_to([P, NTT, E]),
                              ALU.subtract).then_inc(rt_sh, 1)
            own = S8[:, :, :].unsqueeze(3).broadcast_to([P, NTT, E, E])
            other = S8[:, :, :].unsqueeze(2).broadcast_to([P, NTT, E, E])
            rt(dve.tensor_tensor(cmp[:, :, :, :], other, own, ALU.is_gt))
            rt(dve.tensor_tensor(cmp2[:, :, :, :], other, own, ALU.is_equal))
            dve.wait_ge(low_ok, 2)
            flat = "p t e f -> p t (e f)"
            low = lower[:, :, :].rearrange("p e f -> p (e f)").unsqueeze(1).broadcast_to([P, NTT, E * E])
            rt(dve.tensor_tensor(cmp2[:, :, :, :].rearrange(flat), cmp2[:, :, :, :].rearrange(flat), low, ALU.mult))
            rt(dve.tensor_tensor(cmp[:, :, :, :], cmp[:, :, :, :], cmp2[:, :, :, :], ALU.add))
            rt(dve.tensor_reduce(rank[:, :, :], cmp[:, :, :, :], AX, ALU.add))
            rt(dve.tensor_scalar(chosen[:, :, :], rank[:, :, :], 1.5, None, ALU.is_lt))
            dve.wait_ge(rt_ex, 1)
            rt(dve.tensor_tensor(exs[:, :, :], ex[:, :, :], chosen[:, :, :], ALU.mult))
            rt(dve.tensor_reduce(wsum[:, :], exs[:, :, :], AX, ALU.add))
            rt(dve.reciprocal(wrec[:, :], wsum[:, :]))
            rt(dve.tensor_tensor(WG[:, :, :], exs[:, :, :], wrec[:, :].unsqueeze(2).broadcast_to([P, NTT, E]), ALU.mult))

            def hidden(u, n):
                dve.wait_ge(silu_ok, u + 1)
                dve.wait_ge(h3_mm, u + 1)
                if n >= 2:
                    dve.wait_ge(hh_ok, u - 1)
                    dve.wait_ge(hl_ok, u - 1)
                dve.tensor_tensor(hm[:, n % 2, :], bank(2 + n % 2), gl[:, n % 2, :], ALU.mult).then_inc(hm_ok, 1)

            def hidden_lo(u, n):
                dve.wait_ge(hh_ok, u + 1)
                dve.tensor_tensor(h_l[:, (n // FC) % 2, n % FC, :], hm[:, n % 2, :],
                                  as32(h_h[:, (n // FC) % 2, n % FC, :]), ALU.subtract).then_inc(hl_ok, 1)

            def collect(ee, blk):
                k, tb = blk // B, blk % B
                for i in range(NT):
                    t, a = NT * tb + i, NT * (2 * B * ee + blk) + i
                    dve.wait_ge(dn_mm, a + 1)
                    if blk >= B:
                        dve.wait_ge(acc_ok, a + 1 - NT * B)
                    dve.scalar_tensor_tensor(out=X[:, t, :], in0=bank(4 + i % 2, D), scalar=wcol[:, k, t:t + 1],
                                             in1=X[:, t, :], op0=ALU.mult, op1=ALU.add).then_inc(acc_ok, 1)

            def layer_norm_out(tb):
                dve.wait_ge(acc_ok, NT * B * (E - 1) + NT * tb + NT)
                for i in range(NT):
                    ins = dve.bn_stats(ln_st[:, i, :], X[:, NT * tb + i, :])
                ins.then_inc(fln_ch, 1)
                dve.wait_ge(fln_ch, 2 * tb + 1)
                for i in range(NT):
                    ins = dve.bn_aggr(ln_mv[:, i, :], ln_st[:, i, :])
                ins.then_inc(fln_ch, 1)
                dve.wait_ge(fln_ch, 2 * tb + 2)
                dve.tensor_scalar(ln_ve[:, :], ln_mv[:, :, 1], LN_EPS, None, ALU.add).then_inc(flnv_ok, 1)
                dve.wait_ge(flnr_ok, tb + 1)
                for i in range(NT):
                    xi = X[:, NT * tb + i, :]
                    dve.tensor_scalar(xi, xi, ln_mv[:, i, 0:1], ln_rs[:, i:i + 1], ALU.subtract, ALU.mult)\
                        .then_inc(x3_ok, 1)

            def two_experts(ee, first, last):
                if not first:
                    dve.wait_ge(acc_ok, 2 * NT * B * ee)
                dve.tensor_copy(wcol[:, :, :], WG[:, :, bass.ds(2 * ee, 2)].rearrange("p t k -> p k t")).then_inc(wcol_ok, 1)
                dve.wait_ge(wcol_ok, ee + 1)
                for n in range(2 * UNITS):
                    u = 2 * UNITS * ee + n
                    hidden(u, n)
                    if n >= 1:
                        hidden_lo(u - 1, n - 1)
                    if n % FC == FC - 1 and n >= FC:
                        collect(ee, n // FC - 1)
                        if last and n // FC - 1 >= B:
                            layer_norm_out(n // FC - 1 - B)
                hidden_lo(2 * UNITS * (ee + 1) - 1, 2 * UNITS - 1)
                collect(ee, 2 * B - 1)
                if last:
                    layer_norm_out(B - 1)

            two_experts(0, True, False)
            with dve.Fori(1, E // 2 - 1) as ee:
                two_experts(ee, False, False)
            two_experts(E // 2 - 1, False, True)

        @block.tensor
        def _(pe):
            pe.wait_ge(const_pool, 3)
            pe.wait_ge(const_dve, 3)
            pe.wait_ge(w_lo, 1)

            def project(t, i, wait):
                pe.wait_ge(xt_lo, t + 1)
                rows = slice(P * i, P * i + P)
                if wait:
                    pe.wait_ge(cen_ok, NT * t + i)
                for c in range(KC):
                    mm = split3(pe, bank(2), xt_h[:, c, rows], xt_l[:, c, rows], WSh[:, c, 0:2 * D], WSl[:, c, 0:2 * D],
                                c == 0, c == KC - 1)
                mm.then_inc(qk_mm, 1)
                if wait:
                    pe.wait_ge(v_out, NT * t + i)
                for c in range(KC):
                    mm = split3(pe, bank(3, D), xt_h[:, c, rows], xt_l[:, c, rows], WSh[:, c, 2 * D:3 * D],
                                WSl[:, c, 2 * D:3 * D], c == 0, c == KC - 1)
                mm.then_inc(v_mm, 1)

            def turn(b, g):
                for q in range(2):
                    for src, bk, done in ((QX, 0, tq_mm), (KX, 1, tk_mm)):
                        if q == 1:
                            pe.wait_ge(*((qT_ok, 8 * b + 2 * g + 1) if bk == 0 else (kT_ok, 16 * b + 4 * g + 2)))
                        h = 4 * g + 2 * q
                        for i in range(NT):
                            mm = pe.transpose(PS[:, bk, P * i:P * i + P],
                                              as32(src[:, i, h:h + 2, :, :]).rearrange("p h s f -> p (h s f)"),
                                              ident[:, :])
                        mm.then_inc(done, 1)

            def scores(b, g, c):
                for j in range(4):
                    n = 16 * g + 4 * c + j
                    if n >= 2:
                        pe.wait_ge(sqr_ok, 64 * b + n - 1)
                    pe.matmul(PS[:, 4 + n % 2, P * c:T], kT[:, g % 2, j, P * c:P * c + P],
                              qT[:, g % 2, j // 2, P * c:T], start=True, stop=True).then_inc(sc_mm, 1)

            def values(b, g, c):
                pe.wait_ge(mask_ok, 64 * b + 16 * g + 4 * c + 4)
                if c == 0 and g >= 1:
                    pe.wait_ge(osb_ok, QUADS * b + g)
                for j in range(4):
                    n = 16 * g + 4 * c + j
                    mm = pe.matmul(PS[32 * j:32 * j + 32, 6, P * c:T], VS[:, c, 4 * g + j, :], A[:, n % 8, P * c:T],
                                   start=(c == 0), stop=(c == NT - 1))
                mm.then_inc(av_mm, 1)

            def back(b, g):
                pe.wait_ge(osb_ok, QUADS * b + g + 1)
                if g >= 1:
                    pe.wait_ge(y_ok, QUADS * b + g)
                for i in range(NT):
                    mm = pe.transpose(PS[:, 7, P * i:P * i + P], osb[:, g % 2, P * i:P * i + P], ident[:, :])
                mm.then_inc(ot_mm, 1)

            def attention(b, more):
                pe.wait_ge(lo_ok, 8 * b + 8)
                pe.wait_ge(vs_ok, b + 1)
                turn(b, 0)
                for g in range(QUADS):
                    pe.wait_ge(qT_ok, 8 * b + 2 * g + 2)
                    pe.wait_ge(kT_ok, 16 * b + 4 * g + 4)
                    scores(b, g, 0)
                    if g + 1 < QUADS:
                        turn(b, g + 1)
                    for c in range(NT):
                        if c + 1 < NT:
                            scores(b, g, c + 1)
                        if c == 1 and g >= 1:
                            back(b, g - 1)
                        if c == 2 and more:
                            project(b + 1, g, True)
                        values(b, g, c)
                back(b, QUADS - 1)
                pe.wait_ge(y_ok, QUADS * b + QUADS)
                for c in range(KC):
                    for i in range(NT):
                        mm = pe.transpose(PS[:, c, P * i:P * i + P], y[:, i, P * c:P * c + P], ident[:, :])
                    mm.then_inc(yt_mm, 1)
                pe.wait_ge(yl_ok, KC * b + KC)
                for i in range(NT):
                    t = slice(P * i, P * i + P)
                    if i >= 2:
                        pe.wait_ge(res_ok, NT * b + i - 1)
                    for c in range(KC):
                        mm = split3(pe, bank(6 + i % 2, D), y_h[:, c, t], y_l[:, c, t], WSh[:, c, 3 * D:], WSl[:, c, 3 * D:],
                                    c == 0, c == KC - 1)
                    mm.then_inc(o_mm, 1)
                pe.wait_ge(res_ok, NT * b + NT)

            for i in range(NT):
                project(0, i, i >= 1)
            with pe.Fori(0, B - 1) as b:
                attention(b, True)
            attention(B - 1, False)

            def context_product(o, lhs, rhs, first_is_weight):
                ops = []
                for wc, cc in (((0, "h"), Ch), ((0, "h"), Cl), ((0, "l"), Ch), ((1, "h"), Cc), ((1, "l"), Cc)):
                    ops.append((lhs(wc), rhs(cc)) if first_is_weight else (lhs(cc), rhs(wc)))
                for n, (l, r) in enumerate(ops):
                    mm = pe.matmul(o, l, r, start=(n == 0), stop=(n == len(ops) - 1))
                return mm

            def step(b, s):
                kind = s[0]
                if kind == "osplit":
                    return
                if kind == "max":
                    h, v = s[1], s[2]
                    n, i, k = NMX * h + v, v // NB, v % NB
                    if v == 0:
                        pe.wait_ge(ld_h[h % 3], loaded(b, h))
                    if n >= 2:
                        pe.wait_ge(mx_ok, NMX * XH * b + n - 1)
                    pe.matmul(bank(2 + n % 2, BW), QA[:, h % 3, P * i:P * i + P], KA[:, h % 3, BSTART[k]:BSTART[k] + BW],
                              start=True, stop=True).then_inc(mx_mm, 1)
                    return
                m = MISC[s]
                if m >= 2:
                    pe.wait_ge(misc_ok, NM * b + m - 1)
                bk = bank(6 + m % 2)
                if kind == "xt":
                    pe.wait_ge(xs_ok, b + 1)
                    for i in range(NT):
                        mm = pe.transpose(bk[:, P * i:P * i + P], xs[:, i, P * s[1]:P * s[1] + P], ident[:, :])
                if kind == "q":
                    pe.wait_ge(misc_ok, NM * b + MISC[("xt", KC - 1)] + 1)
                    w = slice(P * s[1], P * s[1] + P)
                    for c in range(KC):
                        mm = split3(pe, bk, WQh[:, c, w], WQl[:, c, w], x1_h[:, c, :], x1_l[:, c, :],
                                    c == 0, c == KC - 1)
                if kind == "k":
                    pe.wait_ge(c_lo, 8 * b + 8)
                    w = slice(P * s[1], P * s[1] + P)
                    cols = slice(BSTART[s[2]], BSTART[s[2]] + BW)
                    mm = context_product(bk[:, 0:BW], lambda wc: (WKh if wc[1] == "h" else WKl)[:, wc[0], w],
                                         lambda cc: cc[:, cols], True)
                if kind == "v":
                    r = LROWS[s[1]]
                    cols = slice(P * s[1], P * s[1] + r)
                    mm = context_product(bk[0:r, :], lambda cc: cc[:, cols],
                                         lambda wc: (WVh if wc[1] == "h" else WVl)[:, wc[0], :], False)
                if kind == "mrow":
                    pe.wait_ge(hmax_ok, XH * b + s[1] + 1)
                    mm = pe.transpose(PS[0:NT, 6 + m % 2, 0:P], mx[:, s[1] % 2, :], ident[:, :])
                if kind == "wo":
                    pe.wait_ge(ol_ok, PAIRS * b + s[1] + 1)
                    t = slice(P * s[2], P * s[2] + P)
                    mm = split3(pe, bk[:, 0:D], O_h[:, t], O_l[:, t], WOh[:, s[1], :], WOl[:, s[1], :], True, True)
                mm.then_inc(misc_mm, 1)

            def scores_t(b, h, j):
                u = NL * h + j
                if j == 0:
                    pe.wait_ge(ld_h[h % 3], loaded(b, h))
                    pe.wait_ge(ld_m, 16 * NT * (XH * b + h + 1))
                if u >= 2:
                    pe.wait_ge(exp_ok, NL * XH * b + u - 1)
                keys = slice(P * j, P * j + LROWS[j])
                o = bank(u % 2, rows=LROWS[j])
                pe.matmul(o, KA[:, h % 3, keys], QA[:, h % 3, :], start=True, stop=False)
                pe.matmul(o, KB[:, h % 3, keys], QB[:, h % 3, :], start=False, stop=True).then_inc(st_mm, 1)

            pe.wait_ge(w_lo, 5)
            pe.wait_ge(xconst, 4)
            with pe.Fori(0, B) as b:
                for s in PROLOGUE:
                    step(b, s)
                pe.wait_ge(misc_ok, NM * b + MISC[("v", NL - 1)] + 1)
                scores_t(b, 0, 0)
                for h in range(XH):
                    for j in range(NL):
                        u = NL * h + j
                        if u + 1 < NL * XH:
                            scores_t(b, (u + 1) // NL, (u + 1) % NL)
                        for s in beside(h, j):
                            step(b, s)
                        pe.wait_ge(exp_ok, NL * XH * b + u + 1)
                        if j == 0 and h >= 2:
                            pe.wait_ge(head_ok, XH * b + h - 1)
                        pe.matmul(bank(4 + h % 2), v_ones(j, h), PX[0:LROWS[j], u % NP, :], start=(j == 0),
                                  stop=(j == NL - 1)).then_inc(pv_mm, 1)
                for s in EPILOGUE:
                    step(b, s)

            pe.wait_ge(x2_ok, NT * B + 1)
            for n in range(B * KC):
                if n >= 2:
                    pe.wait_ge(ft_ok, n - 1)
                for i in range(NT):
                    mm = pe.transpose(PS[:, n % 2, P * i:P * i + P],
                                      X[:, NT * (n // KC) + i, P * (n % KC):P * (n % KC) + P], ident[:, :])
                mm.then_inc(ft_mm, 1)
            pe.wait_ge(gate_lo, 1)
            for tb in range(B):
                cols = slice(T * tb, T * tb + T)
                pe.wait_ge(ft_ok, KC * (tb + 1))
                if tb >= 2:
                    pe.wait_ge(gs_ok, tb - 1)
                for c in range(KC):
                    mm = split3(pe, bank(2 + tb % 2, rows=E), G_h[:, c, 0:E], G_l[:, c, 0:E], x2_h[:, c, cols], x2_l[:, c, cols],
                                c == 0, c == KC - 1)
                mm.then_inc(gs_mm, 1)
            pe.wait_ge(gs_ok, B)
            for t in range(B * NT):
                mm = pe.transpose(PS[:, 4, E * t:E * t + E], sT[:, P * t:P * t + P], ident[0:E, 0:E])
            mm.then_inc(gt_mm, 1)
            pe.wait_ge(route, 1)

            def up(ee, n):
                u, k, tb, f = 2 * UNITS * ee + n, n // UNITS, (n // FC) % B, n % FC
                cols = slice(T * tb, T * tb + T)
                for m, done, free in ((0, h1_mm, silu_ok), (1, h3_mm, hm_ok)):
                    if n >= 2:
                        pe.wait_ge(free, u - 1)
                    for c in range(KC):
                        w = slice(FF * c + P * f, FF * c + P * f + P)
                        mm = split3(pe, bank(2 * m + n % 2), W_h[:, k, m, w], W_l[:, k, m, w], x2_h[:, c, cols],
                                    x2_l[:, c, cols], c == 0, c == KC - 1)
                    mm.then_inc(done, 1)

            def down(ee, blk):
                k = blk // B
                pe.wait_ge(hl_ok, FC * (2 * B * ee + blk + 1))
                for i in range(NT):
                    a, t = NT * (2 * B * ee + blk) + i, slice(P * i, P * i + P)
                    if NT * blk + i >= 2:
                        pe.wait_ge(acc_ok, a - 1)
                    for f in range(FC):
                        w = slice(D * f, D * f + D)
                        mm = split3(pe, bank(4 + i % 2, D), h_h[:, blk % 2, f, t], h_l[:, blk % 2, f, t], W_h[:, k, 2, w],
                                    W_l[:, k, 2, w], f == 0, f == FC - 1)
                    mm.then_inc(dn_mm, 1)

            def two_experts(ee, first):
                for n in range(2 * UNITS):
                    if n % UNITS == 0:
                        pe.wait_ge(we_lo, 3 * (2 * ee + n // UNITS) + 3)
                    up(ee, n)
                    if n % FC == FC - 1 and n >= FC:
                        down(ee, n // FC - 1)
                down(ee, 2 * B - 1)

            two_experts(0, True)
            with pe.Fori(1, E // 2 - 1) as ee:
                two_experts(ee, False)
            two_experts(E // 2 - 1, False)


def kernel(**inputs):
    import numpy as _np
    import concourse.bacc as _bacc
    from concourse import mybir as _mybir
    from concourse.bass_utils import run_bass_kernel_spmd as _run

    a = {k: _np.asarray(v) for k, v in inputs.items()}
    lay = {
        "x": a["x"],
        "xt": a["x"].transpose(0, 2, 1),
        "ctxt": a["ctx_768"].transpose(0, 2, 1),
        "wqkv": _np.concatenate([a["L0_attn_Wq"], a["L0_attn_Wk"], a["L0_attn_Wv"]]).T,
        "wo_s": a["L0_attn_Wo"].T,
        "gamma": a["L0_attn_gamma"],
        "beta": a["L0_attn_beta"],
        "wq": a["L0_xattn_Wq"],
        "wk": a["L0_xattn_Wk"],
        "wv": a["L0_xattn_Wv"],
        "wo_x": a["L0_xattn_Wo"],
        "bo": a["L0_xattn_bo"],
        "gate": a["L0_ffn_gate_w"].T,
        "w1": a["L0_ffn_w1"].transpose(0, 2, 1),
        "w3": a["L0_ffn_w3"].transpose(0, 2, 1),
        "w2": a["L0_ffn_w2"].transpose(0, 2, 1),
    }
    nc = _bacc.Bacc("TRN2", target_bir_lowering=False, num_devices=1)
    arrays, args = {}, []
    for name, v in lay.items():
        v = _np.ascontiguousarray(v)
        arrays[f"in_{name}"] = v
        args.append(nc.dram_tensor(f"in_{name}", v.shape, _mybir.dt.from_np(v.dtype), kind="ExternalInput").ap())
    o = nc.dram_tensor("out_0", (B, T, D), _mybir.dt.float32, kind="ExternalOutput").ap()
    decoder_layer(nc, *args, o)
    r = _run(nc, [arrays], core_ids=[0])
    return r.results[0]["out_0"]
```

```python
import concourse.bass as bass
from concourse import mybir
from contextlib import ExitStack

B, T, D = 4, 512, 256
P = 128
NT = T // P
KC = D // P
SH, SF = 16, 16
L, C = 1601, 192
XH, XD = 8, 64
INNER = XH * XD
E, FF = 8, 512
FC = FF // P
LN_EPS = 1e-5
DEN_EPS = 1e-5
QUADS = SH // 4
PAIRS = XH // 2
NL = (L + P - 1) // P
LROWS = [min(P, L - P * j) for j in range(NL)]
BW = 402
BSTART = [0, 400, 800, L - BW]
BEDGE = [0, 402, 802, 1202, L]
NB = len(BSTART)


def decoder_layer(nc, x, xt, ctxt, wqkv, wo_s, gamma, beta, wq, wk, wv, wo_x, bo, gate, w1, w3, w2, out):
    f32 = mybir.dt.float32
    f32r = mybir.dt.float32r
    ALU = mybir.AluOpType
    ACT = mybir.ActivationFunctionType
    AX = mybir.AxisListType.X

    ctx = ExitStack()
    with ctx:
        def sem(name):
            return ctx.enter_context(nc.semaphore(name))

        def keep(name, shape, dt=f32):
            return ctx.enter_context(nc.sbuf_tensor(name, shape, dt))

        def stage_buffers(stack):
            return lambda name, shape, dt=f32: stack.enter_context(nc.sbuf_tensor(name, shape, dt))

        X = keep("X", [P, B * NT, D])
        ident = keep("ident", [P, P])
        gam = keep("gam", [P, SF])
        bet = keep("bet", [P, SF])
        bo_t = keep("bo_t", [P, D])
        neg_half = keep("neg_half", [P, 128])
        ln_st = keep("ln_st", [P, NT, 6])
        ln_mv = keep("ln_mv", [P, NT, 2])
        ln_ve = keep("ln_ve", [P, NT])
        ln_rs = keep("ln_rs", [P, NT])

        PS = ctx.enter_context(nc.psum_tensor("PS", [P, 8, 512], f32))

        both = ExitStack()
        sx = stage_buffers(both)
        WQh, WQl = sx("WQh", [P, KC, INNER], f32r), sx("WQl", [P, KC, INNER], f32r)
        WKh, WKl = sx("WKh", [P, 2, INNER], f32r), sx("WKl", [P, 2, INNER], f32r)
        WVh, WVl = sx("WVh", [P, 2, INNER], f32r), sx("WVl", [P, 2, INNER], f32r)
        WOh, WOl = sx("WOh", [P, PAIRS, D], f32r), sx("WOl", [P, PAIRS, D], f32r)

        st = ExitStack()
        ss = stage_buffers(st)
        raw = ss("raw", [P, 4, 1024])
        WSh, WSl = ss("WSh", [P, KC, 4 * D], f32r), ss("WSl", [P, KC, 4 * D], f32r)
        xt_raw = ss("xt_raw", [P, KC, T])
        xt_h, xt_l = ss("xt_h", [P, KC, T], f32r), ss("xt_l", [P, KC, T], f32r)
        cen = ss("cen", [P, 2, 2 * D])
        feat = ss("feat", [P, NT, 2 * D])
        Vn = ss("Vn", [P, NT, D])
        g_mean = ss("g_mean", [P, 2, 32])
        g_var = ss("g_var", [P, 2, 32])
        g_sd = ss("g_sd", [P, 2, 32])
        g_rs = ss("g_rs", [P, 2, 32])
        g_t = ss("g_t", [P, 2, 32])
        QX = ss("QX", [P, NT, SH, 4, SF], f32r)
        KX = ss("KX", [P, NT, SH, 4, SF], f32r)
        qT = ss("qT", [P, 2, 2, T], f32r)
        kT = ss("kT", [P, 2, 4, T], f32r)
        A = ss("A", [P, 8, T])
        VS = ss("VS", [P, NT, SH, 2 * SF])
        osb = ss("osb", [P, 2, T])
        den = ss("den", [P, NT * 4])
        rden = ss("rden", [P, NT * 4])
        y = ss("y", [P, NT, D])
        y_h, y_l = ss("y_h", [P, KC, T], f32r), ss("y_l", [P, KC, T], f32r)
        st.close()

        xs_ = ExitStack()
        sxx = stage_buffers(xs_)
        first = ExitStack()
        c_first = stage_buffers(first)("c_first", [P, 2, L])
        first.close()
        KA = sxx("KA", [P, 3, L], f32r)
        c_raw = sxx("c_raw", [P, 2, BW])
        NP = 4
        PX = sxx("PX", [P, NP, T])
        R = sxx("R", [P, T])
        O = sxx("O", [P, T])

        def raw_context(b, k):
            return c_first[:, :, BEDGE[k]:BEDGE[k + 1]] if isinstance(b, int) and b == 0 \
                else c_raw[:, :, 0:BEDGE[k + 1] - BEDGE[k]]

        c_tmp = sxx("c_tmp", [P, BW], f32r)
        Ch = sxx("Ch", [P, L], f32r)
        Cl = sxx("Cl", [P, L], f32r)
        Cc = sxx("Cc", [P, L], f32r)
        VX = sxx("VX", [P, NL, PAIRS, 3 * XD])
        Kh, Kl = sxx("Kh", [P, L], f32r), sxx("Kl", [P, L], f32r)
        KB = sxx("KB", [P, 3, L], f32r)
        Qh, Ql = sxx("Qh", [P, T], f32r), sxx("Ql", [P, T], f32r)
        QA = sxx("QA", [P, 3, T], f32r)
        QB = sxx("QB", [P, 3, T], f32r)
        x1_h, x1_l = sxx("x1_h", [P, KC, T], f32r), sxx("x1_l", [P, KC, T], f32r)
        mxp = sxx("mxp", [P, 2, NT, NB])
        mx = sxx("mx", [P, 2, NT])
        mrow = sxx("mrow", [NT, 2, P], f32r)
        between = ExitStack()
        xs = stage_buffers(between)("xs", [P, NT, D])[:, :, :]
        between.close()
        OHL = sxx("OHL", [P, 2, T], f32r)
        O_h, O_l = OHL[:, 0, :], OHL[:, 1, :]
        xs_.close()
        both.close()

        fs = ExitStack()
        sf = stage_buffers(fs)
        x2_h, x2_l = sf("x2_h", [P, KC, B * T], f32r), sf("x2_l", [P, KC, B * T], f32r)
        G_raw = sf("G_raw", [P, KC, P])
        G_h, G_l = sf("G_h", [P, KC, P], f32r), sf("G_l", [P, KC, P], f32r)
        sT = sf("sT", [E, B * T])
        S8 = sf("S8", [P, B * NT, E])
        cmp = sf("cmp", [P, B * NT, E, E])
        cmp2 = sf("cmp2", [P, B * NT, E, E])
        lower = sf("lower", [P, E, E])
        rank = sf("rank", [P, B * NT, E])
        chosen = sf("chosen", [P, B * NT, E])
        smax = sf("smax", [P, B * NT])
        sh = sf("sh", [P, B * NT, E])
        ex = sf("ex", [P, B * NT, E])
        exs = sf("exs", [P, B * NT, E])
        wsum = sf("wsum", [P, B * NT])
        wrec = sf("wrec", [P, B * NT])
        WG = sf("WG", [P, B * NT, E])
        wcol = sf("wcol", [P, 2, B * NT])
        W_raw = sf("W_raw", [P, 3, 1024])
        W_h, W_l = sf("W_h", [P, 2, 3, 1024], f32r), sf("W_l", [P, 2, 3, 1024], f32r)
        gl = sf("gl", [P, 2, T])
        hm = sf("hm", [P, 2, T])
        h_h, h_l = sf("h_h", [P, 2, FC, T], f32r), sf("h_l", [P, 2, FC, T], f32r)
        fs.close()

        def bank(k, n=512, rows=P):
            return PS[0:rows, k, 0:n]

        def as32(ap):
            return ap.bitcast(f32)

        def hold(eng, s, value):
            eng.wait_ge(s, value)
            eng.nop(nofuse=True)

        def split3(pe, o, lh, ll, rh, rl, first, last):
            pe.matmul(o, lh, rh, start=first, stop=False)
            pe.matmul(o, lh, rl, start=False, stop=False)
            return pe.matmul(o, ll, rh, start=False, stop=last)

        ld_w = sem("ld_w")
        ld_w2 = sem("ld_w2")
        ld_x = sem("ld_x")
        ld_xt = sem("ld_xt")
        const_pool = sem("const_pool")
        const_dve = sem("const_dve")
        w_hi = sem("w_hi")
        w_lo = sem("w_lo")
        xt_hi, xt_lo = sem("xt_hi"), sem("xt_lo")
        qk_mm, v_mm = sem("qk_mm"), sem("v_mm")
        v_out, vs_ok = sem("v_out"), sem("vs_ok")
        cch, vch, fch = sem("cch"), sem("vch"), sem("fch")
        nch = sem("nch")
        lch = sem("lch")
        cen_ok, sq_ok, var_ok, sd_ok, fn_ok, nrm_ok, gm_ok, feat_ok = (sem(n) for n in (
            "cen_ok", "sq_ok", "var_ok", "sd_ok", "fn_ok", "nrm_ok", "gm_ok", "feat_ok"))
        hi_ok, lo_ok = sem("hi_ok"), sem("lo_ok")
        tq_mm, tk_mm, qT_ok, kT_ok = sem("tq_mm"), sem("tk_mm"), sem("qT_ok"), sem("kT_ok")
        sc_mm, sqr_ok, mask_ok, av_mm = sem("sc_mm"), sem("sqr_ok"), sem("mask_ok"), sem("av_mm")
        osb_ok, ot_mm, y_ok, yt_mm, yh_ok, yl_ok = (sem(n) for n in (
            "osb_ok", "ot_mm", "y_ok", "yt_mm", "yh_ok", "yl_ok"))
        o_mm, res_ok = sem("o_mm"), sem("res_ok")
        lnv_ok, lnr_ok, x1_ok = sem("lnv_ok"), sem("lnr_ok"), sem("x1_ok")

        ld_bo = sem("ld_bo")
        xconst = sem("xconst")
        ld_c = sem("ld_c")
        ld_h = [sem(f"ld_h{k}") for k in range(3)]
        ld_a = [sem(f"ld_a{k}") for k in range(3)]
        ld_m = sem("ld_m")
        c_hi, c_lo = sem("c_hi"), sem("c_lo")
        xs_ok, xb_ok = sem("xs_ok"), sem("xb_ok")
        misc_mm, misc_hi, misc_ok = sem("misc_mm"), sem("misc_hi"), sem("misc_ok")
        mx_mm, mx_ok, hmax_ok = sem("mx_mm"), sem("mx_ok"), sem("hmax_ok")
        st_mm, exp_ok, pv_mm = sem("st_mm"), sem("exp_ok"), sem("pv_mm")
        rec_ok, head_ok, oh_ok, ol_ok = sem("rec_ok"), sem("head_ok"), sem("oh_ok"), sem("ol_ok")
        xln_ch, xlnv_ok, xlnr_ok, x2_ok = sem("xln_ch"), sem("xlnv_ok"), sem("xlnr_ok"), sem("x2_ok")

        ld_g, gz_ok, gate_hi, gate_lo, low_ok = (sem(n) for n in ("ld_g", "gz_ok", "gate_hi", "gate_lo", "low_ok"))
        ft_mm, ft_hi, ft_ok = sem("ft_mm"), sem("ft_hi"), sem("ft_ok")
        gs_mm, gs_ok, gt_mm, route, rt_sh, rt_ex = (sem(n) for n in ("gs_mm", "gs_ok", "gt_mm", "route", "rt_sh", "rt_ex"))
        ld_e, we_hi, we_lo = sem("ld_e"), sem("we_hi"), sem("we_lo")
        h1_mm, h3_mm, silu_ok, hm_ok, hh_ok, hl_ok = (sem(n) for n in (
            "h1_mm", "h3_mm", "silu_ok", "hm_ok", "hh_ok", "hl_ok"))
        dn_mm, acc_ok, wcol_ok = sem("dn_mm"), sem("acc_ok"), sem("wcol_ok")
        fln_ch, flnv_ok, flnr_ok, x3_ok, st_out = (sem(n) for n in ("fln_ch", "flnv_ok", "flnr_ok", "x3_ok", "st_out"))
        UNITS = B * FC

        def beside(h, j, first, more):
            steps = []
            if j < HQ and (h >= 1 or not first):
                steps += [((0, ("hout", h - 1, j)) if h >= 1 else (-1, ("hout", XH - 1, j)))]
            p = h // 2 + 1
            nb, pair = p // PAIRS, p % PAIRS
            if h == 0 and j + 1 < NL:
                steps += [(0, ("v", j + 1))]
            if h + 1 < XH or more:
                nh, hb = (h + 1) % XH, (h + 1) // XH
                if 1 <= j <= NMX // 2:
                    steps += [(hb, ("max", nh, v)) for v in (2 * j - 2, 2 * j - 1)]
                if j == NMX // 2 + 1:
                    steps += [(hb, ("mrow", nh))]
            if h % 2 == 0 and (nb == 0 or more):
                if 2 <= j < 2 + NB:
                    steps += [(nb, ("k", pair, j - 2))]
                if j == 2 + NB:
                    steps += [(nb, ("q", pair))]
            if h % 2 == 0 and (h >= 2 or not first):
                ob, op = (-1, PAIRS - 1) if h == 0 else (0, h // 2 - 1)
                if j == 7:
                    steps += [(ob, ("osplit", op))]
                if j in (8, 9, 11, 12):
                    steps += [(ob, ("wo", op, (8, 9, 11, 12).index(j)))]
                if h == 0 and j == 12:
                    steps += [(ob, ("norm",))]
            if h == XH - 3 and more:
                if j in (2, 4, 6, 8):
                    steps += [(1, ("ctx", j // 2 - 1))]
                if j == 8:
                    steps += [(1, ("xcopy",))]
                if j in (10, 11):
                    steps += [(1, ("xt", j - 10))]
            if h == XH - 1 and j == NL - 1 and more:
                steps += [(1, ("v", 0))]
            return steps

        NMX = NT * NB
        HQ = 4
        PROLOGUE = [("xcopy",), ("ctx", 0), ("xt", 0), ("xt", 1), ("ctx", 1), ("ctx", 2), ("q", 0), ("ctx", 3)] \
            + [("k", 0, k) for k in range(NB)] + [("max", 0, v) for v in range(NMX)] + [("mrow", 0), ("v", 0)]
        EPILOGUE = [("hout", XH - 1, q) for q in range(HQ)] + [("osplit", PAIRS - 1)] \
            + [("wo", PAIRS - 1, i) for i in range(NT)] + [("norm",)]
        ORDER = [(0, s) for s in PROLOGUE]
        for bb in range(B):
            ORDER += [(bb + d, s) for h in range(XH) for j in range(NL) for d, s in beside(h, j, bb == 0, bb < B - 1)]
        ORDER += [(B - 1, s) for s in EPILOGUE]
        MISC = {bs: n for n, bs in enumerate(bs for bs in ORDER if bs[1][0] not in ("max", "osplit", "norm", "ctx", "xcopy", "hout"))}
        HIGH = {bs: n for n, bs in enumerate(bs for bs in MISC if bs[1][0] in ("xt", "q", "k"))}
        NM, NH = (table[(2, ("q", 0))] - table[(1, ("q", 0))] for table in (MISC, HIGH))
        SPARE, FREED, last_in = {}, {}, {6: None, 7: None}
        turn_to = 6
        for bs, n in MISC.items():
            turn_to = 6 if bs[1] == ("mrow", 4) else turn_to
            SPARE[bs], FREED[bs] = turn_to, last_in[turn_to]
            last_in[turn_to] = n + 1
            turn_to = 13 - turn_to

        def misc(b, s):
            return MISC[(b, s)] if isinstance(b, int) else NM * b + (MISC[(1, s)] - NM)

        def highs(b, s):
            return HIGH[(b, s)] if isinstance(b, int) else NH * b + (HIGH[(1, s)] - NH)

        def spare(b, s):
            return SPARE[(b if isinstance(b, int) else 1, s)]

        def freed(b, s):
            return FREED[(b, s)] if isinstance(b, int) else NM * b + (FREED[(1, s)] - NM)

        def before(b, h, by, per):
            return (b, h - by) if h >= by else (b - 1, h - by + per)

        SLOT_LOADS = [len(range(k, XH, 3)) for k in range(3)]

        def loaded(b, h, parts):
            return 16 * parts * (SLOT_LOADS[h % 3] * b + h // 3 + 1)

        def v_ones(j, h):
            return VX[0:LROWS[j], j, h // 2, XD * (h % 2):XD * (h % 2) + 2 * XD]

        SLOTS = QUADS * NT

        def alongside(n, first, more):
            rest = {0: [("back", 3), ("quad", 3)], 1: [("yt", 0)], 2: [("yt", 1)], 3: [("out", 0)],
                    4: [("out", 1)], 5: [("stats",)], 6: [("rsqrt",)], 7: [("norm",)]}
            own = {0: [("vs", 3)]}
            for g in range(QUADS - 1):
                if g >= 1:
                    own.setdefault(NT * g - 1, []).extend([("turn q", g + 1, 0), ("turn k", g + 1, 0)])
                own.setdefault(NT * g, []).extend([("turn q", g + 1, 1), ("turn k", g + 1, 1)])
                own.setdefault(NT * g + 5, []).extend([("back", g), ("quad", g)])
            ahead = {0: [("x",)], 9: [("split", 0)], 10: [("split", 1)], 11: [("split", 2)], 12: [("split", 3), ("vs", 0)],
                     13: [("vs", 1), ("turn q", 0, 0), ("turn k", 0, 0)], 14: [("vs", 2), ("turn q", 0, 1), ("turn k", 0, 1)],
                     15: [("turn q", 1, 0), ("turn k", 1, 0)]}
            for i in range(NT):
                for after, kind in ((1, "project v"), (1, "project qk"), (2, "centre"), (3, "variance"), (4, "normalise"), (5, "affine")):
                    ahead.setdefault(2 * i + after, []).insert(0, (kind, i))
            last = {5 + 2 * k: [("weights", k)] for k in range(4)}
            return ([(-1, s) for s in rest.get(n, []) if not first] + [(0, s) for s in own.get(n, [])]
                    + ([(1, s) for s in ahead.get(n, [])] if more else [(0, s) for s in last.get(n, [])]))

        LATE = ("turn q", "turn k", "back", "quad", "yt", "out")

        def others_first(steps):
            return [ds for ds in steps if ds[1][0] not in LATE] + [ds for ds in steps if ds[1][0] in LATE]

        FEATURES = ("project qk", "project v", "centre", "variance", "normalise", "affine")
        OPENING = [("x",)] + [(kind, i) for i in range(NT) for kind in FEATURES] \
            + [("split", i) for i in range(NT)] + [("vs", g) for g in range(3)] + [("turn " + part, g, q) for g, q in ((0, 0), (0, 1), (1, 0)) for part in "qk"]
        CLOSING = [("back", 3), ("quad", 3), ("yt", 0), ("yt", 1), ("out", 0), ("out", 1), ("stats",), ("rsqrt",), ("norm",)]

        def started(b, n, least):
            return n >= least or not (isinstance(b, int) and b == 0)

        block = ctx.enter_context(nc.Block())

        @block.sync
        def _(sp):
            sp.dma_start(xt_raw[:, :, :], xt[0].rearrange("(c p) t -> p c t", p=P)).then_inc(ld_xt, 16)
            sp.dma_start(raw[:, 0:2, 0:3 * D], wqkv.rearrange("(c p) n -> p c n", p=P)).then_inc(ld_w, 16)
            sp.dma_start(raw[:, 0:2, 3 * D:4 * D], wo_s.rearrange("(c p) n -> p c n", p=P)).then_inc(ld_w, 16)
            sp.dma_start(gam[:, :], gamma.partition_broadcast(P)).then_inc(ld_w, 16)
            sp.dma_start(bet[:, :], beta.partition_broadcast(P)).then_inc(ld_w, 16)
            sp.dma_start(X[:, :, :], x.rearrange("b (i p) d -> p (b i) d", p=P)).then_inc(ld_x, 16)
            sp.dma_start(raw[:, 2, :].rearrange("p (c n) -> p c n", c=KC),
                         wq.rearrange("(c p) n -> p c n", p=P)).then_inc(ld_w2, 16)
            sp.dma_start(raw[:, 3, :].rearrange("p (c n) -> p c n", c=PAIRS),
                         wo_x.rearrange("(c p) n -> p c n", p=P)).then_inc(ld_w2, 16)
            sp.dma_start(bo_t[:, :], bo.partition_broadcast(P)).then_inc(ld_bo, 16)
            sp.wait_ge(w_lo, 1)
            for k, w in ((0, wk), (1, wv)):
                sp.dma_start(raw[:, k, 0:INNER], w[0:P, :]).then_inc(ld_w2, 16)
                for half in range(2):
                    sp.dma_start(raw[64 * half:64 * half + 64, k, INNER:], w[P:C, :]).then_inc(ld_w2, 16)
            with sp.Fori(1, B) as b:
                hold(sp, xt_lo, b)
                sp.dma_start(xt_raw[:, :, :], xt[bass.ds(b, 1)].rearrange("o (c p) t -> p (o c) t", p=P)).then_inc(ld_xt, 16)
            def context_in(b, k):
                if not (isinstance(b, int) and b == 0):
                    hold(sp, c_lo, 8 * b + 2 * k)
                n = BEDGE[k + 1] - BEDGE[k]
                cols = slice(BEDGE[k], BEDGE[k + 1])
                cb = ctxt[bass.ds(b, 1)].rearrange("o c l -> (o c) l")
                sp.dma_start(raw_context(b, k)[:, 0, :], cb[0:P, cols]).then_inc(ld_c, 16)
                for half in range(2):
                    sp.dma_start(raw_context(b, k)[64 * half:64 * half + 64, 1, :], cb[P:C, cols]).then_inc(ld_c, 16)

            sp.wait_ge(w_lo, 5)
            for k in range(NB):
                context_in(0, k)

            def head_in(b, h):
                s, half = h % 3, slice(64 * (h % 2), 64 * (h % 2) + 64)
                hold(sp, misc_ok, misc(b, ("q", h // 2)) + 1)
                hold(sp, misc_ok, misc(b, ("k", h // 2, NB - 1)) + 1)
                if started(b, h, 3):
                    hb, hh = (b, h - 3) if h >= 3 else (b - 1, {0: 6, 1: 7, 2: 5}[h])
                    hold(sp, st_mm, NL * XH * hb + NL * (hh + 1))
                for dst, src in ((KA[0:64, s, :], Kh), (KA[64:P, s, :], Kh), (QA[0:64, s, :], Qh), (QA[64:P, s, :], Ql)):
                    sp.dma_start(as32(dst), as32(src[half, :])).then_inc(ld_a[s], 16)
                for dst, src in ((KB[0:64, s, :], Kl), (QB[0:64, s, :], Qh)):
                    sp.dma_start(as32(dst), as32(src[half, :])).then_inc(ld_h[s], 16)

            def maxima_in(b, h):
                hold(sp, misc_ok, misc(b, ("mrow", h)) + 1)
                for i in range(NT):
                    sp.dma_start(as32(QB[64:65, h % 3, P * i:P * i + P]), as32(mrow[i:i + 1, h % 2, :])).then_inc(ld_m, 16)

            def cross_attention(b, more):
                head_in(b, 1)
                for h in range(0, XH, 2):
                    if h + 2 < XH:
                        head_in(b, h + 2)
                    maxima_in(b, h + 1)
                    if h + 3 < XH:
                        head_in(b, h + 3)
                        if h + 4 == XH and more:
                            for k in range(NB):
                                context_in(b + 1, k)
                        maxima_in(b, h + 2)
                if more:
                    head_in(b + 1, 0)
                    maxima_in(b + 1, 0)

            head_in(0, 0)
            sp.wait_ge(xconst, 4)
            maxima_in(0, 0)
            cross_attention(0, True)
            with sp.Fori(1, B - 1) as b:
                cross_attention(b, True)
            cross_attention(B - 1, False)
            sp.wait_ge(x2_ok, NT * B + 1)
            sp.wait_ge(gz_ok, 1)
            sp.dma_start(G_raw[:, :, 0:E], gate.rearrange("(c p) e -> p c e", p=P)).then_inc(ld_g, 16)

            def load_expert(e):
                for k, w in enumerate((w1, w3, w2)):
                    src = w[bass.ds(e, 1)].rearrange("o (c p) n -> p (o c) n", p=P)
                    sp.dma_start(W_raw[:, k, :].rearrange("p (c n) -> p c n", c=src.shape[1]), src).then_inc(ld_e, 16)

            load_expert(0)
            with sp.Fori(1, E) as e:
                hold(sp, we_lo, 3 * e)
                load_expert(e)
            for tb in range(B):
                sp.wait_ge(x3_ok, NT * (tb + 1))
                sp.dma_start(out[tb].rearrange("(i p) d -> p i d", p=P), X[:, NT * tb:NT * tb + NT, :]).then_inc(st_out, 16)
            sp.wait_ge(st_out, 16 * B)

        N_LDW = 4

        @block.gpsimd
        def _(pool):
            pool.memset(ident[:, :], 0.0).then_inc(const_pool, 1)
            pool.memset(neg_half[:, :], -0.5).then_inc(const_pool, 1)
            pool.wait_ge(const_pool, 2)
            pool.affine_select(out=ident[:, :], in_=ident[:, :], compare_op=ALU.not_equal, fill=1.0,
                               base=0, pattern=[[-1, P]], channel_multiplier=1).then_inc(const_pool, 1)
            pool.wait_ge(ld_w, 16 * N_LDW)

            def step(b, s):
                if s[0] == "rsqrt":
                    pool.wait_ge(lnv_ok, b + 1)
                    pool.tensor_tensor(ln_rs[:, :], ln_ve[:, :], neg_half[:, 0:NT], ALU.pow).then_inc(lnr_ok, 1)

            def attention(b, first, more):
                for n in range(SLOTS):
                    for j in range(4):
                        u, c = 4 * n + j, n % NT
                        hold(pool, sqr_ok, 64 * b + u + 1)
                        blk = A[:, u % 8, P * c:P * c + P]
                        pool.affine_select(out=blk, in_=blk, compare_op=ALU.is_ge, fill=0.0, base=0,
                                           pattern=[[1, P]], channel_multiplier=-1).then_inc(mask_ok, 1)
                    for d, s in alongside(n, first, more):
                        step(b + d, s)

            for s in OPENING:
                step(0, s)
            attention(0, True, True)
            with pool.Fori(1, B - 1) as b:
                attention(b, False, True)
            attention(B - 1, False, False)
            for s in CLOSING:
                step(B - 1, s)
            pool.wait_ge(x1_ok, NT * B)
            pool.wait_ge(w_lo, 5)
            pool.memset(as32(KB[64:P, :, :]), 0.0).then_inc(xconst, 1)
            pool.wait_ge(xconst, 1)
            pool.memset(as32(QB[64:P, :, :]), 0.0).then_inc(xconst, 1)
            pool.wait_ge(xconst, 2)
            pool.memset(VX[:, :, :, XD:2 * XD], 1.0).then_inc(xconst, 1)
            pool.wait_ge(xconst, 3)
            pool.memset(as32(KB[64:65, :, :]), 1.0).then_inc(xconst, 1)
            with pool.Fori(0, B) as b:
                pool.wait_ge(xlnv_ok, b + 1)
                pool.tensor_tensor(ln_rs[:, :], ln_ve[:, :], neg_half[:, 0:NT], ALU.pow).then_inc(xlnr_ok, 1)
            pool.wait_ge(x2_ok, NT * B + 1)
            pool.memset(lower[:, :, :], 1.0).then_inc(low_ok, 1)
            pool.wait_ge(low_ok, 1)
            pool.affine_select(out=lower[:, :, :], in_=lower[:, :, :], compare_op=ALU.is_gt, fill=0.0, base=0,
                               pattern=[[1, E], [-1, E]], channel_multiplier=0).then_inc(low_ok, 1)

            def split_expert(e, k):
                for m in range(3):
                    pool.wait_ge(we_hi, 3 * e + m + 1)
                    pool.tensor_tensor(W_l[:, k, m, :], W_raw[:, m, :], as32(W_h[:, k, m, :]), ALU.subtract)\
                        .then_inc(we_lo, 1)

            with pool.Fori(0, E // 2) as ee:
                split_expert(2 * ee, 0)
                split_expert(2 * ee + 1, 1)
            for tb in range(B):
                pool.wait_ge(flnv_ok, tb + 1)
                pool.tensor_tensor(ln_rs[:, :], ln_ve[:, :], neg_half[:, 0:NT], ALU.pow).then_inc(flnr_ok, 1)

        @block.scalar
        def _(act):
            act.wait_ge(ld_w, 16 * N_LDW)
            act.copy(WSh[:, :, :], raw[:, 0:2, :]).then_inc(w_hi, 1)

            def x_high(t):
                act.wait_ge(ld_xt, 16 * t + 16)
                act.copy(xt_h[:, :, :], xt_raw[:, :, :]).then_inc(xt_hi, 1)

            def squares(t, i, wait):
                act.wait_ge(v_mm, NT * t + i + 1)
                if wait:
                    act.wait_ge(vs_ok, QUADS * t)
                    act.wait_ge(lo_ok, 8 * t)
                act.copy(Vn[:, i, :], bank(3, D)).then_inc(v_out, 1)
                act.wait_ge(cen_ok, NT * t + i + 1)
                act.activation(feat[:, i, :], cen[:, i % 2, :], ACT.Square).then_inc(sq_ok, 1)

            def deviation(t, i):
                act.wait_ge(var_ok, NT * t + i + 1)
                act.activation(g_sd[:, i % 2, :], g_var[:, i % 2, :], ACT.Sqrt).then_inc(sd_ok, 1)

            def high(t, i):
                if started(t, 0, 1):
                    act.wait_ge(tk_mm, 8 * t)
                act.wait_ge(feat_ok, NT * t + i + 1)
                f = feat[:, i, :].rearrange("p (s h f) -> p s h f", s=2, f=SF)
                act.copy(QX[:, i, :, 0:2, :], f[:, 0].unsqueeze(2).broadcast_to([P, SH, 2, SF])).then_inc(hi_ok, 1)
                act.copy(KX[:, i, :, 0:4:2, :], f[:, 1].unsqueeze(2).broadcast_to([P, SH, 2, SF])).then_inc(hi_ok, 1)

            def values_in(t, g):
                act.wait_ge(v_out, NT * t + NT)
                if started(t, 0, 1):
                    act.wait_ge(av_mm, 16 * t - 16 + 4 * g + 4)
                act.copy(VS[:, :, 4 * g:4 * g + 4, 0:SF],
                         Vn[:, :, 4 * SF * g:4 * SF * (g + 1)].rearrange("p i (h f) -> p i h f", f=SF)).then_inc(vs_ok, 1)

            def turn(b, g, q):
                act.wait_ge(tq_mm, 8 * b + 2 * g + q + 1)
                act.copy(qT[:, g % 2, q, :], bank(0)).then_inc(qT_ok, 1)

            def cross_weight_high(n):
                dst = (WKh, WVh, WQh, WOh)[n]
                act.wait_ge(ld_w2, 16 * 8)
                act.copy(dst[:, :, :], raw[:, n, :].rearrange("p (c n) -> p c n", c=dst.shape[1])).then_inc(w_hi, 1)

            def step(b, s):
                kind, i = s[0], s[-1]
                if kind == "x":
                    x_high(b)
                if kind == "centre":
                    squares(b, i, started(b, 0, 1))
                if kind == "normalise":
                    deviation(b, i)
                if kind == "split":
                    high(b, i)
                if kind == "vs":
                    values_in(b, i)
                if kind == "turn q":
                    turn(b, s[1], s[2])
                if kind == "yt":
                    act.wait_ge(yt_mm, KC * b + i + 1)
                    act.copy(y_h[:, i, :], bank(7)).then_inc(yh_ok, 1)
                if kind == "weights":
                    cross_weight_high(i)

            def squared_scores(b, n):
                for j in range(4):
                    u, c = 4 * n + j, n % NT
                    act.wait_ge(sc_mm, 64 * b + u + 1)
                    if started(b, u, 8):
                        act.wait_ge(av_mm, 16 * b + (u - 8) // 4 + 1)
                    act.activation(A[:, u % 8, P * c:T], PS[:, 4 + u % 2, P * c:T], ACT.Square,
                                   scale=0.25).then_inc(sqr_ok, 1)

            def attention(b, first, more):
                for n in range(SLOTS):
                    if n + 1 < SLOTS:
                        squared_scores(b, n + 1)
                    elif more:
                        squared_scores(b + 1, 0)
                    for d, s in others_first(alongside(n, first, more)):
                        step(b + d, s)

            for s in OPENING:
                step(0, s)
            squared_scores(0, 0)
            attention(0, True, True)
            with act.Fori(1, B - 1) as b:
                attention(b, False, True)
            attention(B - 1, False, False)
            for s in CLOSING:
                step(B - 1, s)
            def context_high(b, k):
                n, lo, hi = BEDGE[k + 1] - BEDGE[k], BEDGE[k], BEDGE[k + 1]
                act.wait_ge(ld_c, 48 * NB * b + 48 * (k + 1) if started(b, 0, 1) else 48 * NB)
                if started(b, k, 1):
                    act.wait_ge(c_lo, 8 * b + 2 * k)
                if k == 0 and started(b, 0, 1):
                    act.wait_ge(misc_mm, misc(b - 1, ("k", PAIRS - 1, NB - 1)) + 1)
                act.copy(Ch[:, lo:hi], raw_context(b, k)[:, 0, :]).then_inc(c_hi, 1)
                act.copy(Cc[0:64, lo:hi], raw_context(b, k)[0:64, 1, :]).then_inc(c_hi, 1)
                act.copy(c_tmp[64:P, 0:n], raw_context(b, k)[64:P, 1, :]).then_inc(c_hi, 1)

            def split_out(b, p):
                act.wait_ge(head_ok, HQ * (XH * b + 2 * p + 2))
                if started(b, p, 1):
                    pb, pp = before(b, p, 1, PAIRS)
                    act.wait_ge(misc_mm, misc(pb, ("wo", pp, NT - 1)) + 1)
                act.copy(O_h, O[:, :]).then_inc(oh_ok, 1)

            def step(b, s):
                kind = s[0]
                if kind == "ctx":
                    context_high(b, s[1])
                if kind == "osplit":
                    split_out(b, s[1])
                if kind not in ("xt", "q", "k"):
                    return
                bk = bank(spare(b, s))
                act.wait_ge(misc_mm, misc(b, s) + 1)
                if kind != "xt" and started(b, s[1], 1):
                    pb, pp = before(b, s[1], 1, PAIRS)
                    for hh in (2 * pp, 2 * pp + 1):
                        act.wait_ge(ld_a[hh % 3], loaded(pb, hh, 4))
                        act.wait_ge(ld_h[hh % 3], loaded(pb, hh, 2))
                if kind == "xt":
                    ins = act.copy(x1_h[:, s[1], :], bk)
                if kind == "q":
                    ins = act.copy(Qh[:, :], bk)
                if kind == "k":
                    lo, hi = BEDGE[s[2]], BEDGE[s[2] + 1]
                    ins = act.copy(Kh[:, lo:hi], bk[:, lo - BSTART[s[2]]:hi - BSTART[s[2]]])
                ins.then_inc(misc_hi, 1)

            def cross_attention(b, first, more):
                for h in range(XH):
                    for j in range(NL):
                        u = NL * h + j
                        act.wait_ge(st_mm, NL * XH * b + u + 1)
                        if started(b, u, NP):
                            act.wait_ge(pv_mm, NL * XH * b + u - NP + 1)
                        r = LROWS[j]
                        act.activation(PX[0:r, u % NP, :], bank(u % 2, rows=r), ACT.Exp, scale=XD ** -0.5)\
                            .then_inc(exp_ok, 1)
                        for d, s in beside(h, j, first, more):
                            step(b + d, s)

            act.wait_ge(x1_ok, NT * B)
            for s in PROLOGUE:
                step(0, s)
            cross_attention(0, True, True)
            with act.Fori(1, B - 1) as b:
                cross_attention(b, False, True)
            cross_attention(B - 1, False, False)
            for s in EPILOGUE:
                step(B - 1, s)

            act.wait_ge(ld_g, 16)
            act.copy(G_h[:, :, :], G_raw[:, :, :]).then_inc(gate_hi, 1)

            def split_expert(e, k, again):
                if again:
                    act.wait_ge(dn_mm, 4 * B * (e - 1))
                for m in range(3):
                    act.wait_ge(ld_e, 48 * e + 48)
                    act.copy(W_h[:, k, m, :], W_raw[:, m, :]).then_inc(we_hi, 1)

            split_expert(0, 0, False)
            for n in range(B * KC):
                act.wait_ge(ft_mm, n + 1)
                act.copy(x2_h[:, n % KC, T * (n // KC):T * (n // KC + 1)], bank(n % 2)).then_inc(ft_hi, 1)
            for tb in range(B):
                act.wait_ge(gs_mm, tb + 1)
                act.copy(sT[:, T * tb:T * tb + T], bank(2 + tb % 2, rows=E)).then_inc(gs_ok, 1)
            act.wait_ge(rt_sh, 1)
            act.activation(ex[:, :, :], sh[:, :, :], ACT.Exp).then_inc(rt_ex, 1)

            def hidden(u, n):
                act.wait_ge(h1_mm, u + 1)
                if n >= 2:
                    act.wait_ge(hm_ok, u - 1)
                act.activation(gl[:, n % 2, :], bank(n % 2), ACT.Silu).then_inc(silu_ok, 1)

            def hidden_hi(u, n, g, later):
                act.wait_ge(hm_ok, u + 1)
                if later:
                    act.wait_ge(dn_mm, 4 * (g - 1))
                act.copy(h_h[:, (n // FC) % 2, n % FC, :], hm[:, n % 2, :]).then_inc(hh_ok, 1)

            def two_experts(ee, first, last):
                for n in range(2 * UNITS):
                    u, g = 2 * UNITS * ee + n, 2 * B * ee + n // FC
                    hidden(u, n)
                    if n >= 1:
                        hidden_hi(u - 1, n - 1, 2 * B * ee + (n - 1) // FC, not first or (n - 1) // FC >= 2)
                    if n == 2 * FC:
                        split_expert(2 * ee + 1, 1, not first)
                    if n == UNITS + 2 * FC and not last:
                        split_expert(2 * ee + 2, 0, True)
                n = 2 * UNITS - 1
                hidden_hi(2 * UNITS * ee + n, n, 2 * B * ee + n // FC, True)

            two_experts(0, True, False)
            with act.Fori(1, E // 2 - 1) as ee:
                two_experts(ee, False, False)
            two_experts(E // 2 - 1, False, True)

        @block.vector
        def _(dve):
            dve.memset(VS[:, :, :, SF:], 1.0).then_inc(const_dve, 1)
            dve.memset(as32(kT[64:P, :, 0:4:2, :]), 0.0).then_inc(const_dve, 1)
            dve.memset(as32(kT[0:64, :, 1:4:2, :]), 0.0).then_inc(const_dve, 1)
            dve.wait_ge(ld_w, 16 * N_LDW)
            dve.wait_ge(w_hi, 1)
            dve.tensor_tensor(WSl[:, :, :], raw[:, 0:2, :], as32(WSh[:, :, :]), ALU.subtract).then_inc(w_lo, 1)

            def x_low(t):
                dve.wait_ge(xt_hi, t + 1)
                dve.tensor_tensor(xt_l[:, :, :], xt_raw[:, :, :], as32(xt_h[:, :, :]), ALU.subtract).then_inc(xt_lo, 1)

            def chain(ins, s, value):
                ins.then_inc(s, 1)
                dve.wait_ge(s, value)

            def centre(t, i, wait):
                at = 2 * (NT * t + i)
                v = bank(2).rearrange("p (g f) -> p g f", f=SF)
                dve.wait_ge(qk_mm, NT * t + i + 1)
                chain(dve.tensor_reduce(g_mean[:, i % 2, :], v, AX, ALU.add), cch, at + 1)
                chain(dve.tensor_scalar(g_mean[:, i % 2, :], g_mean[:, i % 2, :], -1.0 / SF, None, ALU.mult), cch, at + 2)
                if wait:
                    dve.wait_ge(feat_ok, NT * t + i - 1)
                dve.tensor_tensor(cen[:, i % 2, :].rearrange("p (g f) -> p g f", f=SF), v,
                                  g_mean[:, i % 2, :].unsqueeze(2).broadcast_to([P, 32, SF]), ALU.add).then_inc(cen_ok, 1)

            def variance(t, i):
                dve.wait_ge(sq_ok, NT * t + i + 1)
                chain(dve.tensor_reduce(g_var[:, i % 2, :], feat[:, i, :].rearrange("p (g f) -> p g f", f=SF), AX, ALU.add),
                      vch, NT * t + i + 1)
                dve.tensor_scalar(g_var[:, i % 2, :], g_var[:, i % 2, :], 1.0 / SF, LN_EPS, ALU.mult, ALU.add)\
                    .then_inc(var_ok, 1)

            def normalise(t, i):
                at = 4 * (NT * t + i)
                rs, tt = g_rs[:, i % 2, :], g_t[:, i % 2, :]
                dve.wait_ge(sd_ok, NT * t + i + 1)
                chain(dve.reciprocal(rs, g_sd[:, i % 2, :]), fch, at + 1)
                chain(dve.tensor_tensor(tt, rs, rs, ALU.mult), fch, at + 2)
                chain(dve.tensor_tensor(tt, tt, g_var[:, i % 2, :], ALU.mult), fch, at + 3)
                chain(dve.tensor_scalar(tt, tt, -0.5, 1.5, ALU.mult, ALU.add), fch, at + 4)
                dve.tensor_tensor(rs, rs, tt, ALU.mult).then_inc(fn_ok, 1)
                dve.wait_ge(fn_ok, NT * t + i + 1)
                v = cen[:, i % 2, :].rearrange("p (g f) -> p g f", f=SF)
                dve.tensor_tensor(v, v, rs.unsqueeze(2).broadcast_to([P, 32, SF]), ALU.mult).then_inc(nrm_ok, 1)

            def affine(t, i):
                dve.wait_ge(nrm_ok, NT * t + i + 1)
                v = cen[:, i % 2, :].rearrange("p (g f) -> p g f", f=SF)
                w = feat[:, i, :].rearrange("p (g f) -> p g f", f=SF)
                dve.tensor_tensor(v, v, gam[:, :].unsqueeze(1).broadcast_to([P, 32, SF]), ALU.mult).then_inc(gm_ok, 1)
                dve.wait_ge(gm_ok, NT * t + i + 1)
                dve.tensor_tensor(w, v, bet[:, :].unsqueeze(1).broadcast_to([P, 32, SF]), ALU.add)\
                    .then_inc(feat_ok, 1)

            def low(t, i):
                f = feat[:, i, :].rearrange("p (s h f) -> p s h f", s=2, f=SF)
                dve.wait_ge(hi_ok, 8 * t + 2 * i + 1)
                dve.tensor_tensor(QX[:, i, :, 2:4, :], f[:, 0].unsqueeze(2).broadcast_to([P, SH, 2, SF]),
                                  as32(QX[:, i, :, 0:2, :]), ALU.subtract).then_inc(lo_ok, 1)
                dve.wait_ge(hi_ok, 8 * t + 2 * i + 2)
                dve.tensor_tensor(KX[:, i, :, 1:4:2, :], f[:, 1].unsqueeze(2).broadcast_to([P, SH, 2, SF]),
                                  as32(KX[:, i, :, 0:4:2, :]), ALU.subtract).then_inc(lo_ok, 1)

            def turn(b, g, q):
                dve.wait_ge(tk_mm, 8 * b + 2 * g + q + 1)
                dve.tensor_copy(kT[0:64, g % 2, 2 * q, :], bank(1, rows=64)).then_inc(kT_ok, 1)
                dve.tensor_copy(kT[64:P, g % 2, 2 * q + 1, :], PS[64:P, 1, :]).then_inc(kT_ok, 1)

            def quad_out(b, g):
                dve.wait_ge(av_mm, 16 * b + 4 * g + 4)
                if started(b, g, 2):
                    dve.wait_ge(ot_mm, QUADS * b + g - 1)
                dve.tensor_copy(osb[:, g % 2, :], bank(6)).then_inc(osb_ok, 1)

            def quad_norm(b, g):
                dve.wait_ge(ot_mm, QUADS * b + g + 1)
                at = 2 * (QUADS * b + g)
                o = bank(7).rearrange("p (i j f) -> p i j f", i=NT, j=4)
                chain(dve.tensor_scalar(den[:, :].rearrange("p (i j) -> p i j", j=4), o[:, :, :, SF], DEN_EPS, None,
                                        ALU.add), nch, at + 1)
                chain(dve.reciprocal(rden[:, :], den[:, :]), nch, at + 2)
                dve.tensor_tensor(y[:, :, 4 * SF * g:4 * SF * g + 4 * SF].rearrange("p i (j f) -> p i j f", f=SF),
                                  o[:, :, :, 0:SF],
                                  rden[:, :].rearrange("p (i j) -> p i j", j=4).unsqueeze(3)
                                  .broadcast_to([P, NT, 4, SF]), ALU.mult).then_inc(y_ok, 1)

            def cross_weight_low(n):
                dst, high = ((WKl, WKh), (WVl, WVh), (WQl, WQh), (WOl, WOh))[n]
                dve.wait_ge(w_hi, n + 2)
                dve.tensor_tensor(dst[:, :, :], raw[:, n, :].rearrange("p (c n) -> p c n", c=dst.shape[1]),
                                  as32(high[:, :, :]), ALU.subtract).then_inc(w_lo, 1)

            def layer_statistics(b):
                for i in range(NT):
                    xi = X[:, bass.ds(NT * b + i, 1), :].rearrange("p o d -> p (o d)")
                    hold(dve, res_ok, 2 * b + i // 2 + 1)
                    ins = dve.bn_stats(ln_st[:, i, :], xi)
                chain(ins, lch, 2 * b + 1)
                dve.nop(nofuse=True)
                for i in range(NT):
                    ins = dve.bn_aggr(ln_mv[:, i, :], ln_st[:, i, :])
                chain(ins, lch, 2 * b + 2)
                dve.tensor_scalar(ln_ve[:, :], ln_mv[:, :, 1], LN_EPS, None, ALU.add).then_inc(lnv_ok, 1)

            def layer_norm(b):
                dve.wait_ge(lnr_ok, b + 1)
                for i in range(NT):
                    xi = X[:, bass.ds(NT * b + i, 1), :].rearrange("p o d -> p (o d)")
                    dve.tensor_scalar(xi, xi, ln_mv[:, i, 0:1], ln_rs[:, i:i + 1], ALU.subtract, ALU.mult)\
                        .then_inc(x1_ok, 1)

            def step(b, s):
                kind, i = s[0], s[-1]
                if kind == "x":
                    x_low(b)
                if kind == "centre":
                    centre(b, i, started(b, i, 2))
                if kind == "variance":
                    variance(b, i)
                if kind == "normalise":
                    normalise(b, i)
                if kind == "affine":
                    affine(b, i)
                if kind == "split":
                    low(b, i)
                if kind == "turn k":
                    turn(b, s[1], s[2])
                if kind == "quad":
                    quad_norm(b, i)
                if kind == "yt":
                    dve.wait_ge(yh_ok, KC * b + i + 1)
                    dve.tensor_tensor(y_l[:, i, :], bank(7), as32(y_h[:, i, :]), ALU.subtract).then_inc(yl_ok, 1)
                if kind == "out":
                    xi = X[:, bass.ds(NT * b + 2 * i, 2), :]
                    dve.wait_ge(o_mm, 2 * b + i + 1)
                    dve.tensor_tensor(xi, bank(7).rearrange("p (two d) -> p two d", two=2), xi, ALU.add).then_inc(res_ok, 1)
                if kind == "stats":
                    layer_statistics(b)
                if kind == "norm":
                    layer_norm(b)
                if kind == "weights":
                    cross_weight_low(i)

            def attention(b, first, more):
                for n in range(SLOTS):
                    steps = alongside(n, first, more)
                    if n % NT == NT - 1:
                        quad_out(b, n // NT)
                    for d, s in steps:
                        if s[0] not in LATE and s[0] != "x":
                            step(b + d, s)
                    for d, s in steps:
                        if s[0] in LATE and s[0] != "x":
                            step(b + d, s)
                    if (1, ("x",)) in steps:
                        step(b + 1, ("x",))

            dve.wait_ge(ld_x, 16)
            for s in OPENING:
                step(0, s)
            attention(0, True, True)
            with dve.Fori(1, B - 1) as b:
                attention(b, False, True)
            attention(B - 1, False, False)
            for s in CLOSING:
                step(B - 1, s)

            dve.wait_ge(x1_ok, NT * B)
            dve.wait_ge(ld_bo, 16)
            dve.tensor_copy(ln_ve[:, :], ln_ve[:, :]).then_inc(x2_ok, 1)

            def context_low(b, k):
                n, lo, hi = BEDGE[k + 1] - BEDGE[k], BEDGE[k], BEDGE[k + 1]
                dve.wait_ge(c_hi, 12 * b + 3 * k + 1)
                dve.tensor_tensor(Cl[:, lo:hi], raw_context(b, k)[:, 0, :], as32(Ch[:, lo:hi]), ALU.subtract)\
                    .then_inc(c_lo, 1)
                dve.wait_ge(c_hi, 12 * b + 3 * k + 3)
                dve.tensor_tensor(Cc[64:P, lo:hi], raw_context(b, k)[64:P, 1, :], as32(c_tmp[64:P, 0:n]), ALU.subtract)\
                    .then_inc(c_lo, 1)

            def x_in(b):
                xb = X[:, bass.ds(NT * b, NT), :]
                if started(b, 0, 1):
                    dve.wait_ge(misc_mm, misc(b - 1, ("wo", 1, NT - 1)) + 1)
                dve.tensor_copy(xs, xb).then_inc(xs_ok, 1)
                dve.wait_ge(xs_ok, b + 1)
                dve.tensor_tensor(xb, xb, bo_t[:, :].unsqueeze(1).broadcast_to([P, NT, D]), ALU.add).then_inc(xb_ok, 1)

            def layer_norm(b):
                for i in range(NT):
                    xi = X[:, bass.ds(NT * b + i, 1), :].rearrange("p o d -> p (o d)")
                    hold(dve, misc_ok, misc(b, ("wo", PAIRS - 1, i)) + 1)
                    ins = dve.bn_stats(ln_st[:, i, :], xi)
                ins.then_inc(xln_ch, 1)
                hold(dve, xln_ch, 2 * b + 1)
                for i in range(NT):
                    ins = dve.bn_aggr(ln_mv[:, i, :], ln_st[:, i, :])
                ins.then_inc(xln_ch, 1)
                dve.wait_ge(xln_ch, 2 * b + 2)
                dve.tensor_scalar(ln_ve[:, :], ln_mv[:, :, 1], LN_EPS, None, ALU.add).then_inc(xlnv_ok, 1)
                dve.wait_ge(xlnr_ok, b + 1)
                for i in range(NT):
                    xi = X[:, bass.ds(NT * b + i, 1), :].rearrange("p o d -> p (o d)")
                    dve.tensor_scalar(xi, xi, ln_mv[:, i, 0:1], ln_rs[:, i:i + 1], ALU.subtract, ALU.mult)\
                        .then_inc(x2_ok, 1)

            def step(b, s):
                kind = s[0]
                if kind == "ctx":
                    context_low(b, s[1])
                    return
                if kind == "xcopy":
                    x_in(b)
                    return
                if kind == "norm":
                    layer_norm(b)
                    return
                if kind == "hout":
                    head_out(b, s[1], s[2])
                    return
                if kind == "max":
                    h, v = s[1], s[2]
                    n = NMX * h + v
                    dve.wait_ge(mx_mm, NMX * XH * b + n + 1)
                    if started(b, h, 2) and v == 0:
                        dve.wait_ge(hmax_ok, XH * b + h - 1)
                    dve.tensor_reduce(mxp[:, h % 2, v // NB, v % NB:v % NB + 1], bank(2 + n % 2, BW), AX, ALU.max)\
                        .then_inc(mx_ok, 1)
                    if v == NMX - 1:
                        dve.wait_ge(mx_ok, NMX * XH * b + n + 1)
                        if started(b, h, 2):
                            hb, hh = before(b, h, 2, XH)
                            dve.wait_ge(misc_mm, misc(hb, ("mrow", hh)) + 1)
                        dve.tensor_reduce(mx[:, h % 2, :], mxp[:, h % 2, :, :], AX, ALU.max).then_inc(hmax_ok, 1)
                    return
                if kind == "osplit":
                    dve.wait_ge(oh_ok, PAIRS * b + s[1] + 1)
                    if started(b, s[1], 1):
                        pb, pp = before(b, s[1], 1, PAIRS)
                        dve.wait_ge(misc_mm, misc(pb, ("wo", pp, NT - 1)) + 1)
                    dve.tensor_tensor(O_l, O[:, :], as32(O_h), ALU.subtract).then_inc(ol_ok, 1)
                    return
                bk = bank(spare(b, s))
                if kind in ("xt", "q", "k"):
                    dve.wait_ge(misc_hi, highs(b, s) + 1)
                else:
                    dve.wait_ge(misc_mm, misc(b, s) + 1)
                if kind == "xt":
                    ins = dve.tensor_tensor(x1_l[:, s[1], :], bk, as32(x1_h[:, s[1], :]), ALU.subtract)
                if kind == "q":
                    ins = dve.tensor_tensor(Ql[:, :], bk, as32(Qh[:, :]), ALU.subtract)
                if kind == "k":
                    lo, hi = BEDGE[s[2]], BEDGE[s[2] + 1]
                    ins = dve.tensor_tensor(Kl[:, lo:hi], bk[:, lo - BSTART[s[2]]:hi - BSTART[s[2]]],
                                            as32(Kh[:, lo:hi]), ALU.subtract)
                if kind == "v":
                    r = LROWS[s[1]]
                    dst = VX[0:r, s[1], :, :].rearrange("p q (three d) -> p q three d", d=XD)[:, :, 0:3:2, :]
                    ins = dve.tensor_copy(dst, bank(spare(b, s), rows=r).rearrange("p (q two d) -> p q two d",
                                                                                       two=2, d=XD))
                if kind == "mrow":
                    h = s[1]
                    if started(b, h, 2):
                        dve.wait_ge(ld_m, 16 * NT * (XH * b + h - 1))
                    ins = dve.tensor_scalar(mrow[:, h % 2, :], bank(spare(b, s), P, NT), -1.0, None, ALU.mult)
                if kind == "wo":
                    xi = X[:, bass.ds(NT * b + s[2], 1), :].rearrange("p o d -> p (o d)")
                    if s[1] >= 1:
                        dve.wait_ge(misc_ok, misc(b, ("wo", s[1] - 1, s[2])) + 1)
                    else:
                        dve.wait_ge(xb_ok, b + 1)
                    ins = dve.tensor_tensor(xi, bank(spare(b, s), D), xi, ALU.add)
                ins.then_inc(misc_ok, 1)

            def head_out(b, h, q):
                bk, p = 4 + h % 2, h // 2
                t = slice(T // HQ * q, T // HQ * (q + 1))
                val = slice(64 * (h % 2), 64 * (h % 2) + 64)
                tot = slice(64 - 64 * (h % 2), 128 - 64 * (h % 2))
                dve.wait_ge(pv_mm, NL * (XH * b + h + 1))
                if started(b, h, 2):
                    dve.wait_ge(head_ok, HQ * (XH * b + h - 1))
                    dve.wait_ge(ol_ok, PAIRS * b + p)
                dve.reciprocal(R[val, t], PS[tot, bk, t]).then_inc(rec_ok, 1)
                dve.wait_ge(rec_ok, HQ * (XH * b + h) + q + 1)
                dve.tensor_tensor(O[val, t], PS[val, bk, t], R[val, t], ALU.mult).then_inc(head_ok, 1)

            def cross_attention(b, first, more):
                for h in range(XH):
                    for j in range(NL):
                        for d, s in beside(h, j, first, more):
                            step(b + d, s)

            for s in PROLOGUE:
                step(0, s)
            cross_attention(0, True, True)
            with dve.Fori(1, B - 1) as b:
                cross_attention(b, False, True)
            cross_attention(B - 1, False, False)
            for s in EPILOGUE:
                step(B - 1, s)

            dve.wait_ge(x2_ok, NT * B + 1)
            dve.memset(G_raw[:, :, :], 0.0).then_inc(gz_ok, 1)
            dve.wait_ge(gate_hi, 1)
            dve.tensor_tensor(G_l[:, :, :], G_raw[:, :, :], as32(G_h[:, :, :]), ALU.subtract).then_inc(gate_lo, 1)
            for n in range(B * KC):
                cols = slice(T * (n // KC), T * (n // KC + 1))
                dve.wait_ge(ft_hi, n + 1)
                dve.tensor_tensor(x2_l[:, n % KC, cols], bank(n % 2), as32(x2_h[:, n % KC, cols]), ALU.subtract)\
                    .then_inc(ft_ok, 1)
            routed = [0]

            def rt(ins):
                routed[0] += 1
                ins.then_inc(route, 1)
                dve.wait_ge(route, routed[0])

            NTT = B * NT
            dve.wait_ge(gt_mm, 1)
            rt(dve.tensor_copy(S8[:, :, :], bank(4, NTT * E).rearrange("p (t e) -> p t e", e=E)))
            rt(dve.tensor_reduce(smax[:, :], S8[:, :, :], AX, ALU.max))
            dve.tensor_tensor(sh[:, :, :], S8[:, :, :], smax[:, :].unsqueeze(2).broadcast_to([P, NTT, E]),
                              ALU.subtract).then_inc(rt_sh, 1)
            own = S8[:, :, :].unsqueeze(3).broadcast_to([P, NTT, E, E])
            other = S8[:, :, :].unsqueeze(2).broadcast_to([P, NTT, E, E])
            rt(dve.tensor_tensor(cmp[:, :, :, :], other, own, ALU.is_gt))
            rt(dve.tensor_tensor(cmp2[:, :, :, :], other, own, ALU.is_equal))
            dve.wait_ge(low_ok, 2)
            flat = "p t e f -> p t (e f)"
            low = lower[:, :, :].rearrange("p e f -> p (e f)").unsqueeze(1).broadcast_to([P, NTT, E * E])
            rt(dve.tensor_tensor(cmp2[:, :, :, :].rearrange(flat), cmp2[:, :, :, :].rearrange(flat), low, ALU.mult))
            rt(dve.tensor_tensor(cmp[:, :, :, :], cmp[:, :, :, :], cmp2[:, :, :, :], ALU.add))
            rt(dve.tensor_reduce(rank[:, :, :], cmp[:, :, :, :], AX, ALU.add))
            rt(dve.tensor_scalar(chosen[:, :, :], rank[:, :, :], 1.5, None, ALU.is_lt))
            dve.wait_ge(rt_ex, 1)
            rt(dve.tensor_tensor(exs[:, :, :], ex[:, :, :], chosen[:, :, :], ALU.mult))
            rt(dve.tensor_reduce(wsum[:, :], exs[:, :, :], AX, ALU.add))
            rt(dve.reciprocal(wrec[:, :], wsum[:, :]))
            rt(dve.tensor_tensor(WG[:, :, :], exs[:, :, :], wrec[:, :].unsqueeze(2).broadcast_to([P, NTT, E]), ALU.mult))

            def hidden(u, n):
                dve.wait_ge(silu_ok, u + 1)
                dve.wait_ge(h3_mm, u + 1)
                if n >= 2:
                    dve.wait_ge(hh_ok, u - 1)
                    dve.wait_ge(hl_ok, u - 1)
                dve.tensor_tensor(hm[:, n % 2, :], bank(2 + n % 2), gl[:, n % 2, :], ALU.mult).then_inc(hm_ok, 1)

            def hidden_lo(u, n):
                dve.wait_ge(hh_ok, u + 1)
                dve.tensor_tensor(h_l[:, (n // FC) % 2, n % FC, :], hm[:, n % 2, :],
                                  as32(h_h[:, (n // FC) % 2, n % FC, :]), ALU.subtract).then_inc(hl_ok, 1)

            def collect(ee, blk):
                k, tb = blk // B, blk % B
                for i in range(NT):
                    t, a = NT * tb + i, NT * (2 * B * ee + blk) + i
                    dve.wait_ge(dn_mm, a + 1)
                    if blk >= B:
                        dve.wait_ge(acc_ok, a + 1 - NT * B)
                    dve.scalar_tensor_tensor(out=X[:, t, :], in0=bank(4 + i % 2, D), scalar=wcol[:, k, t:t + 1],
                                             in1=X[:, t, :], op0=ALU.mult, op1=ALU.add).then_inc(acc_ok, 1)

            def layer_norm_out(tb):
                dve.wait_ge(acc_ok, NT * B * (E - 1) + NT * tb + NT)
                for i in range(NT):
                    ins = dve.bn_stats(ln_st[:, i, :], X[:, NT * tb + i, :])
                ins.then_inc(fln_ch, 1)
                dve.wait_ge(fln_ch, 2 * tb + 1)
                for i in range(NT):
                    ins = dve.bn_aggr(ln_mv[:, i, :], ln_st[:, i, :])
                ins.then_inc(fln_ch, 1)
                dve.wait_ge(fln_ch, 2 * tb + 2)
                dve.tensor_scalar(ln_ve[:, :], ln_mv[:, :, 1], LN_EPS, None, ALU.add).then_inc(flnv_ok, 1)
                dve.wait_ge(flnr_ok, tb + 1)
                for i in range(NT):
                    xi = X[:, NT * tb + i, :]
                    dve.tensor_scalar(xi, xi, ln_mv[:, i, 0:1], ln_rs[:, i:i + 1], ALU.subtract, ALU.mult)\
                        .then_inc(x3_ok, 1)

            def two_experts(ee, first, last):
                if not first:
                    dve.wait_ge(acc_ok, 2 * NT * B * ee)
                dve.tensor_copy(wcol[:, :, :], WG[:, :, bass.ds(2 * ee, 2)].rearrange("p t k -> p k t")).then_inc(wcol_ok, 1)
                dve.wait_ge(wcol_ok, ee + 1)
                for n in range(2 * UNITS):
                    u = 2 * UNITS * ee + n
                    hidden(u, n)
                    if n >= 1:
                        hidden_lo(u - 1, n - 1)
                    if n % FC == FC - 1 and n >= FC:
                        collect(ee, n // FC - 1)
                        if last and n // FC - 1 >= B:
                            layer_norm_out(n // FC - 1 - B)
                hidden_lo(2 * UNITS * (ee + 1) - 1, 2 * UNITS - 1)
                collect(ee, 2 * B - 1)
                if last:
                    layer_norm_out(B - 1)

            two_experts(0, True, False)
            with dve.Fori(1, E // 2 - 1) as ee:
                two_experts(ee, False, False)
            two_experts(E // 2 - 1, False, True)

        @block.tensor
        def _(pe):
            pe.wait_ge(const_pool, 3)
            pe.wait_ge(const_dve, 3)
            pe.wait_ge(w_lo, 1)

            def project_qk(t, i):
                pe.wait_ge(xt_lo, t + 1)
                if started(t, i, 1):
                    pe.wait_ge(cen_ok, NT * t + i)
                rows = slice(P * i, P * i + P)
                for c in range(KC):
                    mm = split3(pe, bank(2), xt_h[:, c, rows], xt_l[:, c, rows], WSh[:, c, 0:2 * D], WSl[:, c, 0:2 * D],
                                c == 0, c == KC - 1)
                mm.then_inc(qk_mm, 1)

            def project_v(t, i):
                if started(t, i, 1):
                    pe.wait_ge(v_out, NT * t + i)
                rows = slice(P * i, P * i + P)
                for c in range(KC):
                    mm = split3(pe, bank(3, D), xt_h[:, c, rows], xt_l[:, c, rows], WSh[:, c, 2 * D:3 * D],
                                WSl[:, c, 2 * D:3 * D], c == 0, c == KC - 1)
                mm.then_inc(v_mm, 1)

            def turn(b, g, q, src, bk, done, free, per):
                h = 4 * g + 2 * q
                if g == 0:
                    pe.wait_ge(lo_ok, 8 * b + 8)
                if started(b, 2 * g + q, 1):
                    pe.wait_ge(free, per * (8 * b + 2 * g + q))
                for i in range(NT):
                    mm = pe.transpose(PS[:, bk, P * i:P * i + P],
                                      as32(src[:, i, h:h + 2, :, :]).rearrange("p h s f -> p (h s f)"), ident[:, :])
                mm.then_inc(done, 1)

            def score(b, n, j):
                g, c, u = n // NT, n % NT, 4 * n + j
                if c == 0 and j == 0:
                    pe.wait_ge(qT_ok, 8 * b + 2 * g + 2)
                    pe.wait_ge(kT_ok, 16 * b + 4 * g + 4)
                if started(b, u, 2):
                    pe.wait_ge(sqr_ok, 64 * b + u - 1)
                pe.matmul(PS[:, 4 + u % 2, P * c:T], kT[:, g % 2, j, P * c:P * c + P],
                          qT[:, g % 2, j // 2, P * c:T], start=True, stop=True).then_inc(sc_mm, 1)

            def value(b, n, j):
                g, c, u = n // NT, n % NT, 4 * n + j
                if c == 0 and j == 0:
                    pe.wait_ge(vs_ok, QUADS * b + g + 1)
                    if started(b, g, 1):
                        pe.wait_ge(osb_ok, QUADS * b + g)
                pe.wait_ge(mask_ok, 64 * b + u + 1)
                mm = pe.matmul(PS[32 * j:32 * j + 32, 6, P * c:T], VS[:, c, 4 * g + j, :], A[:, u % 8, P * c:T],
                               start=(c == 0), stop=(c == NT - 1))
                if j == 3:
                    mm.then_inc(av_mm, 1)

            def back(b, g):
                pe.wait_ge(osb_ok, QUADS * b + g + 1)
                if g >= 1:
                    pe.wait_ge(y_ok, QUADS * b + g)
                elif started(b, 0, 1):
                    pe.wait_ge(res_ok, 2 * b)
                for i in range(NT):
                    mm = pe.transpose(PS[:, 7, P * i:P * i + P], osb[:, g % 2, P * i:P * i + P], ident[:, :])
                mm.then_inc(ot_mm, 1)

            def step(b, s):
                kind, i = s[0], s[-1]
                if kind == "project qk":
                    project_qk(b, i)
                if kind == "project v":
                    project_v(b, i)
                if kind == "turn q":
                    turn(b, s[1], s[2], QX, 0, tq_mm, qT_ok, 1)
                if kind == "turn k":
                    turn(b, s[1], s[2], KX, 1, tk_mm, kT_ok, 2)
                if kind == "back":
                    back(b, i)
                if kind == "yt":
                    pe.wait_ge(y_ok, QUADS * b + QUADS)
                    if i >= 1:
                        pe.wait_ge(yl_ok, KC * b + i)
                    for t in range(NT):
                        mm = pe.transpose(PS[:, 7, P * t:P * t + P], y[:, t, P * i:P * i + P], ident[:, :])
                    mm.then_inc(yt_mm, 1)
                if kind == "out":
                    pe.wait_ge(yl_ok, KC * b + KC)
                    if i >= 1:
                        pe.wait_ge(res_ok, 2 * b + i)
                    for half in range(2):
                        t = slice(P * (2 * i + half), P * (2 * i + half) + P)
                        for c in range(KC):
                            mm = split3(pe, PS[:, 7, D * half:D * half + D], y_h[:, c, t], y_l[:, c, t],
                                        WSh[:, c, 3 * D:], WSl[:, c, 3 * D:], c == 0, c == KC - 1)
                    mm.then_inc(o_mm, 1)

            PE_STEPS = ("project qk", "project v", "turn q", "turn k", "back", "yt", "out")

            def attention(b, first, more):
                for n in range(SLOTS):
                    steps = [(d, s) for d, s in alongside(n, first, more) if s[0] in PE_STEPS]
                    for j in range(4):
                        if n + 1 < SLOTS:
                            score(b, n + 1, j)
                        elif more:
                            score(b + 1, 0, j)
                        value(b, n, j)
                        for d, s in steps[len(steps) * j // 4:len(steps) * (j + 1) // 4]:
                            step(b + d, s)

            for s in OPENING:
                step(0, s)
            for j in range(4):
                score(0, 0, j)
            attention(0, True, True)
            with pe.Fori(1, B - 1) as b:
                attention(b, False, True)
            attention(B - 1, False, False)
            for s in CLOSING:
                step(B - 1, s)
            pe.wait_ge(res_ok, 2 * B)

            def context_product(o, lhs, rhs, first_is_weight):
                ops = []
                for wc, cc in (((0, "h"), Ch), ((0, "h"), Cl), ((0, "l"), Ch), ((1, "h"), Cc), ((1, "l"), Cc)):
                    ops.append((lhs(wc), rhs(cc)) if first_is_weight else (lhs(cc), rhs(wc)))
                for n, (l, r) in enumerate(ops):
                    mm = pe.matmul(o, l, r, start=(n == 0), stop=(n == len(ops) - 1))
                return mm

            def step(b, s):
                kind = s[0]
                if kind in ("osplit", "ctx", "xcopy", "norm", "hout"):
                    return
                if kind == "max":
                    h, v = s[1], s[2]
                    n, i, k = NMX * h + v, v // NB, v % NB
                    if v == 0:
                        pe.wait_ge(ld_a[h % 3], loaded(b, h, 4))
                    if started(b, n, 2):
                        pe.wait_ge(mx_ok, NMX * XH * b + n - 1)
                    pe.matmul(bank(2 + n % 2, BW), QA[:, h % 3, P * i:P * i + P], KA[:, h % 3, BSTART[k]:BSTART[k] + BW],
                              start=True, stop=True).then_inc(mx_mm, 1)
                    return
                if freed(b, s) is not None:
                    pe.wait_ge(misc_ok, freed(b, s))
                bk = bank(spare(b, s))
                if kind == "xt":
                    pe.wait_ge(xs_ok, b + 1)
                    for i in range(NT):
                        mm = pe.transpose(bk[:, P * i:P * i + P], xs[:, i, P * s[1]:P * s[1] + P], ident[:, :])
                if kind == "q":
                    pe.wait_ge(misc_ok, misc(b, ("xt", KC - 1)) + 1)
                    w = slice(P * s[1], P * s[1] + P)
                    for c in range(KC):
                        mm = split3(pe, bk, WQh[:, c, w], WQl[:, c, w], x1_h[:, c, :], x1_l[:, c, :],
                                    c == 0, c == KC - 1)
                if kind == "k":
                    pe.wait_ge(c_lo, 8 * b + 2 * s[2] + 2)
                    w = slice(P * s[1], P * s[1] + P)
                    cols = slice(BSTART[s[2]], BSTART[s[2]] + BW)
                    mm = context_product(bk[:, 0:BW], lambda wc: (WKh if wc[1] == "h" else WKl)[:, wc[0], w],
                                         lambda cc: cc[:, cols], True)
                if kind == "v":
                    r = LROWS[s[1]]
                    cols = slice(P * s[1], P * s[1] + r)
                    mm = context_product(bk[0:r, :], lambda cc: cc[:, cols],
                                         lambda wc: (WVh if wc[1] == "h" else WVl)[:, wc[0], :], False)
                if kind == "mrow":
                    pe.wait_ge(hmax_ok, XH * b + s[1] + 1)
                    mm = pe.transpose(PS[0:NT, spare(b, s), 0:P], mx[:, s[1] % 2, :], ident[:, :])
                if kind == "wo":
                    pe.wait_ge(ol_ok, PAIRS * b + s[1] + 1)
                    t = slice(P * s[2], P * s[2] + P)
                    mm = split3(pe, bk[:, 0:D], OHL[:, 0, t], OHL[:, 1, t], WOh[:, s[1], :], WOl[:, s[1], :], True, True)
                mm.then_inc(misc_mm, 1)

            def scores_t(b, h, j):
                u = NL * h + j
                if j == 0:
                    pe.wait_ge(ld_h[h % 3], loaded(b, h, 2))
                    pe.wait_ge(ld_m, 16 * NT * (XH * b + h + 1))
                if started(b, u, 2):
                    pe.wait_ge(exp_ok, NL * XH * b + u - 1)
                keys = slice(P * j, P * j + LROWS[j])
                o = bank(u % 2, rows=LROWS[j])
                pe.matmul(o, KA[:, h % 3, keys], QA[:, h % 3, :], start=True, stop=False)
                pe.matmul(o, KB[:, h % 3, keys], QB[:, h % 3, :], start=False, stop=True).then_inc(st_mm, 1)

            pe.wait_ge(w_lo, 5)

            def cross_attention(b, first, more):
                for h in range(XH):
                    for j in range(NL):
                        u = NL * h + j
                        if u + 1 < NL * XH:
                            scores_t(b, (u + 1) // NL, (u + 1) % NL)
                        elif more:
                            scores_t(b + 1, 0, 0)
                        for d, s in beside(h, j, first, more):
                            step(b + d, s)
                        if h == 0:
                            pe.wait_ge(misc_ok, misc(b, ("v", j)) + 1)
                        pe.wait_ge(exp_ok, NL * XH * b + u + 1)
                        if j == 0 and started(b, h, 2):
                            pe.wait_ge(head_ok, HQ * (XH * b + h - 1))
                        pe.matmul(bank(4 + h % 2), v_ones(j, h), PX[0:LROWS[j], u % NP, :], start=(j == 0),
                                  stop=(j == NL - 1)).then_inc(pv_mm, 1)

            for s in PROLOGUE:
                step(0, s)
            pe.wait_ge(xconst, 4)
            scores_t(0, 0, 0)
            cross_attention(0, True, True)
            with pe.Fori(1, B - 1) as b:
                cross_attention(b, False, True)
            cross_attention(B - 1, False, False)
            for s in EPILOGUE:
                step(B - 1, s)

            pe.wait_ge(x2_ok, NT * B + 1)
            for n in range(B * KC):
                if n >= 2:
                    pe.wait_ge(ft_ok, n - 1)
                for i in range(NT):
                    mm = pe.transpose(PS[:, n % 2, P * i:P * i + P],
                                      X[:, NT * (n // KC) + i, P * (n % KC):P * (n % KC) + P], ident[:, :])
                mm.then_inc(ft_mm, 1)
            pe.wait_ge(gate_lo, 1)
            for tb in range(B):
                cols = slice(T * tb, T * tb + T)
                pe.wait_ge(ft_ok, KC * (tb + 1))
                if tb >= 2:
                    pe.wait_ge(gs_ok, tb - 1)
                for c in range(KC):
                    mm = split3(pe, bank(2 + tb % 2, rows=E), G_h[:, c, 0:E], G_l[:, c, 0:E], x2_h[:, c, cols], x2_l[:, c, cols],
                                c == 0, c == KC - 1)
                mm.then_inc(gs_mm, 1)
            pe.wait_ge(gs_ok, B)
            for t in range(B * NT):
                mm = pe.transpose(PS[:, 4, E * t:E * t + E], sT[:, P * t:P * t + P], ident[0:E, 0:E])
            mm.then_inc(gt_mm, 1)
            pe.wait_ge(route, 1)

            def up(ee, n):
                u, k, tb, f = 2 * UNITS * ee + n, n // UNITS, (n // FC) % B, n % FC
                cols = slice(T * tb, T * tb + T)
                for m, done, free in ((0, h1_mm, silu_ok), (1, h3_mm, hm_ok)):
                    if n >= 2:
                        pe.wait_ge(free, u - 1)
                    for c in range(KC):
                        w = slice(FF * c + P * f, FF * c + P * f + P)
                        mm = split3(pe, bank(2 * m + n % 2), W_h[:, k, m, w], W_l[:, k, m, w], x2_h[:, c, cols],
                                    x2_l[:, c, cols], c == 0, c == KC - 1)
                    mm.then_inc(done, 1)

            def down(ee, blk):
                k = blk // B
                pe.wait_ge(hl_ok, FC * (2 * B * ee + blk + 1))
                for i in range(NT):
                    a, t = NT * (2 * B * ee + blk) + i, slice(P * i, P * i + P)
                    if NT * blk + i >= 2:
                        pe.wait_ge(acc_ok, a - 1)
                    for f in range(FC):
                        w = slice(D * f, D * f + D)
                        mm = split3(pe, bank(4 + i % 2, D), h_h[:, blk % 2, f, t], h_l[:, blk % 2, f, t], W_h[:, k, 2, w],
                                    W_l[:, k, 2, w], f == 0, f == FC - 1)
                    mm.then_inc(dn_mm, 1)

            def two_experts(ee, first):
                for n in range(2 * UNITS):
                    if n % UNITS == 0:
                        pe.wait_ge(we_lo, 3 * (2 * ee + n // UNITS) + 3)
                    up(ee, n)
                    if n % FC == FC - 1 and n >= FC:
                        down(ee, n // FC - 1)
                down(ee, 2 * B - 1)

            two_experts(0, True)
            with pe.Fori(1, E // 2 - 1) as ee:
                two_experts(ee, False)
            two_experts(E // 2 - 1, False)


def kernel(**inputs):
    import numpy as _np
    import concourse.bacc as _bacc
    from concourse import mybir as _mybir
    from concourse.bass_utils import run_bass_kernel_spmd as _run

    a = {k: _np.asarray(v) for k, v in inputs.items()}
    lay = {
        "x": a["x"],
        "xt": a["x"].transpose(0, 2, 1),
        "ctxt": a["ctx_768"].transpose(0, 2, 1),
        "wqkv": _np.concatenate([a["L0_attn_Wq"], a["L0_attn_Wk"], a["L0_attn_Wv"]]).T,
        "wo_s": a["L0_attn_Wo"].T,
        "gamma": a["L0_attn_gamma"],
        "beta": a["L0_attn_beta"],
        "wq": a["L0_xattn_Wq"],
        "wk": a["L0_xattn_Wk"],
        "wv": a["L0_xattn_Wv"],
        "wo_x": a["L0_xattn_Wo"],
        "bo": a["L0_xattn_bo"],
        "gate": a["L0_ffn_gate_w"].T,
        "w1": a["L0_ffn_w1"].transpose(0, 2, 1),
        "w3": a["L0_ffn_w3"].transpose(0, 2, 1),
        "w2": a["L0_ffn_w2"].transpose(0, 2, 1),
    }
    nc = _bacc.Bacc("TRN2", target_bir_lowering=False, num_devices=1)
    arrays, args = {}, []
    for name, v in lay.items():
        v = _np.ascontiguousarray(v)
        arrays[f"in_{name}"] = v
        args.append(nc.dram_tensor(f"in_{name}", v.shape, _mybir.dt.from_np(v.dtype), kind="ExternalInput").ap())
    o = nc.dram_tensor("out_0", (B, T, D), _mybir.dt.float32, kind="ExternalOutput").ap()
    decoder_layer(nc, *args, o)
    r = _run(nc, [arrays], core_ids=[0])
    return r.results[0]["out_0"]
```
